# Optimizing a Trainium2 kernel written in Bass

```python
import numpy as np
import jax
import jax.numpy as jnp

def _softmax(x, axis=-1):
    return jax.nn.softmax(x, axis=axis)

def _gelu(x):
    return jax.nn.gelu(x, approximate=True)

def _silu(x):
    return jax.nn.silu(x)

def _sigmoid(x):
    return jax.nn.sigmoid(x)

def _layernorm(x, axis=-1, eps=1e-05):
    m = jnp.mean(x, axis=axis, keepdims=True)
    v = jnp.var(x, axis=axis, keepdims=True)
    return (x - m) / jnp.sqrt(v + eps)

def _scatter_add(tgt, idx, src, axis=0):
    return tgt.at[idx].add(src)

def _segment_sum(src, seg, n):
    return jax.ops.segment_sum(src, seg, n)
kernel_name = 'mk_gnn_resnorm_d4_gnn_r32_880740'

def setup_inputs(seed: int=0):
    np.random.seed(seed)
    _w = jnp.asarray

    def _rec_inputs():
        import jax
        import jax.numpy as jnp
        _gk = jax.random.key(seed)
        x = -0.000202 + 1 * jax.random.normal(jax.random.fold_in(_gk, 1), (3125, 64), jnp.float32)
        _s = jax.random.randint(jax.random.fold_in(_gk, 2), (25000,), 0, 3125, jnp.int32)
        _d = jax.random.randint(jax.random.fold_in(_gk, 3), (25000,), 0, 3125, jnp.int32)
        _loop = jnp.arange(3125, dtype=jnp.int32)
        src = jnp.concatenate([_s, _d, _loop])
        dst = jnp.concatenate([_d, _s, _loop])
        _o = jnp.argsort(dst, stable=True)
        src = src[_o]
        dst = dst[_o]
        edge_attr_3 = 0.000669165 + 0.999965 * jax.random.normal(jax.random.fold_in(_gk, 12), (53125, 3), jnp.float32)
        edge_weight = jax.random.uniform(jax.random.fold_in(_gk, 14), (53125,), jnp.float32, 0.0, 0.999998)
        return (x, src, dst, edge_attr_3, edge_weight)
    x, src, dst, edge_attr_3, edge_weight = _rec_inputs()

    def _L0_gnn_setup():
        import jax, jax.numpy as jnp
        import numpy as np
        K_LAYERS = 10
        ALPHA = 0.1
        N_NODES = 3125
        N_EDGES = 50000
        D_FEAT = 64
        key = jax.random.key(seed)
        k1, k2, k3 = jax.random.split(key, 3)
        features = jax.random.normal(k1, (N_NODES, D_FEAT), dtype=jnp.float32)
        src = jax.random.randint(k2, (N_EDGES,), 0, N_NODES, dtype=jnp.int64)
        dst = jax.random.randint(k3, (N_EDGES,), 0, N_NODES, dtype=jnp.int64)
        return {'features': features, 'src': src, 'dst': dst}
    _L0_gnn_all = _L0_gnn_setup()
    _L0_gnn_in = {k: v for k, v in _L0_gnn_all.items() if k in ()}
    del _L0_gnn_all

    def _L1_gnn_setup():
        import jax, jax.numpy as jnp
        import numpy as np
        N_NODES = 50000
        N_EDGES = 25000
        D_FEAT = 64
        key = jax.random.key(seed)
        k1, k2, k3 = jax.random.split(key, 3)
        x = jax.random.normal(k1, (N_NODES, D_FEAT), dtype=jnp.float32)
        edge_index = jax.random.randint(k2, (2, N_EDGES), 0, N_NODES, dtype=jnp.int64)
        edge_weight = jax.random.uniform(k3, (N_EDGES,), dtype=jnp.float32)
        eps = jnp.zeros((1,), dtype=jnp.float32)
        return {'x': x, 'edge_index': edge_index, 'edge_weight': edge_weight, 'eps': eps}
    _L1_gnn_all = _L1_gnn_setup()
    _L1_gnn_in = {k: v for k, v in _L1_gnn_all.items() if k in ('eps',)}
    del _L1_gnn_all

    def _L2_gnn_setup():
        import jax, jax.numpy as jnp
        import numpy as np
        N, E = (50000, 25000)
        C, ED, L = (64, 3, 3)
        EPS = 1e-05

        def _layer_norm(h, g, b):
            mu = jnp.mean(h, axis=-1, keepdims=True)
            var = jnp.var(h, axis=-1, keepdims=True)
            return (h - mu) * jax.lax.rsqrt(var + EPS) * g + b
        key = jax.random.key(seed)
        ks = jax.random.split(key, 20)
        s = 0.1
        inp = {'x': jax.random.normal(ks[0], (N, C), dtype=jnp.float32), 'edge_index': jax.random.randint(ks[1], (2, E), 0, N, dtype=jnp.int64), 'edge_attr': jax.random.normal(ks[2], (E, ED), dtype=jnp.float32), 'W_node': jax.random.normal(ks[3], (L, C, C), dtype=jnp.float32) * s, 'W_e1': jax.random.normal(ks[4], (L, ED, C), dtype=jnp.float32) * s, 'b_e1': jnp.zeros((L, C), dtype=jnp.float32), 'W_e2': jax.random.normal(ks[5], (L, C, C), dtype=jnp.float32) * s, 'b_e2': jnp.zeros((L, C), dtype=jnp.float32), 'Wa1': jax.random.normal(ks[6], (L, 2 * C + ED, C), dtype=jnp.float32) * s, 'ba1': jnp.zeros((L, C), dtype=jnp.float32), 'Wa2': jax.random.normal(ks[7], (L, C, 1), dtype=jnp.float32) * s, 'ba2': jnp.zeros((L, 1), dtype=jnp.float32), 'bias': jnp.zeros((L, C), dtype=jnp.float32), 'ln_g': jnp.ones((L, C), dtype=jnp.float32), 'ln_b': jnp.zeros((L, C), dtype=jnp.float32)}
        return inp
    _L2_gnn_all = _L2_gnn_setup()
    _L2_gnn_in = {k: v for k, v in _L2_gnn_all.items() if k in ('W_node', 'W_e1', 'b_e1', 'W_e2', 'b_e2', 'Wa1', 'ba1', 'Wa2', 'ba2', 'bias', 'ln_g', 'ln_b')}
    del _L2_gnn_all

    def _L3_gnn_setup():
        import jax, jax.numpy as jnp
        import numpy as np
        N_NODES = 50000
        N_EDGES = 25000
        C_IN = 64
        C_OUT = 64
        K = 3

        def _propagate(x, row, col, edge_weight, n_nodes):
            deg = jax.ops.segment_sum(edge_weight, row, num_segments=n_nodes)
            deg_inv = jnp.where(deg > 0, jax.lax.rsqrt(jnp.where(deg > 0, deg, 1.0)), 0.0)
            norm = deg_inv[row] * edge_weight * deg_inv[col]
            msg = norm[:, None] * x[col]
            return jax.ops.segment_sum(msg, row, num_segments=n_nodes)
        key = jax.random.key(seed)
        k1, k2, k3, k4, k5, k6 = jax.random.split(key, 6)
        x = jax.random.normal(k1, (N_NODES, C_IN), dtype=jnp.float32)
        edge_index = jax.random.randint(k2, (2, N_EDGES), 0, N_NODES, dtype=jnp.int32)
        edge_weight = jax.random.uniform(k3, (N_EDGES,), dtype=jnp.float32)
        limit = float(np.sqrt(6.0 / (C_IN + C_OUT)))
        theta_forward = jax.random.uniform(k4, (K, C_IN, C_OUT), minval=-limit, maxval=limit, dtype=jnp.float32)
        theta_backward = jax.random.uniform(k5, (K, C_IN, C_OUT), minval=-limit, maxval=limit, dtype=jnp.float32)
        return {'x': x, 'edge_index': edge_index, 'edge_weight': edge_weight, 'theta_forward': theta_forward, 'theta_backward': theta_backward}
    _L3_gnn_all = _L3_gnn_setup()
    _L3_gnn_in = {k: v for k, v in _L3_gnn_all.items() if k in ('theta_forward', 'theta_backward')}
    del _L3_gnn_all
    return {'x': x, 'src': src, 'dst': dst, 'edge_attr_3': edge_attr_3, 'edge_weight': edge_weight, 'L1_gnn_eps': _L1_gnn_in['eps'], 'L2_gnn_W_node': _L2_gnn_in['W_node'], 'L2_gnn_W_e1': _L2_gnn_in['W_e1'], 'L2_gnn_b_e1': _L2_gnn_in['b_e1'], 'L2_gnn_W_e2': _L2_gnn_in['W_e2'], 'L2_gnn_b_e2': _L2_gnn_in['b_e2'], 'L2_gnn_Wa1': _L2_gnn_in['Wa1'], 'L2_gnn_ba1': _L2_gnn_in['ba1'], 'L2_gnn_Wa2': _L2_gnn_in['Wa2'], 'L2_gnn_ba2': _L2_gnn_in['ba2'], 'L2_gnn_bias': _L2_gnn_in['bias'], 'L2_gnn_ln_g': _L2_gnn_in['ln_g'], 'L2_gnn_ln_b': _L2_gnn_in['ln_b'], 'L3_gnn_theta_forward': _L3_gnn_in['theta_forward'], 'L3_gnn_theta_backward': _L3_gnn_in['theta_backward']}

def reference(x, src, dst, edge_attr_3, edge_weight, L1_gnn_eps, L2_gnn_W_node, L2_gnn_W_e1, L2_gnn_b_e1, L2_gnn_W_e2, L2_gnn_b_e2, L2_gnn_Wa1, L2_gnn_ba1, L2_gnn_Wa2, L2_gnn_ba2, L2_gnn_bias, L2_gnn_ln_g, L2_gnn_ln_b, L3_gnn_theta_forward, L3_gnn_theta_backward):
    import jax
    import jax.numpy as jnp

    def _L0_gnn_ref(features, src, dst):
        import jax, jax.numpy as jnp
        import numpy as np
        K_LAYERS = 10
        ALPHA = 0.1
        N_NODES = 3125
        N_EDGES = 50000
        D_FEAT = 64
        n = features.shape[0]
        ones = jnp.ones((src.shape[0],), dtype=features.dtype)
        deg_out = jax.ops.segment_sum(ones, src, num_segments=n)
        deg_in = jax.ops.segment_sum(ones, dst, num_segments=n)
        norm_src = jnp.clip(deg_out, 1.0) ** (-0.5)
        norm_dst = jnp.clip(deg_in, 1.0) ** (-0.5)
        h0 = features
        h = features
        for _ in range(K_LAYERS):
            msg = (h * norm_src[:, None])[src]
            agg = jax.ops.segment_sum(msg, dst, num_segments=n)
            h = (1.0 - ALPHA) * (agg * norm_dst[:, None]) + ALPHA * h0
        return h

    def _L1_gnn_ref(x, edge_index, edge_weight, eps):
        import jax, jax.numpy as jnp
        import numpy as np
        N_NODES = 50000
        N_EDGES = 25000
        D_FEAT = 64
        row, col = (edge_index[0], edge_index[1])
        w = jnp.where(row != col, edge_weight, jnp.zeros_like(edge_weight))
        msgs = w[:, None] * x[col]
        agg = jax.ops.segment_sum(msgs, row, num_segments=x.shape[0])
        return (1.0 + eps[0]) * x + agg

    def _L2_gnn_ref(x, edge_index, edge_attr, W_node, W_e1, b_e1, W_e2, b_e2, Wa1, ba1, Wa2, ba2, bias, ln_g, ln_b):
        import jax, jax.numpy as jnp
        import numpy as np
        N, E = (50000, 25000)
        C, ED, L = (64, 3, 3)
        EPS = 1e-05

        def _layer_norm(h, g, b):
            mu = jnp.mean(h, axis=-1, keepdims=True)
            var = jnp.var(h, axis=-1, keepdims=True)
            return (h - mu) * jax.lax.rsqrt(var + EPS) * g + b
        src = edge_index[0]
        dst = edge_index[1]
        n = x.shape[0]
        h = x
        for l in range(W_node.shape[0]):
            h_in = h
            hx = h @ W_node[l]
            ef = jax.nn.relu(edge_attr @ W_e1[l] + b_e1[l]) @ W_e2[l] + b_e2[l]
            xi = hx[dst]
            xj = hx[src]
            att_in = jnp.concatenate([xi, xj, edge_attr], axis=-1)
            a = jax.nn.sigmoid(jax.nn.relu(att_in @ Wa1[l] + ba1[l]) @ Wa2[l] + ba2[l])
            msg = a * (xj + ef)
            out = jax.ops.segment_sum(msg, dst, num_segments=n) + bias[l]
            out = _layer_norm(out, ln_g[l], ln_b[l])
            if l < W_node.shape[0] - 1:
                out = jax.nn.relu(out)
            h = out + h_in
        return h

    def _L3_gnn_ref(x, edge_index, edge_weight, theta_forward, theta_backward):
        import jax, jax.numpy as jnp
        import numpy as np
        N_NODES = 50000
        N_EDGES = 25000
        C_IN = 64
        C_OUT = 64
        K = 3

        def _propagate(x, row, col, edge_weight, n_nodes):
            deg = jax.ops.segment_sum(edge_weight, row, num_segments=n_nodes)
            deg_inv = jnp.where(deg > 0, jax.lax.rsqrt(jnp.where(deg > 0, deg, 1.0)), 0.0)
            norm = deg_inv[row] * edge_weight * deg_inv[col]
            msg = norm[:, None] * x[col]
            return jax.ops.segment_sum(msg, row, num_segments=n_nodes)
        row, col = (edge_index[0], edge_index[1])
        n_nodes = x.shape[0]
        k = theta_forward.shape[0]
        Tx_0 = x
        Tx_1 = _propagate(x, row, col, edge_weight, n_nodes)
        out = Tx_0 @ theta_forward[0] + Tx_1 @ theta_backward[0]
        for i in range(1, k):
            Tx_2 = _propagate(Tx_1, row, col, edge_weight, n_nodes)
            out = out + Tx_2 @ theta_forward[i] + Tx_1 @ theta_backward[i]
            Tx_1 = Tx_2
        return out
    edge_index = jnp.stack([src, dst])
    x = _layernorm(x + _L0_gnn_ref(x, src, dst), axis=-1)
    x = _layernorm(x + _L1_gnn_ref(x, edge_index, edge_weight, L1_gnn_eps), axis=-1)
    x = _layernorm(x + _L2_gnn_ref(x, edge_index, edge_attr_3, L2_gnn_W_node, L2_gnn_W_e1, L2_gnn_b_e1, L2_gnn_W_e2, L2_gnn_b_e2, L2_gnn_Wa1, L2_gnn_ba1, L2_gnn_Wa2, L2_gnn_ba2, L2_gnn_bias, L2_gnn_ln_g, L2_gnn_ln_b), axis=-1)
    x = _layernorm(x + _L3_gnn_ref(x, edge_index, edge_weight, L3_gnn_theta_forward, L3_gnn_theta_backward), axis=-1)
    return x

_drawn_inputs = setup_inputs


def setup_inputs(seed=0):
    import zlib

    import numpy as np

    out = dict(_drawn_inputs(seed))
    spreads = {'L2_gnn_b_e1': (0.0, 0.1),
     'L2_gnn_b_e2': (0.0, 0.1),
     'L2_gnn_ba1': (0.0, 2.0),
     'L2_gnn_ba2': (0.0, 2.0),
     'L2_gnn_bias': (0.0, 0.34),
     'L2_gnn_ln_g': (1.0, 0.2),
     'L2_gnn_ln_b': (0.0, 0.1)}
    factors = {}
    for name, (base, spread) in spreads.items():
        noise = np.random.default_rng([zlib.crc32(name.encode()), seed]).standard_normal(out[name].shape)
        drawn = base * np.exp(spread * noise) if base else spread * noise
        out[name] = jnp.asarray(drawn.astype(out[name].dtype))
    for name, factor in factors.items():
        out[name] = (out[name] * factor).astype(out[name].dtype)
    return out
```

```python
from contextlib import ExitStack, contextmanager

import concourse.bass as bass
from concourse import mybir

ALU = mybir.AluOpType
ACT = mybir.ActivationFunctionType
AX = mybir.AxisListType
F32 = mybir.dt.float32
BF16 = mybir.dt.bfloat16
I32 = mybir.dt.int32
U32 = mybir.dt.uint32

P = 128
D = 64


@contextmanager
def semaphore(nc, name):
    handle = nc.alloc_semaphore(name=name)
    yield handle
    nc.gpsimd.sem_clear(handle)
    nc.release_semaphore(handle)


def since(engine, sem, value):
    if not isinstance(value, int) or value > 0:
        engine.wait_ge(sem, value)


def rounds(engine, count, body, ahead=1):
    for i in range(ahead):
        body(i)
    with engine.Fori(ahead, count) as i:
        body(i)


class Shapes:

    def __init__(self, n_nodes, n_edges):
        self.n = n_nodes
        self.e = n_edges
        self.blocks = -(-n_nodes // P)
        self.last_rows = n_nodes - (self.blocks - 1) * P
        self.in_tiles = -(-n_edges // P)
        self.groups = 4
        self.group_rows = -(-self.in_tiles // self.groups)
        self.last_edges = n_edges - (self.in_tiles - 1) * P
        assert self.groups * self.group_rows == self.in_tiles and self.last_edges < P
        self.buckets = self.blocks * self.blocks
        self.body = 8
        tiles = n_edges // P + self.buckets
        self.tiles = -(-tiles // self.body) * self.body
        self.rec = 8
        self.dst_tiles = n_edges // P + self.blocks
        assert self.dst_tiles % self.body == 0
        self.split = 32
        self.split_used = 22
        self.ring = 5
        assert self.blocks % self.ring == 0
        self.hops = 10
        self.layers = 3
        self.keep = 0.9
        self.eps = 1e-5
        self.rank_half = 13
        assert self.in_tiles % (4 * self.rank_half) == 0
        self.div_mul, self.div_shift = 1311, 15
        assert all(q * self.div_mul >> self.div_shift == q // self.blocks for q in range(self.buckets + 1))


def edges_in(nc, g, S):
    R, NG, B = S.group_rows, S.groups, S.blocks
    with ExitStack() as ctx:
        sb = lambda name, shape, dt: ctx.enter_context(nc.sbuf_tensor(name, shape, dt))
        sem = lambda name: ctx.enter_context(semaphore(nc, name))
        ends = [sb("src_rows", [R, NG, P], I32), sb("dst_rows", [R, NG, P], I32)]
        w_rows = sb("w_rows", [R, NG, P], F32)
        ea_rows = sb("ea_rows", [R, NG, 3 * P], F32)
        blk_i = [sb("src_blk_i", [R, NG * P], I32), sb("dst_blk_i", [R, NG * P], I32)]
        loc_i = [sb("src_loc_i", [R, NG * P], I32), sb("dst_loc_i", [R, NG * P], I32)]
        blk_f = [sb("src_blk_f", [R, NG, P], F32), sb("dst_blk_f", [R, NG, P], F32)]
        loc_f = [sb("src_loc_f", [R, NG, P], F32), sb("dst_loc_f", [R, NG, P], F32)]
        key_f = sb("key_f", [R, NG, P], F32)
        src_f = sb("src_f", [R, NG, P], F32)
        fill = sb("fill", [P, S.tiles * S.rec], F32)
        turned = ctx.enter_context(nc.psum_tensor("turned", [P, 8, 512], F32))

        padded = sem("padded")
        s_in = sem("edges_landed")
        own = sem("split_steps")
        split = sem("rows_split")
        s_store = sem("rows_stored")
        s_turn = sem("field_turned")
        taken = sem("field_taken")
        filled = sem("fill_ready")

        block = ctx.enter_context(nc.Block())
        last = NG - 1
        full = S.last_edges

        @block.sync
        def _(sp):
            sp.wait_ge(padded, 4)
            for x, rows, k in ((g.src, ends[0], 1), (g.dst, ends[1], 1), (g.w, w_rows, 1), (g.ea, ea_rows, 3)):
                n = last * R * P * k
                sp.dma_start(rows[:, 0:last, :], x[0:n].rearrange("(j r e) -> r j e", j=last, r=R)).then_inc(s_in, 16)
                m = n + (R - 1) * P * k
                sp.dma_start(rows[0:R - 1, last, :], x[n:m].rearrange("(r e) -> r e", r=R - 1)).then_inc(s_in, 16)
                sp.dma_start(rows[R - 1:R, last, 0:full * k], x[m:m + full * k].rearrange("(r e) -> r e", r=1)).then_inc(s_in, 16)
            sp.wait_ge(split, 1)
            sp.dma_start(g.key_rows[:, :].rearrange("(j r) e -> r j e", j=NG), key_f[:, :, :]).then_inc(s_store, 16)
            sp.dma_start(g.blk_rows[:, :].rearrange("(j r) e -> r j e", j=NG), blk_f[1][:, :, :]).then_inc(s_store, 16)
            sp.wait_ge(filled, 1)
            sp.dma_start(g.slots[:, :].rearrange("(p t) f -> p (t f)", p=P), fill[:, :]).then_inc(s_store, 16)
            sp.dma_start(g.dst_slots[:, :].rearrange("(p t) f -> p (t f)", p=P),
                         fill[:, 0:S.dst_tiles * S.rec]).then_inc(s_store, 16)
            sp.wait_ge(s_store, 64)

        @block.gpsimd
        def _(pool):
            nc.gpsimd.memset(fill[:, :], -1.0).then_inc(filled, 1)

        @block.vector
        def _(dve):
            for rows in ends:
                nc.vector.memset(rows[:, last, :], -P).then_inc(padded, 1)
            for rows in (w_rows, ea_rows):
                nc.vector.memset(rows[:, last, :], 0.0).then_inc(padded, 1)
            nc.vector.memset(g.rec[:, :, 3:4], 1.0)
            dve.wait_ge(s_in, 16 * 12)
            for k in range(2):
                flat = ends[k][:, :, :].rearrange("r j e -> r (j e)")
                nc.vector.tensor_scalar(blk_i[k][:, :], flat, 7, None, ALU.arith_shift_right).then_inc(own, 1)
                nc.vector.tensor_scalar(loc_i[k][:, :], flat, P - 1, None, ALU.bitwise_and).then_inc(own, 1)
            dve.wait_ge(own, 4)
            nc.vector.tensor_copy(src_f[:, :, :], ends[0][:, :, :])
            for k in range(2):
                nc.vector.tensor_copy(blk_f[k][:, :, :].rearrange("r j e -> r (j e)"), blk_i[k][:, :]).then_inc(own, 1)
                nc.vector.tensor_copy(loc_f[k][:, :, :].rearrange("r j e -> r (j e)"), loc_i[k][:, :]).then_inc(own, 1)
            dve.wait_ge(own, 8)
            nc.vector.scalar_tensor_tensor(
                out=key_f[:, :, :].rearrange("r j e -> r (j e)"), in0=blk_f[1][:, :, :].rearrange("r j e -> r (j e)"),
                scalar=float(B), in1=blk_f[0][:, :, :].rearrange("r j e -> r (j e)"), op0=ALU.mult, op1=ALU.add,
            ).then_inc(split, 1)
            for f, out in enumerate((g.src_blk[:, :], g.dst_blk[:, :], g.rec[:, :, 0], g.rec[:, :, 1], g.rec[:, :, 2],
                                     g.rec[:, :, 4], g.rec[:, :, 5], g.rec[:, :, 6], g.rec[:, :, 7])):
                dve.wait_ge(s_turn, f + 1)
                nc.vector.tensor_copy(out, turned[:, f % 8, 0:S.in_tiles]).then_inc(taken, 1)

        @block.tensor
        def _(pe):
            pe.wait_ge(split, 1)
            fields = [blk_f[0][:, j, :] for j in range(NG)], [blk_f[1][:, j, :] for j in range(NG)], \
                [loc_f[0][:, j, :] for j in range(NG)], [loc_f[1][:, j, :] for j in range(NG)], \
                [w_rows[:, j, :] for j in range(NG)], \
                *[[ea_rows[:, j, k:3 * P:3] for j in range(NG)] for k in range(3)], [src_f[:, j, :] for j in range(NG)]
            for f, rows in enumerate(fields):
                if f >= 8:
                    pe.wait_ge(taken, f - 7)
                for j in range(NG):
                    mm = nc.tensor.transpose(turned[:, f % 8, j * R:(j + 1) * R], rows[j], g.ident[0:R, 0:R])
                mm.then_inc(s_turn, 1)


def constants(nc, g, S):
    with ExitStack() as ctx:
        made = ctx.enter_context(semaphore(nc, "constants_made"))
        block = ctx.enter_context(nc.Block())

        @block.gpsimd
        def _(pool):
            nc.gpsimd.iota(g.iota_free[:, :], pattern=[[1, P]], base=0, channel_multiplier=0,
                           allow_small_or_imprecise_dtypes=True).then_inc(made, 1)
            nc.gpsimd.iota(g.iota_part[:, :], pattern=[[0, 1]], base=0, channel_multiplier=1,
                           allow_small_or_imprecise_dtypes=True).then_inc(made, 1)

        @block.vector
        def _(dve):
            dve.wait_ge(made, 2)
            nc.vector.tensor_scalar(g.ident[:, :], g.iota_free[:, :], g.iota_part[:, 0:1], None, ALU.is_equal)
            nc.vector.tensor_scalar(g.off_diagonal[:, :], g.iota_free[:, :], g.iota_part[:, 0:1], None, ALU.not_equal)
            nc.vector.tensor_scalar(g.earlier[:, :], g.iota_free[:, :], g.iota_part[:, 0:1], None, ALU.is_lt)
            nc.vector.tensor_scalar(g.before[:, :], g.iota_free[:, :], g.iota_part[:, 0:1], None, ALU.is_gt)



def count_buckets(nc, g, S):
    B, T = S.blocks, S.in_tiles
    CH = S.rank_half
    NB = T // CH
    with ExitStack() as ctx:
        sb = lambda name, shape, dt: ctx.enter_context(nc.sbuf_tensor(name, shape, dt))
        sem = lambda name: ctx.enter_context(semaphore(nc, name))
        dst_hot = sb("dst_hot", [P, T, B], BF16)
        tile_counts = sb("tile_counts", [B, T, B], F32)
        ones = sb("ones_row", [B, T], F32)
        n_int = sb("n_int", [B, 2, B], I32)
        n_tiles = sb("n_tiles", [B, B], F32)
        upto = sb("tiles_upto", [B, B], F32)
        ahead = sb("tiles_ahead", [B, B], F32)
        first = sb("first_tile", [B, B], F32)
        end = sb("end_tile", [B, B], F32)
        first_slot = sb("first_slot", [B, B], F32)
        edges_upto = sb("edges_upto", [B, B], F32)
        edges_ahead = sb("edges_ahead", [B, B], F32)
        d_int = sb("dst_tiles_int", [B, 2], I32)
        d_tiles = sb("dst_tiles", [B, 1], F32)
        d_first = sb("dst_first", [B, 2], F32)
        d_slot = sb("dst_first_slot", [B, 1], F32)
        count_ps = ctx.enter_context(nc.psum_tensor("count_ps", [B, 2, 512], F32))
        base_ps = ctx.enter_context(nc.psum_tensor("base_ps", [B, 512], F32))
        hot = sem("one_hots")
        counted = sem("tiles_counted")
        copied = sem("counts_copied")
        own = sem("count_steps")
        upto_ready = sem("tiles_upto_ready")
        d_ready = sem("dst_tiles_ready")
        d_base = sem("dst_base_ready")
        d_first_ready = sem("dst_first_ready")
        base_ready = sem("row_base_ready")
        first_ready = sem("first_tile_ready")
        s_store = sem("first_tile_stored")
        block = ctx.enter_context(nc.Block())

        @block.tensor
        def _(pe):
            pe.wait_ge(hot, 2)
            for n in range(NB):
                if n >= 2:
                    pe.wait_ge(copied, n - 1)
                for j in range(CH):
                    c = n * CH + j
                    mm = nc.tensor.matmul(count_ps[:, n % 2, j * B:(j + 1) * B], dst_hot[:, c, :], g.src_hot[:, c, :],
                                          start=True, stop=True)
                mm.then_inc(counted, 1)
            pe.wait_ge(upto_ready, 1)
            nc.tensor.matmul(base_ps[:, 0:1], g.before[0:B, 0:B], upto[:, B - 1:B], start=True, stop=True).then_inc(base_ready, 1)
            pe.wait_ge(d_ready, 1)
            nc.tensor.matmul(base_ps[:, 1:2], g.before[0:B, 0:B], d_tiles[:, :], start=True, stop=True).then_inc(d_base, 1)

        @block.vector
        def _(dve):
            steps = [0]

            def step(ins):
                steps[0] += 1
                ins.then_inc(own, 1)
                dve.wait_ge(own, steps[0])

            io = g.iota_free[:, 0:B].unsqueeze(1).broadcast_to([P, T, B])
            for hots, blk in ((g.src_hot, g.src_blk), (dst_hot, g.dst_blk)):
                nc.vector.tensor_tensor(hots[:, :, :], blk[:, :].unsqueeze(2).broadcast_to([P, T, B]), io,
                                        ALU.is_equal).then_inc(hot, 1)
            step(nc.vector.memset(ones[:, :], 1.0))
            step(nc.vector.memset(g.start[:, 0, :], 0.0))
            nc.vector.scalar_tensor_tensor(out=g.key_col[:, :], in0=g.dst_blk[:, :], scalar=float(B), in1=g.src_blk[:, :],
                                           op0=ALU.mult, op1=ALU.add)
            for n in range(NB):
                dve.wait_ge(counted, n + 1)
                nc.vector.tensor_copy(tile_counts[:, n * CH:(n + 1) * CH, :].rearrange("b t a -> b (t a)"),
                                      count_ps[:, n % 2, 0:CH * B]).then_inc(copied, 1)
            dve.wait_ge(copied, NB)
            for a in range(B):
                scan = nc.vector.tensor_tensor_scan(g.start[:, 1:T + 1, a], ones[:, :], tile_counts[:, :, a], 0.0,
                                                    ALU.mult, ALU.add)
                scan.then_inc(own, 1)
            steps[0] += B
            dve.wait_ge(own, steps[0])
            step(nc.vector.tensor_scalar(n_int[:, 0, :], g.start[:, T, :], float(P - 1), None, ALU.add))
            step(nc.vector.tensor_scalar(n_int[:, 1, :], n_int[:, 0, :], 7, None, ALU.arith_shift_right))
            step(nc.vector.tensor_scalar(n_tiles[:, :], n_int[:, 1, :], 1.0, None, ALU.max))
            nc.vector.tensor_tensor_scan(upto[:, :], ones[:, 0:B], n_tiles[:, :], 0.0, ALU.mult, ALU.add).then_inc(upto_ready, 1)
            dve.wait_ge(upto_ready, 1)
            step(nc.vector.tensor_tensor(ahead[:, :], upto[:, :], n_tiles[:, :], ALU.subtract))
            dve.wait_ge(base_ready, 1)
            nc.vector.tensor_scalar(end[:, :], upto[:, :], base_ps[:, 0:1], None, ALU.add).then_inc(first_ready, 1)
            nc.vector.tensor_scalar(first[:, :], ahead[:, :], base_ps[:, 0:1], None, ALU.add).then_inc(first_ready, 1)
            dve.wait_ge(first_ready, 2)
            step(nc.vector.tensor_scalar(first_slot[:, :], first[:, :], float(P), None, ALU.mult))
            step(nc.vector.tensor_tensor_scan(edges_upto[:, :], ones[:, 0:B], g.start[:, T, :], 0.0, ALU.mult, ALU.add))
            step(nc.vector.tensor_tensor(edges_ahead[:, :], edges_upto[:, :], g.start[:, T, :], ALU.subtract))
            step(nc.vector.tensor_scalar(d_int[:, 0:1], edges_upto[:, B - 1:B], float(P - 1), None, ALU.add))
            step(nc.vector.tensor_scalar(d_int[:, 1:2], d_int[:, 0:1], 7, None, ALU.arith_shift_right))
            nc.vector.tensor_copy(d_tiles[:, :], d_int[:, 1:2]).then_inc(d_ready, 1)
            dve.wait_ge(d_base, 1)
            nc.vector.tensor_copy(d_first[:, 0:1], base_ps[:, 1:2]).then_inc(d_first_ready, 1)
            nc.vector.tensor_tensor(d_first[:, 1:2], d_tiles[:, :], base_ps[:, 1:2], ALU.add).then_inc(d_first_ready, 1)
            dve.wait_ge(d_first_ready, 2)
            step(nc.vector.tensor_scalar(d_slot[:, :], d_first[:, 0:1], float(P), None, ALU.mult))
            step(nc.vector.tensor_tensor(edges_ahead[:, :], edges_ahead[:, :], first_slot[:, :], ALU.subtract))
            step(nc.vector.tensor_scalar(g.shift[:, :], edges_ahead[:, :], d_slot[:, 0:1], None, ALU.add))
            nc.vector.tensor_tensor(g.start[:, 0:T, :], g.start[:, 0:T, :],
                                    first_slot[:, :].unsqueeze(1).broadcast_to([B, T, B]), ALU.add)

        @block.sync
        def _(sp):
            sp.wait_ge(first_ready, 2)
            sp.dma_start(g.first_tiles[0:B * B].rearrange("(b a) -> b a", b=B), first[:, :]).then_inc(s_store, 16)
            sp.dma_start(g.first_tiles[B * B:B * B + 1].rearrange("(b a) -> b a", b=1), end[B - 1:B, B - 1:B]).then_inc(s_store, 16)
            sp.wait_ge(d_first_ready, 2)
            with nc.allow_non_contiguous_dma("one number per block"):
                sp.dma_start(g.dst_firsts[0:B].rearrange("(b a) -> b a", a=1), d_first[:, 0:1]).then_inc(s_store, 16)
            sp.dma_start(g.dst_firsts[B:B + 1].rearrange("(b a) -> b a", a=1), d_first[B - 1:B, 1:2]).then_inc(s_store, 16)
            sp.wait_ge(s_store, 64)


def tile_tables(nc, g, S):
    B, NT, ND = S.blocks, S.tiles, S.dst_tiles
    NC = -(-(NT + 2) // P)
    with ExitStack() as ctx:
        sb = lambda name, shape, dt: ctx.enter_context(nc.sbuf_tensor(name, shape, dt))
        sem = lambda name: ctx.enter_context(semaphore(nc, name))
        firsts = sb("firsts", [P, B * B + 1], F32)
        le = sb("begun", [P, B * B + 1], F32)
        num = sb("tile_num", [P, NC], F32)
        cnt = sb("buckets_begun", [P, NC], F32)
        bucket = sb("bucket_row", [P, NC * P], F32)
        q_i = sb("q_i", [1, 2, NT], I32)
        d_firsts = sb("dst_firsts_sb", [1, B + 1], F32)
        d_num = sb("dst_tile_num", [1, ND], F32)
        d_begun = sb("dst_begun", [1, ND, B + 1], F32)
        d_cnt = sb("dst_cnt", [1, ND], F32)
        q_f = sb("q_f", [1, 6, NT], F32)
        landed = sem("firsts_landed")
        numbered = sem("tiles_numbered")
        own = sem("table_steps")
        cnt_ready = sem("buckets_found")
        bucket_back = sem("bucket_row_landed")
        turned = sem("bucket_row_stored")
        block = ctx.enter_context(nc.Block())

        @block.gpsimd
        def _(pool):
            nc.gpsimd.iota(num[:, :], pattern=[[P, NC]], base=0, channel_multiplier=1,
                           allow_small_or_imprecise_dtypes=True).then_inc(numbered, 1)
            nc.gpsimd.iota(d_num[:, :], pattern=[[1, ND]], base=0, channel_multiplier=0,
                           allow_small_or_imprecise_dtypes=True).then_inc(numbered, 1)

        @block.sync
        def _(sp):
            sp.dma_start(firsts[:, :], g.first_tiles[:].unsqueeze(0).broadcast_to([P, B * B + 1])).then_inc(landed, 16)
            sp.dma_start(d_firsts[:, :], g.dst_firsts[:].unsqueeze(0)).then_inc(landed, 16)
            sp.wait_ge(cnt_ready, 1)
            with nc.allow_non_contiguous_dma("one number per tile"):
                sp.dma_start(g.bucket_of[:].rearrange("(c p) -> p c", p=P), cnt[:, :]).then_inc(turned, 16)
            sp.wait_ge(turned, 16)
            sp.dma_start(bucket[:, :], g.bucket_of[:].unsqueeze(0).broadcast_to([P, NC * P])).then_inc(bucket_back, 16)

        @block.vector
        def _(dve):
            steps = [0]

            def step(ins):
                steps[0] += 1
                ins.then_inc(own, 1)
                dve.wait_ge(own, steps[0])

            dve.wait_ge(landed, 32)
            dve.wait_ge(numbered, 2)
            for c in range(NC):
                ins = nc.vector.tensor_scalar(le[:, :], firsts[:, :], num[:, c:c + 1], 0.0, ALU.is_le, ALU.add,
                                              accum_out=cnt[:, c:c + 1])
                if c < NC - 1:
                    step(ins)
            ins.then_inc(cnt_ready, 1)
            step(nc.vector.tensor_tensor(d_begun[:, :, :], d_firsts[:, :].unsqueeze(1).broadcast_to([1, ND, B + 1]),
                                         d_num[:, :].unsqueeze(2).broadcast_to([1, ND, B + 1]), ALU.is_le))
            step(nc.vector.tensor_reduce(d_cnt[:, :], d_begun[:, :, :], AX.X, ALU.add))
            step(nc.vector.tensor_scalar(g.dst_tab[:, :], d_cnt[:, :], -1.0, None, ALU.add))
            dve.wait_ge(bucket_back, 16)
            step(nc.vector.memset(g.same[:, :], 0.0))
            step(nc.vector.tensor_tensor(g.same[:, 1:NT + 1], bucket[:, 1:NT + 1], bucket[:, 0:NT], ALU.is_equal))
            row = bucket[0:1, 0:NT]
            q, k, a, b, same_next, spare = (q_f[:, n, :] for n in range(6))
            step(nc.vector.tensor_scalar(q, row, -1.0, None, ALU.add))
            step(nc.vector.tensor_scalar(q_i[:, 0, :], q, float(S.div_mul), None, ALU.mult))
            step(nc.vector.tensor_scalar(q_i[:, 1, :], q_i[:, 0, :], S.div_shift, None, ALU.arith_shift_right))
            step(nc.vector.tensor_copy(b, q_i[:, 1, :]))
            step(nc.vector.scalar_tensor_tensor(out=a, in0=b, scalar=-float(B), in1=q, op0=ALU.mult, op1=ALU.add))
            tab = g.tab
            step(nc.vector.tensor_copy(tab[:, 0, :], a))
            step(nc.vector.tensor_copy(tab[:, 1, :], b))
            step(nc.vector.tensor_copy(spare.rearrange("o (n s) -> o n s", s=S.body),
                                       g.iota_free[0:1, 0:S.body].unsqueeze(1).broadcast_to([1, NT // S.body, S.body])))
            step(nc.vector.tensor_scalar(spare, spare, float(P), float(S.blocks * P), ALU.mult, ALU.add))
            same_next = g.same[0:1, 1:NT + 1]
            for n, blk in ((2, b), (3, a)):
                step(nc.vector.scalar_tensor_tensor(out=q, in0=blk, scalar=-float(P), in1=spare, op0=ALU.mult, op1=ALU.add))
                step(nc.vector.tensor_tensor(k, q, same_next, ALU.mult))
                step(nc.vector.scalar_tensor_tensor(out=tab[:, n, :], in0=blk, scalar=float(P), in1=k, op0=ALU.mult, op1=ALU.add))


def slot_edges(nc, g, S):
    B, T, CH = S.blocks, S.in_tiles, S.rank_half
    C2 = 2 * CH
    NCH = T // C2
    with ExitStack() as ctx:
        sb = lambda name, shape, dt: ctx.enter_context(nc.sbuf_tensor(name, shape, dt))
        sem = lambda name: ctx.enter_context(semaphore(nc, name))
        keys = sb("keys_spread", [P, 2, C2 * P], F32)
        blks = sb("blks_spread", [B, 2, C2 * P], F32)
        hot_t = sb("dst_hot_turned", [B, 2, C2 * P], F32)
        start_ring = sb("start_ring", [B, 2, C2 * B], F32)
        rec_ring = sb("rec_ring", [P, 2, C2, S.rec], F32)
        picked = sb("picked", [P, C2, B], F32)
        base = sb("base_slot", [P, C2], F32)
        shifted = sb("shifted", [P, C2, B], F32)
        shift = sb("shift_of_edge", [P, C2], F32)
        rank = sb("rank_in_tile", [P, C2], F32)
        off = sb("no_edge", [P, C2], F32)
        slot_i = sb("slot_i", [P, 3, C2], I32)
        dslot_i = sb("dst_slot_i", [P, 3, C2], I32)
        drow_f = sb("dst_row_f", [P, C2], F32)
        row_f = sb("row_f", [P, C2], F32)
        index = sb("slot_index", [P, 2, C2], U32)
        look_ps = ctx.enter_context(nc.psum_tensor("look_ps", [P, 4, 512], F32))
        shift_ps = ctx.enter_context(nc.psum_tensor("shift_ps", [P, 4, 512], F32))
        spread_free = sem("spread_free")
        landed = [sem("even_chunk_landed"), sem("odd_chunk_landed")]
        hot_ready = sem("turned_hot_ready")
        looked = sem("bases_looked_up")
        look_free = sem("look_ps_free")
        own = sem("slot_steps")
        ring_free = sem("record_ring_free")
        indexed = sem("slots_indexed")
        sent = nc.alloc_semaphore(name="records_sent")
        g.sent = nc.alloc_semaphore(name="records_sent_by_dst")
        block = ctx.enter_context(nc.Block())
        NS = 12
        no_slot = float(4 * S.tiles * P)

        @block.sync
        def _(sp):
            with sp.Fori(0, NCH // 2) as i:
                for h in range(2):
                    q = i * 2 + h
                    sp.wait_ge(spread_free, q + 1)
                    rows = bass.ds(q * C2, C2)
                    sp.dma_start(keys[:, h, :], g.key_rows[rows, :].rearrange("t e -> (t e)").unsqueeze(0).broadcast_to([P, C2 * P])).then_inc(landed[h], 16)
                    sp.dma_start(blks[:, h, :], g.blk_rows[rows, :].rearrange("t e -> (t e)").unsqueeze(0).broadcast_to([B, C2 * P])).then_inc(landed[h], 16)

        @block.tensor
        def _(pe):
            with pe.Fori(0, NCH // 2) as i:
                for h in range(2):
                    q = i * 2 + h
                    pe.wait_ge(hot_ready, 2 * q + 2)
                    pe.wait_ge(look_free, q + 1)
                    for j in range(C2):
                        mm = nc.tensor.matmul(look_ps[:, 2 * h + j // CH, (j % CH) * B:(j % CH + 1) * B],
                                              hot_t[:, h, j * P:(j + 1) * P], start_ring[:, h, j * B:(j + 1) * B],
                                              start=True, stop=True)
                        mm = nc.tensor.matmul(shift_ps[:, 2 * h + j // CH, (j % CH) * B:(j % CH + 1) * B],
                                              hot_t[:, h, j * P:(j + 1) * P], g.shift[:, :], start=True, stop=True)
                    mm.then_inc(looked, 1)

        @block.vector
        def _(dve):
            dve.sem_inc(spread_free, 2)
            dve.sem_inc(look_free, 2)

            def pair(i):
                for h in range(2):
                    q = i * 2 + h
                    steps = [0]

                    def step(ins):
                        steps[0] += 1
                        ins.then_inc(own, 1)
                        dve.wait_ge(own, q * NS + steps[0])

                    cols = bass.ds(q * C2, C2)
                    dve.wait_ge(landed[h], i * 32 + 32)
                    nc.vector.tensor_scalar(hot_t[:, h, :], blks[:, h, :], g.iota_part[0:B, 0:1], None, ALU.is_equal).then_inc(hot_ready, 1)
                    nc.vector.tensor_copy(start_ring[:, h, :].rearrange("b (t a) -> b t a", a=B), g.start[:, cols, :]).then_inc(hot_ready, 1)
                    for j in range(C2):
                        ins = nc.vector.scalar_tensor_tensor(
                            out=keys[:, h, j * P:(j + 1) * P], in0=keys[:, h, j * P:(j + 1) * P], scalar=g.key_col[:, bass.ds(q * C2 + j, 1)],
                            in1=g.earlier[:, :], op0=ALU.is_equal, op1=ALU.mult, accum_out=rank[:, j:j + 1])
                    ins.then_inc(spread_free, 1)
                    dve.wait_ge(spread_free, q + 3)
                    dve.wait_ge(looked, q + 1)
                    for k in range(2):
                        hot = g.src_hot[:, bass.ds(q * C2 + k * CH, CH), :]
                        nc.vector.tensor_tensor(picked[:, k * CH:(k + 1) * CH, :],
                                                look_ps[:, 2 * h + k, 0:CH * B].rearrange("p (t a) -> p t a", a=B),
                                                hot, ALU.mult)
                        ins = nc.vector.tensor_tensor(shifted[:, k * CH:(k + 1) * CH, :],
                                                      shift_ps[:, 2 * h + k, 0:CH * B].rearrange("p (t a) -> p t a", a=B),
                                                      hot, ALU.mult)
                    ins.then_inc(look_free, 1)
                    dve.wait_ge(look_free, q + 3)
                    step(nc.vector.tensor_reduce(base[:, :], picked[:, :, :], AX.X, ALU.add))
                    step(nc.vector.tensor_tensor(slot_i[:, 0, :], base[:, :], rank[:, :], ALU.add))
                    step(nc.vector.tensor_scalar(slot_i[:, 1, :], slot_i[:, 0, :], 7, None, ALU.arith_shift_right))
                    step(nc.vector.tensor_scalar(slot_i[:, 2, :], slot_i[:, 0, :], P - 1, None, ALU.bitwise_and))
                    step(nc.vector.scalar_tensor_tensor(out=row_f[:, :], in0=slot_i[:, 2, :], scalar=float(S.tiles),
                                                        in1=slot_i[:, 1, :], op0=ALU.mult, op1=ALU.add))
                    step(nc.vector.tensor_scalar(off[:, :], g.key_col[:, cols], 0.0, no_slot, ALU.is_lt, ALU.mult))
                    step(nc.vector.tensor_reduce(shift[:, :], shifted[:, :, :], AX.X, ALU.add))
                    step(nc.vector.tensor_tensor(dslot_i[:, 0, :], slot_i[:, 0, :], shift[:, :], ALU.add))
                    step(nc.vector.tensor_scalar(dslot_i[:, 1, :], dslot_i[:, 0, :], 7, None, ALU.arith_shift_right))
                    step(nc.vector.tensor_scalar(dslot_i[:, 2, :], dslot_i[:, 0, :], P - 1, None, ALU.bitwise_and))
                    step(nc.vector.scalar_tensor_tensor(out=drow_f[:, :], in0=dslot_i[:, 2, :], scalar=float(S.dst_tiles),
                                                        in1=dslot_i[:, 1, :], op0=ALU.mult, op1=ALU.add))
                    nc.vector.tensor_tensor(g.dst_index[:, cols], drow_f[:, :], off[:, :], ALU.add)
                    since(dve, ring_free, q)
                    nc.vector.tensor_copy(rec_ring[:, h, :, :], g.rec[:, cols, :]).then_inc(indexed, 1)
                    step(nc.vector.tensor_tensor(index[:, h, :], row_f[:, :], off[:, :], ALU.add))
                    assert steps[0] == NS

            rounds(dve, NCH // 2, pair)

        @block.gpsimd
        def _(pool):
            last_row = pool.to_reg(S.tiles * P - 1)

            def pair(i):
                for h in range(2):
                    q = i * 2 + h
                    since(pool, sent, q * (16 * C2))
                    pool.wait_ge(indexed, q + 1)
                    pool.wait_ge(own, q * NS + NS)
                    pool.sem_inc(ring_free, 1)
                    for j in range(C2):
                        nc.gpsimd.indirect_dma_start(
                            out=g.slots[:, :], out_offset=bass.IndirectOffsetOnAxis(ap=index[:, h, j:j + 1], axis=0),
                            in_=rec_ring[:, h, j, :], in_offset=None, bounds_check=last_row, oob_is_err=False,
                        ).then_inc(sent, 16)

            rounds(pool, NCH // 2, pair)
            pool.wait_ge(sent, NCH * 16 * C2)


def load_slots(nc, g, S):
    with ExitStack() as ctx:
        landed = ctx.enter_context(semaphore(nc, "slots_landed"))
        block = ctx.enter_context(nc.Block())

        @block.sync
        def _(sp):
            sp.dma_start(g.recs[:, :, :].rearrange("p t f -> p (t f)"),
                         g.slots[:, :].rearrange("(p t) f -> p (t f)", p=P)).then_inc(landed, 16)
            sp.wait_ge(landed, 16)


def send_by_dst(nc, g, S, pool, C2, rec_stage, index_stage, sent, copied, begun):
    last_row = pool.to_reg(S.dst_tiles * P - 1)

    def chunk(i):
        since(pool, sent, i * (16 * C2))
        cols = bass.ds(i * C2, C2)
        nc.gpsimd.tensor_copy(rec_stage[:, :, :], g.rec[:, cols, :]).then_inc(copied, 1)
        nc.gpsimd.tensor_copy(index_stage[:, :], g.dst_index[:, cols]).then_inc(copied, 1)
        pool.wait_ge(copied, i * 2 + 2)
        pool.sem_inc(begun, 1)
        for j in range(C2):
            nc.gpsimd.indirect_dma_start(
                out=g.dst_slots[:, :], out_offset=bass.IndirectOffsetOnAxis(ap=index_stage[:, j:j + 1], axis=0),
                in_=rec_stage[:, j, :], in_offset=None, bounds_check=last_row, oob_is_err=False,
            ).then_inc(sent, 16)

    rounds(pool, S.in_tiles // C2, chunk)
    pool.wait_ge(sent, S.in_tiles * 16)


def numbers(nc, engine, ap, top):
    _, values = nc.values_load_multi_w_load_instructions(
        ap, engines=[engine], min_val=0, max_val=top,
        skip_runtime_bounds_check_because="stage 3 makes the row from counts of buckets, all of them in this range")
    return values


def build_matrices(nc, g, S):
    B, NT, U = S.blocks, S.tiles, S.body
    H = U // 2
    with ExitStack() as ctx:
        sb = lambda name, shape, dt=F32: ctx.enter_context(nc.sbuf_tensor(name, shape, dt))
        sem = lambda name: ctx.enter_context(semaphore(nc, name))
        src_hot = sb("src_hot_e", [P, U, P])
        dst_hot = sb("dst_hot_e", [P, U, P])
        wsrc_hot = sb("wsrc_hot_e", [P, U, P])
        one_w = sb("weight_and_one", [P, U, 2])
        done = sb("block_done", [P, U, 2 * P])
        ps = ctx.enter_context(nc.psum_tensor("block_ps", [P, U, 512], F32))
        hot = sem("hots_ready")
        mult = sem("blocks_multiplied")
        ready = sem("blocks_ready")
        degs = sem("degrees_added")
        zero = sem("sums_zeroed")
        out = [sem(f"block_out_{s}") for s in range(U)]
        C2 = 2 * S.rank_half
        rec_stage = sb("rec_stage", [P, C2, S.rec])
        index_stage = sb("index_stage", [P, C2], U32)
        copied = sem("records_staged")
        begun = sem("chunk_begun")
        block = ctx.enter_context(nc.Block())

        @block.gpsimd
        def _(pool):
            send_by_dst(nc, g, S, pool, C2, rec_stage, index_stage, g.sent, copied, begun)

        @block.vector
        def _(dve):
            nc.vector.memset(done[:, U - 1, :], 0.0).then_inc(zero, 1)
            nc.vector.memset(g.deg[:, :, :], 0.0).then_inc(zero, 1)
            dve.wait_ge(zero, 2)

            def eight(i):
                for h in range(2):
                    blk_a = numbers(nc, mybir.EngineType.DVE, g.tab[0:1, 0, bass.ds(i * U + h * H, H)], B)
                    blk_b = numbers(nc, mybir.EngineType.DVE, g.tab[0:1, 1, bass.ds(i * U + h * H, H)], B)
                    since(dve, mult, i * U)
                    for k in range(H):
                        s = h * H + k
                        rec = lambda f: g.recs[:, bass.ds(i * U + s, 1), f]
                        nc.vector.tensor_scalar(src_hot[:, s, :], g.iota_free[:, :], rec(0), None, ALU.is_equal).then_inc(hot, 1)
                        nc.vector.tensor_scalar(dst_hot[:, s, :], g.iota_free[:, :], rec(1), None, ALU.is_equal).then_inc(hot, 1)
                        nc.vector.tensor_scalar(wsrc_hot[:, s, :], g.iota_free[:, :], rec(0), rec(2), ALU.is_equal, ALU.mult).then_inc(hot, 1)
                        nc.vector.tensor_copy(one_w[:, s, :], g.recs[:, bass.ds(i * U + s, 1), 2:4]).then_inc(hot, 1)
                    for k in range(H):
                        s = h * H + k
                        n = i * U + s
                        dve.wait_ge(mult, n + 1)
                        since(dve, out[s], i * 32)
                        since(dve, ready, n)
                        since(dve, degs, 2 * n)
                        nc.vector.scalar_tensor_tensor(out=done[:, s, :], in0=done[:, (s - 1) % U, :], scalar=g.same[:, bass.ds(n, 1)],
                                                       in1=ps[:, s, 0:2 * P], op0=ALU.mult, op1=ALU.add).then_inc(ready, 1)
                        for blk, c0, c1 in ((blk_a[k], 0, 2), (blk_b[k], 2, 3)):
                            d = g.deg[:, bass.ds(blk, 1), c0:c1].rearrange("p o c -> p (o c)")
                            nc.vector.tensor_tensor(d, d, ps[:, s, 2 * P + c0:2 * P + c1], ALU.add).then_inc(degs, 1)

            rounds(dve, NT // U, eight)

        @block.tensor
        def _(pe):
            def eight(i):
                for s in range(U):
                    n = i * U + s
                    pe.wait_ge(hot, 4 * n + 4)
                    since(pe, degs, i * 2 * U)
                    nc.tensor.matmul(ps[:, s, 0:P], src_hot[:, s, :], dst_hot[:, s, :], start=True, stop=True)
                    nc.tensor.matmul(ps[:, s, 2 * P:2 * P + 2], src_hot[:, s, :], one_w[:, s, :], start=True, stop=True)
                    nc.tensor.matmul(ps[:, s, P:2 * P], dst_hot[:, s, :], wsrc_hot[:, s, :], start=True, stop=True)
                    nc.tensor.matmul(ps[:, s, 2 * P + 2:2 * P + 3], dst_hot[:, s, :], one_w[:, s, 1:2], start=True, stop=True).then_inc(mult, 1)

            rounds(pe, NT // U, eight)

        @block.sync
        def _(sp):
            top = (B + U - 1) * P
            with sp.Fori(0, NT // U) as i:
                for h in range(2):
                    blk_a, blk_b, row_c, row_w = (
                        numbers(nc, mybir.EngineType.SP, g.tab[0:1, f, bass.ds(i * U + h * H, H)], m)
                        for f, m in ((0, B), (1, B), (2, top), (3, top)))
                    for k in range(H):
                        s = h * H + k
                        sp.wait_ge(ready, i * U + s + 1)
                        sp.dma_start(g.counts[bass.ds(row_c[k], P), bass.ds(blk_a[k] * P, P)], done[:, s, 0:P]).then_inc(out[s], 16)
                        sp.dma_start(g.weights[bass.ds(row_w[k], P), bass.ds(blk_b[k] * P, P)], done[:, s, P:2 * P]).then_inc(out[s], 16)
            for s in range(U):
                sp.wait_ge(out[s], 32 * (NT // U))


def load_features(nc, g, S):
    with ExitStack() as ctx:
        zero = ctx.enter_context(semaphore(nc, "x_zeroed"))
        landed = ctx.enter_context(semaphore(nc, "x_landed"))
        block = ctx.enter_context(nc.Block())
        full = (S.blocks - 1) * P

        @block.vector
        def _(dve):
            nc.vector.memset(g.x[:, S.blocks - 1, :], 0.0).then_inc(zero, 1)

        @block.sync
        def _(sp):
            sp.wait_ge(zero, 1)
            sp.dma_start(g.x[:, 0:S.blocks - 1, :], g.x_in[0:full, :].rearrange("(b p) d -> p b d", p=P)).then_inc(landed, 16)
            sp.dma_start(g.x[0:S.last_rows, S.blocks - 1, :], g.x_in[full:S.n, :]).then_inc(landed, 16)
            sp.wait_ge(landed, 32)


def spread(ap, n):
    return ap.unsqueeze(2).broadcast_to([ap.shape[0], ap.shape[1], n])


def degree_scales(nc, g, S):
    B = S.blocks
    with ExitStack() as ctx:
        sb = lambda name, shape, dt=F32: ctx.enter_context(nc.sbuf_tensor(name, shape, dt))
        sem = lambda name: ctx.enter_context(semaphore(nc, name))
        clipped = sb("clipped", [P, 3, B])
        root = sb("root", [P, 3, B])
        inv = sb("inverse_root", [P, 3, B])
        there = sb("has_weight", [P, B])
        own = sem("scale_steps")
        clip_ready = sem("clipped_ready")
        root_ready = sem("roots_ready")
        block = ctx.enter_context(nc.Block())

        @block.scalar
        def _(act):
            act.wait_ge(clip_ready, 1)
            nc.scalar.activation(root[:, :, :], clipped[:, :, :], ACT.Sqrt).then_inc(root_ready, 1)

        @block.vector
        def _(dve):
            steps = [0]

            def step(ins):
                steps[0] += 1
                ins.then_inc(own, 1)
                dve.wait_ge(own, steps[0])

            step(nc.vector.tensor_scalar(clipped[:, 0, :], g.deg[:, 0:B, 1], 1.0, None, ALU.max))
            step(nc.vector.tensor_scalar(clipped[:, 1, :], g.deg[:, 0:B, 2], 1.0, None, ALU.max))
            step(nc.vector.tensor_scalar(there[:, :], g.deg[:, 0:B, 0], 0.0, None, ALU.is_gt))
            step(nc.vector.tensor_tensor(clipped[:, 2, :], g.deg[:, 0:B, 0], there[:, :], ALU.mult))
            step(nc.vector.scalar_tensor_tensor(out=clipped[:, 2, :], in0=clipped[:, 2, :], scalar=1.0, in1=there[:, :],
                                                op0=ALU.add, op1=ALU.subtract))
            clip = nc.vector.memset(inv[:, :, :], 0.0)
            clip.then_inc(clip_ready, 1)
            dve.wait_ge(root_ready, 1)
            step(nc.vector.reciprocal(inv[:, :, :], root[:, :, :]))
            step(nc.vector.tensor_tensor(g.w_inv[:, :], inv[:, 2, :], there[:, :], ALU.mult))
            step(nc.vector.tensor_scalar(g.hop_last[:, :], inv[:, 1, :], S.keep, None, ALU.mult))
            step(nc.vector.tensor_tensor(g.hop[:, :], g.hop_last[:, :], inv[:, 0, :], ALU.mult))
            step(nc.vector.tensor_scalar(g.rest_last[:, :, :], g.x[:, :, :], 1.0 - S.keep, None, ALU.mult))
            step(nc.vector.tensor_tensor(g.rest[:, :, :], g.rest_last[:, :, :], spread(inv[:, 0, :], D), ALU.mult))
            step(nc.vector.tensor_tensor(g.hs[0][:, :, :], g.x[:, :, :], spread(inv[:, 0, :], D), ALU.mult))


def sweeps(nc, g, S, name, matrix, repeats, places, finish, clear_diagonal=False):
    B = S.blocks
    RING = S.ring
    with ExitStack() as ctx:
        sem = lambda n: ctx.enter_context(semaphore(nc, f"{name}_{n}"))
        rows = ctx.enter_context(nc.sbuf_tensor(f"{name}_rows", [P, RING, B * P], F32))
        ps = ctx.enter_context(nc.psum_tensor(f"{name}_ps", [P, RING, 512], F32))
        landed = [sem(f"row_landed_{s}") for s in range(RING)]
        free = sem("row_free")
        cleared = sem("diagonal_cleared")
        summed = sem("product_summed")
        own = sem("sweep_steps")
        block = ctx.enter_context(nc.Block())
        NP = len(places)

        @block.sync
        def _(sp):
            with sp.Fori(0, repeats) as r:
                for p in range(NP):
                    with sp.Fori(0, B // RING) as i:
                        for s in range(RING):
                            n = (r * NP + p) * B + i * RING + s
                            sp.wait_ge(free, n + 1)
                            sp.dma_start(rows[:, s, :], matrix[bass.ds((i * RING + s) * P, P), 0:B * P]).then_inc(landed[s], 16)

        @block.tensor
        def _(pe):
            with pe.Fori(0, repeats) as r:
                for p in range(NP):
                    h = places[p][0]
                    with pe.Fori(0, B // RING) as i:
                        for s in range(RING):
                            n = (r * NP + p) * B + i * RING + s
                            pe.wait_ge(landed[s], (r * NP + p) * (16 * B // RING) + i * 16 + 16)
                            pe.wait_ge(free, n + 1)
                            if s == 0:
                                pe.wait_ge(free, (r * NP + p) * B + RING)
                            if clear_diagonal:
                                pe.wait_ge(cleared, n + 1)
                            for k in range(B):
                                mm = nc.tensor.matmul(ps[:, s, 0:D], rows[:, s, k * P:(k + 1) * P], h[:, k, :],
                                                      start=(k == 0), stop=(k == B - 1))
                            mm.then_inc(summed, 1)

        @block.vector
        def _(dve):
            dve.sem_inc(free, RING)
            with dve.Fori(0, repeats) as r:
                for p in range(NP):
                    with dve.Fori(0, B // RING) as i:
                        for s in range(RING):
                            n = (r * NP + p) * B + i * RING + s
                            if clear_diagonal:
                                dve.wait_ge(landed[s], (r * NP + p) * (16 * B // RING) + i * 16 + 16)
                                own_block = rows[:, s, bass.ds((i * RING + s) * P, P)]
                                nc.vector.tensor_tensor(own_block, own_block, g.off_diagonal[:, :], ALU.mult).then_inc(cleared, 1)
                            dve.wait_ge(summed, n + 1)
                            finish(p, i * RING + s, ps[:, s, 0:D]).then_inc(free, 1)


def node(ap, m):
    return ap[:, bass.ds(m, 1), :].rearrange("p o d -> p (o d)")


def node_scale(ap, m):
    return ap[:, bass.ds(m, 1)]


def hops(nc, g, S):
    def even_odd(p, m, product):
        return nc.vector.scalar_tensor_tensor(out=node(g.hs[1 - p], m), in0=product, scalar=node_scale(g.hop, m),
                                              in1=node(g.rest, m), op0=ALU.mult, op1=ALU.add)

    def last(p, m, product):
        if p == 0:
            return even_odd(p, m, product)
        return nc.vector.scalar_tensor_tensor(out=node(g.hs[0], m), in0=product, scalar=node_scale(g.hop_last, m),
                                              in1=node(g.rest_last, m), op0=ALU.mult, op1=ALU.add)

    pairs = [(g.hs[0], g.hs[1]), (g.hs[1], g.hs[0])]
    sweeps(nc, g, S, "hop", g.counts, S.hops // 2 - 1, pairs, even_odd)
    sweeps(nc, g, S, "lasthop", g.counts, 1, pairs, last)


def layer_norm(nc, g, S, name, z_in, out, before=None, after=None):
    B = S.blocks
    with ExitStack() as ctx:
        sb = lambda n, shape, dt=F32: ctx.enter_context(nc.sbuf_tensor(f"{name}_{n}", shape, dt))
        sem = lambda n: ctx.enter_context(semaphore(nc, f"{name}_{n}"))
        mean = sb("mean", [P, B])
        var = sb("var", [P, B])
        root = sb("root", [P, B])
        inv = sb("inv", [P, B])
        sq = sb("squares", [P, B, D])
        own = sem("steps")
        var_ready = sem("variance_ready")
        root_ready = sem("root_ready")
        block = ctx.enter_context(nc.Block())

        @block.scalar
        def _(act):
            act.wait_ge(var_ready, 1)
            nc.scalar.activation(root[:, :], var[:, :], ACT.Sqrt).then_inc(root_ready, 1)

        @block.vector
        def _(dve):
            steps = [0]

            def step(ins):
                steps[0] += 1
                ins.then_inc(own, 1)
                dve.wait_ge(own, steps[0])

            if before:
                before(step)
            step(nc.vector.tensor_reduce(mean[:, :], z_in[:, :, :], AX.X, ALU.add))
            step(nc.vector.tensor_scalar(mean[:, :], mean[:, :], 1.0 / D, None, ALU.mult))
            step(nc.vector.tensor_tensor(out[:, :, :], z_in[:, :, :], spread(mean[:, :], D), ALU.subtract))
            step(nc.vector.tensor_tensor(sq[:, :, :], out[:, :, :], out[:, :, :], ALU.mult))
            step(nc.vector.tensor_reduce(var[:, :], sq[:, :, :], AX.X, ALU.add))
            nc.vector.tensor_scalar(var[:, :], var[:, :], 1.0 / D, S.eps, ALU.mult, ALU.add).then_inc(var_ready, 1)
            dve.wait_ge(root_ready, 1)
            step(nc.vector.reciprocal(inv[:, :], root[:, :]))
            step(nc.vector.tensor_tensor(out[:, :, :], out[:, :, :], spread(inv[:, :], D), ALU.mult))
            if after:
                after(step)


def first_layers(nc, g, S):
    B = S.blocks
    with ExitStack() as ctx:
        sb = lambda name, shape, dt=F32: ctx.enter_context(nc.sbuf_tensor(name, shape, dt))
        g.rest = sb("rest", [P, B, D])
        g.rest_last = sb("rest_last", [P, B, D])
        g.hs = [sb("hs_even", [P, B, D]), sb("hs_odd", [P, B, D])]
        g.hop = sb("hop", [P, B])
        g.hop_last = sb("hop_last", [P, B])
        eps1 = sb("one_plus_eps", [P, 1])
        degree_scales(nc, g, S)
        hops(nc, g, S)

        def add_x(step):
            step(nc.vector.tensor_tensor(g.hs[0][:, :, :], g.hs[0][:, :, :], g.x[:, :, :], ALU.add))

        layer_norm(nc, g, S, "norm0", g.hs[0], g.x, add_x)
        with semaphore(nc, "eps_landed") as landed, nc.Block() as block:
            @block.sync
            def _(sp):
                sp.dma_start(eps1[:, :], g.eps1_in[:].unsqueeze(0).broadcast_to([P, 1])).then_inc(landed, 16)

            @block.vector
            def _(dve):
                dve.wait_ge(landed, 16)
                nc.vector.tensor_scalar(eps1[:, :], eps1[:, :], 1.0, None, ALU.add)

        def neighbours(p, m, product):
            return nc.vector.scalar_tensor_tensor(out=node(g.hs[0], m), in0=node(g.x, m), scalar=eps1[:, 0:1],
                                                  in1=product, op0=ALU.mult, op1=ALU.add)

        sweeps(nc, g, S, "weighted", g.weights, 1, [(g.x, g.hs[0])], neighbours, clear_diagonal=True)
        layer_norm(nc, g, S, "norm1", g.hs[0], g.x, add_x)


def split_slots(nc, g, S):
    ND, R, F = S.dst_tiles, S.rec, S.split
    G = 4
    N = ND // G
    with ExitStack() as ctx:
        sb = lambda name, shape, dt=F32: ctx.enter_context(nc.sbuf_tensor(name, shape, dt))
        sem = lambda name: ctx.enter_context(semaphore(nc, name))
        recs = sb("dst_recs", [P, ND, R])
        left = sb("attr_left", [P, ND, 3])
        parts = sb("split_records", [P, ND, F], BF16)
        ident_b = sb("ident_b", [P, P], BF16)
        node_f = sb("src_node_f", [P, ND])
        taken = sb("records_taken", [P, 2, G * R])
        taken_b = sb("split_taken", [P, 2, G * F], BF16)
        out = sb("attr_turned", [G * R, 2, P])
        out_b = sb("split_turned", [G * F, 2, P], BF16)
        ps = ctx.enter_context(nc.psum_tensor("records_ps", [P, 2, 512], F32))
        ps_b = ctx.enter_context(nc.psum_tensor("split_ps", [P, 2, 1024], BF16))
        landed = sem("dst_records_landed")
        own = sem("split_steps")
        copied = sem("records_copied")
        tr = sem("records_transposed")
        ready = sem("turned_ready")
        ready_b = sem("split_turned_ready")
        stored = [sem("even_turned_stored"), sem("odd_turned_stored")]
        block = ctx.enter_context(nc.Block())

        @block.sync
        def _(sp):
            sp.dma_start(recs[:, :, :].rearrange("p t f -> p (t f)"),
                         g.dst_slots[:, :].rearrange("(p t) f -> p (t f)", p=P)).then_inc(landed, 16)

            def pair(i):
                for h in range(2):
                    n = i * 2 + h
                    sp.wait_ge(ready, n + 1)
                    sp.wait_ge(ready_b, n + 1)
                    cols = bass.ds(n * (G * P), G * P)
                    sp.dma_start(g.attr_rows[:, cols].rearrange("f (t e) -> t f e", e=P), out[:, h, :]).then_inc(stored[h], 16)
                    sp.dma_start(g.split_rows[:, cols].rearrange("f (t e) -> t f e", e=P), out_b[:, h, :]).then_inc(stored[h], 16)

            rounds(sp, N // 2, pair)
            for h in range(2):
                sp.wait_ge(stored[h], N // 2 * 32)

        @block.vector
        def _(dve):
            steps = [0]

            def step(ins):
                steps[0] += 1
                ins.then_inc(own, 1)
                dve.wait_ge(own, steps[0])

            step(nc.vector.memset(parts[:, :, :], 0.0))
            nc.vector.memset(parts[:, :, 1:4], 1.0)
            nc.vector.tensor_copy(ident_b[:, :], g.ident[:, :])
            dve.wait_ge(landed, 16)
            nc.vector.tensor_copy(parts[:, :, 0], recs[:, :, 1])
            nc.vector.tensor_copy(g.dst_col[:, :], recs[:, :, 1])
            step(nc.vector.tensor_scalar(node_f[:, :], recs[:, :, 7], 0.0, None, ALU.max))
            nc.vector.tensor_copy(g.src_node[:, :], node_f[:, :])
            hi, mid, low = parts[:, :, 4:7], parts[:, :, 7:10], parts[:, :, 10:13]
            step(nc.vector.tensor_copy(hi, recs[:, :, 4:7]))
            step(nc.vector.tensor_tensor(left[:, :, :], recs[:, :, 4:7], hi, ALU.subtract))
            step(nc.vector.tensor_copy(mid, left[:, :, :]))
            step(nc.vector.tensor_tensor(left[:, :, :], left[:, :, :], mid, ALU.subtract))
            nc.vector.tensor_copy(low, left[:, :, :])
            nc.vector.tensor_copy(parts[:, :, 13:19], parts[:, :, 4:10])
            step(nc.vector.tensor_copy(parts[:, :, 19:22], hi))

            def pair(i):
                for h in range(2):
                    n = i * 2 + h
                    since(dve, tr, n - 1)
                    tiles = bass.ds(n * G, G)
                    nc.vector.tensor_copy(taken[:, h, :].rearrange("p (t f) -> p t f", f=R), recs[:, tiles, :]).then_inc(copied, 1)
                    nc.vector.tensor_copy(taken_b[:, h, :].rearrange("p (t f) -> p t f", f=F), parts[:, tiles, :]).then_inc(copied, 1)
                    dve.wait_ge(tr, n + 1)
                    since(dve, stored[h], i * 32)
                    nc.vector.tensor_copy(out[:, h, :], ps[0:G * R, h, 0:P]).then_inc(ready, 1)
                    nc.vector.tensor_copy(out_b[:, h, :], ps_b[:, h, 0:P]).then_inc(ready_b, 1)

            rounds(dve, N // 2, pair)

        @block.tensor
        def _(pe):
            def pair(i):
                for h in range(2):
                    n = i * 2 + h
                    pe.wait_ge(copied, n * 2 + 2)
                    since(pe, ready_b, n - 1)
                    nc.tensor.transpose(ps[0:G * R, h, 0:P], taken[:, h, :], g.ident[:, :])
                    nc.tensor.transpose(ps_b[:, h, 0:P], taken_b[:, h, :], ident_b[:, :]).then_inc(tr, 1)

            rounds(pe, N // 2, pair)


def node_tables(nc, g, S, l):
    B = S.blocks
    CH = [(c, min(4, B - c)) for c in range(0, B, 4)]
    with ExitStack() as ctx:
        sb = lambda name, shape, dt=F32: ctx.enter_context(nc.sbuf_tensor(f"l{l}_{name}", shape, dt))
        sem = lambda name: ctx.enter_context(semaphore(nc, f"l{l}_{name}"))
        h_t = sb("h_turned", [D, B * P])
        hx_t = sb("hx_turned", [D, B * P])
        w_att = sb("w_attention", [D, 2 * D])
        table = sb("table", [P, B, 3 * D])
        left = sb("left", [P, B, D])
        w_left = sb("w_left", [S.split_used, D])
        w_hi = sb("w_hi", [S.split_used, D], BF16)
        w_mid = sb("w_mid", [S.split_used, D], BF16)
        w_low = sb("w_low", [S.split_used, D], BF16)
        ps = lambda name: ctx.enter_context(nc.psum_tensor(f"l{l}_{name}", [P, 2, 512], F32))
        t_ps, x_ps, n_ps = ps("turn_ps"), ps("hx_ps"), ps("table_ps")
        landed = sem("weights_landed")
        e1_landed = sem("edge_weights_landed")
        zeroed = sem("weights_zeroed")
        turned = sem("h_turned")
        turned_sb = sem("h_turned_copied")
        hx = sem("hx_ready")
        hx_sb = sem("hx_copied")
        tab = sem("table_ready")
        tab_sb = sem("table_copied")
        tab_out = sem("table_stored")
        own = sem("node_steps")
        split_w = sem("edge_weights_split")
        placed = sem("edge_weights_placed")
        block = ctx.enter_context(nc.Block())

        @block.gpsimd
        def _(pool):
            nc.gpsimd.memset(g.w_edge[:, :], 0.0).then_inc(zeroed, 1)

        @block.sync
        def _(sp):
            def load(out, src, s=landed):
                sp.dma_start(out, src).then_inc(s, 16)
            row = lambda v: v.unsqueeze(0)
            sp.wait_ge(zeroed, 2)
            for k in range(1, 4):
                load(g.w_e1[k:k + 1, :], row(g.b_e1[l]), e1_landed)
            for k in range(6):
                load(g.w_e1[4 + 3 * k:7 + 3 * k, :], g.W_e1[l], e1_landed)
            load(g.w_node[:, :], g.W_node[l])
            load(w_att[:, 0:D], g.Wa1[l, D:2 * D, :])
            load(w_att[:, D:2 * D], g.Wa1[l, 0:D, :])
            load(g.wa2[:, :], g.Wa2[l].rearrange("d o -> (d o)").unsqueeze(0).broadcast_to([P, D]))
            load(g.ba2[:, :], row(g.ba2_in[l]).broadcast_to([P, 1]))
            load(g.bias[:, :], row(g.bias_in[l]).broadcast_to([P, D]))
            load(g.ln_g[:, :], row(g.ln_g_in[l]).broadcast_to([P, D]))
            load(g.ln_b[:, :], row(g.ln_b_in[l]).broadcast_to([P, D]))
            load(g.w_edge[0:D, D:2 * D], g.W_e2[l])
            load(g.w_edge[D:D + 1, D:2 * D], row(g.b_e2[l]))
            load(g.w_edge[D:D + 1, 0:D], row(g.ba1[l]))
            load(g.w_edge[D + 1:D + 4, 0:D], g.Wa1[l, 2 * D:2 * D + 3, :])
            sp.wait_ge(split_w, 3)
            for part, rows in ((w_hi, (1, 2)), (w_hi, (4, 13)), (w_mid, (2, 3)), (w_mid, (13, 19)), (w_low, (3, 4)), (w_low, (19, 22))):
                sp.dma_start(g.w_e1_parts[rows[0]:rows[1], :], part[rows[0]:rows[1], :]).then_inc(placed, 16)
            sp.wait_ge(tab_sb, B)
            sp.dma_start(g.src_table[:, :].rearrange("(b p) c -> p b c", p=P), table[:, :, 0:2 * D]).then_inc(tab_out, 16)
            sp.wait_ge(tab_out, 16)
            sp.wait_ge(placed, 16 * 6)
            sp.wait_ge(landed, 16 * 12)

        @block.tensor
        def _(pe):
            for c, (m0, k) in enumerate(CH):
                if c >= 2:
                    pe.wait_ge(turned_sb, c - 1)
                for m in range(k):
                    mm = nc.tensor.transpose(t_ps[0:D, c % 2, m * P:(m + 1) * P], g.h[:, m0 + m, :], g.ident[:, :])
                mm.then_inc(turned, 1)
            pe.wait_ge(landed, 16 * 12)
            for c, (m0, k) in enumerate(CH):
                pe.wait_ge(turned_sb, c + 1)
                if c >= 2:
                    pe.wait_ge(hx_sb, c - 1)
                nc.tensor.matmul(x_ps[0:D, c % 2, 0:k * P], g.w_node[:, :], h_t[:, m0 * P:(m0 + k) * P],
                                 start=True, stop=True).then_inc(hx, 1)
            for m in range(B):
                pe.wait_ge(hx_sb, m // 4 + 1)
                if m >= 2:
                    pe.wait_ge(tab_sb, m - 1)
                cols = slice(m * P, (m + 1) * P)
                nc.tensor.matmul(n_ps[:, m % 2, 0:2 * D], hx_t[:, cols], w_att[:, :], start=True, stop=True)
                nc.tensor.matmul(n_ps[:, m % 2, 2 * D:3 * D], h_t[:, cols], g.w_node[:, :], start=True, stop=True).then_inc(tab, 1)

        @block.vector
        def _(dve):
            steps = [0]

            def step(ins):
                steps[0] += 1
                ins.then_inc(own, 1)
                dve.wait_ge(own, steps[0])

            nc.vector.memset(g.w_e1[:, :], 0.0).then_inc(zeroed, 1)
            nc.vector.memset(g.sums_t[:, :, :], 0.0)
            nc.vector.memset(g.dst_parts[:, B, :, :], 0.0)
            nc.vector.memset(g.w_e1_parts[:, :], 0.0)
            for c, (m0, k) in enumerate(CH):
                dve.wait_ge(turned, c + 1)
                nc.vector.tensor_copy(h_t[:, m0 * P:(m0 + k) * P], t_ps[0:D, c % 2, 0:k * P]).then_inc(turned_sb, 1)
            dve.wait_ge(e1_landed, 16 * 9)
            nc.vector.tensor_copy(w_hi[:, :], g.w_e1[:, :]).then_inc(split_w, 1)
            dve.wait_ge(split_w, 1)
            step(nc.vector.tensor_tensor(w_left[:, :], g.w_e1[:, :], w_hi[:, :], ALU.subtract))
            nc.vector.tensor_copy(w_mid[:, :], w_left[:, :]).then_inc(split_w, 1)
            dve.wait_ge(split_w, 2)
            step(nc.vector.tensor_tensor(w_left[:, :], w_left[:, :], w_mid[:, :], ALU.subtract))
            nc.vector.tensor_copy(w_low[:, :], w_left[:, :]).then_inc(split_w, 1)
            for m in range(B):
                dve.wait_ge(tab, m + 1)
                nc.vector.tensor_copy(table[:, m, 0:D], n_ps[:, m % 2, 0:D])
                nc.vector.tensor_copy(table[:, m, 2 * D:3 * D], n_ps[:, m % 2, D:2 * D])
                nc.vector.tensor_copy(table[:, m, D:2 * D], n_ps[:, m % 2, 2 * D:3 * D]).then_inc(tab_sb, 1)
            dve.wait_ge(tab_sb, B)
            of_dst = table[:, :, 2 * D:3 * D]
            parts = [g.dst_parts[:, 0:B, k, :] for k in range(3)]
            step(nc.vector.tensor_copy(parts[0], of_dst))
            step(nc.vector.tensor_tensor(left[:, :, :], of_dst, parts[0], ALU.subtract))
            step(nc.vector.tensor_copy(parts[1], left[:, :, :]))
            step(nc.vector.tensor_tensor(left[:, :, :], left[:, :, :], parts[1], ALU.subtract))
            step(nc.vector.tensor_copy(parts[2], left[:, :, :]))

        @block.scalar
        def _(act):
            for c, (m0, k) in enumerate(CH):
                act.wait_ge(hx, c + 1)
                nc.scalar.copy(hx_t[:, m0 * P:(m0 + k) * P], x_ps[0:D, c % 2, 0:k * P]).then_inc(hx_sb, 1)


def edge_layer(nc, g, S, l):
    B, ND = S.blocks, S.dst_tiles
    H = 4
    K1 = S.split_used
    with ExitStack() as ctx:
        sb = lambda name, shape, dt=F32: ctx.enter_context(nc.sbuf_tensor(f"l{l}_{name}", shape, dt))
        sem = lambda name: ctx.enter_context(semaphore(nc, f"l{l}_{name}"))
        ps = lambda name, k: ctx.enter_context(nc.psum_tensor(f"l{l}_{name}", [P, k, 512], F32))
        split = sb("split", [K1, 2, H * P], BF16)
        hidden = sb("hidden", [D + 4, 2, H * P])
        index = sb("gather_index", [P, 4, H], U32)
        gathered = sb("gathered", [P, 4, H, 2 * D])
        node_hot = sb("node_hot", [P, 2, H * P], BF16)
        edge_hot = sb("edge_hot", [P, 2, H, P])
        edge = sb("edge", [P, 2, H, 2 * D])
        scored = sb("scored", [P, 2, H, D])
        logit = sb("logit", [P, 2, H])
        att = sb("attention", [P, 2, H])
        msg = sb("message", [P, 2, H, D])
        spread_ps = ps("spread_ps", 1)
        hidden_ps = ps("hidden_ps", 1)
        edge_ps = ps("edge_ps", 2)
        sum_ps = ps("sum_ps", 2)
        landed = [sem("even_rows_landed"), sem("odd_rows_landed")]
        gather_done = g.gather_done[l]
        indexed = sem("gather_index_ready")
        begun = sem("gather_begun")
        spread_done = sem("spread_done")
        x_done = sem("x_done")
        hot_done = sem("node_hot_done")
        relu_done = sem("hidden_done")
        y_done = sem("y_done")
        edge_done = sem("edge_sums_done")
        weighed = sem("scores_weighed")
        scored_done = sem("scored_done")
        att_done = sem("attention_done")
        msg_done = sem("message_done")
        edge_hot_done = sem("edge_hot_done")
        z_done = sem("z_done")
        added = sem("sums_added")
        block = ctx.enter_context(nc.Block())
        N = ND // H
        assert N % 2 == 0

        @block.sync
        def _(sp):
            def half(n, h):
                since(sp, x_done, n - 1)
                since(sp, y_done, n - 1)
                cols = bass.ds(n * (H * P), H * P)
                sp.dma_start(split[:, h, :], g.split_rows[0:K1, cols]).then_inc(landed[h], 16)
                sp.dma_start(hidden[D:D + 4, h, :], g.attr_rows[3:7, cols]).then_inc(landed[h], 16)

            def pair(i):
                half(i * 2, 0)
                half(i * 2 + 1, 1)

            rounds(sp, N // 2, pair)

        @block.gpsimd
        def _(pool):
            def gather(n, r):
                since(pool, edge_done, n - 3)
                nc.gpsimd.tensor_copy(index[:, r, :], g.src_node[:, bass.ds(n * H, H)]).then_inc(indexed, 1)
                pool.wait_ge(indexed, n + 1)
                pool.sem_inc(begun, 1)
                for j in range(H):
                    nc.gpsimd.indirect_dma_start(
                        out=gathered[:, r, j, :], out_offset=None, in_=g.src_table[:, :],
                        in_offset=bass.IndirectOffsetOnAxis(ap=index[:, r, j:j + 1], axis=0),
                    ).then_inc(gather_done[r], 16)

            def four(i):
                for r in range(4):
                    gather(i * 4 + r, r)

            rounds(pool, N // 4, four)
            for r in range(N % 4):
                gather(N // 4 * 4 + r, r)

        @block.tensor
        def _(pe):
            def x(n, h):
                pe.wait_ge(landed[h], (n - h) * 16 + 32)
                since(pe, hot_done, n)
                nc.tensor.matmul(spread_ps[:, 0, :], g.select[:, :], split[:, h, :], start=True, stop=True).then_inc(spread_done, 1)
                since(pe, relu_done, n)
                nc.tensor.matmul(hidden_ps[0:D, 0, :], g.w_e1_parts[:, :], split[:, h, :], start=True, stop=True).then_inc(x_done, 1)

            def y(n, h):
                blk = numbers(nc, mybir.EngineType.PE, g.dst_tab[0:1, bass.ds(n * H, H)], B)
                pe.wait_ge(hot_done, n + 1)
                pe.wait_ge(relu_done, n + 1)
                since(pe, edge_done, n - 1)
                for j in range(H):
                    cols = slice(j * P, (j + 1) * P)
                    att_cols = slice(j * P, j * P + D)
                    nc.tensor.matmul(edge_ps[:, h, cols], hidden[:, h, cols], g.w_edge[:, :], start=True, stop=False, skip_group_check=True)
                    for k in range(3):
                        mm = nc.tensor.matmul(edge_ps[:, h, att_cols], node_hot[:, h, cols],
                                              g.dst_parts[:, bass.ds(blk[j], 1), k, :].rearrange("p o d -> p (o d)"),
                                              start=False, stop=(k == 2), skip_group_check=True)
                mm.then_inc(y_done, 1)

            def z(n, h):
                pe.wait_ge(msg_done, n + 1)
                pe.wait_ge(edge_hot_done, n + 1)
                since(pe, added, (n - 1) * H)
                for j in range(H):
                    mm = nc.tensor.matmul(sum_ps[0:D, h, j * P:(j + 1) * P], msg[:, h, j, :], edge_hot[:, h, j, :],
                                          start=True, stop=True)
                mm.then_inc(z_done, 1)

            x(0, 0)
            x(1, 1)
            y(0, 0)
            x(2, 0)
            y(1, 1)
            z(0, 0)
            with pe.Fori(1, N // 2 - 1) as i:
                x(i * 2 + 1, 1)
                y(i * 2, 0)
                z(i * 2 - 1, 1)
                x(i * 2 + 2, 0)
                y(i * 2 + 1, 1)
                z(i * 2, 0)
            x(N - 1, 1)
            y(N - 2, 0)
            z(N - 3, 1)
            y(N - 1, 1)
            z(N - 2, 0)
            z(N - 1, 1)

        @block.scalar
        def _(act):
            def relu(n, h):
                act.wait_ge(x_done, n + 1)
                since(act, y_done, n - 1)
                nc.scalar.activation(hidden[0:D, h, :], hidden_ps[0:D, 0, :], ACT.Relu).then_inc(relu_done, 1)

            def message(n, h):
                act.wait_ge(scored_done, n + 1)
                since(act, msg_done, n - 1)
                nc.scalar.activation(att[:, h, :], logit[:, h, :], ACT.Sigmoid, bias=g.ba2[:, 0:1]).then_inc(att_done, 1)
                act.wait_ge(att_done, n + 1)
                since(act, z_done, n - 1)
                for j in range(H):
                    ins = nc.scalar.activation(msg[:, h, j, :], edge[:, h, j, D:2 * D], ACT.Copy, scale=att[:, h, j:j + 1])
                ins.then_inc(msg_done, 1)

            relu(0, 0)
            relu(1, 1)
            message(0, 0)

            def pair(i):
                relu(i * 2 + 2, 0)
                message(i * 2 + 1, 1)
                relu(i * 2 + 3, 1)
                message(i * 2 + 2, 0)

            rounds(act, N // 2 - 1, pair)
            message(N - 1, 1)

        @block.vector
        def _(dve):
            def hots(n, h):
                dve.wait_ge(spread_done, n + 1)
                since(dve, y_done, n - 1)
                nc.vector.tensor_scalar(node_hot[:, h, :], spread_ps[:, 0, :], g.iota_part[:, 0:1], None,
                                        ALU.is_equal).then_inc(hot_done, 1)

            def score(n, h, r, turn):
                since(dve, z_done, n - 1)
                nc.vector.tensor_tensor(edge_hot[:, h, :, :], g.iota_free[:, :].unsqueeze(1).broadcast_to([P, H, P]),
                                        g.dst_col[:, bass.ds(n * H, H)].unsqueeze(2).broadcast_to([P, H, P]),
                                        ALU.is_equal).then_inc(edge_hot_done, 1)
                dve.wait_ge(y_done, n + 1)
                dve.wait_ge(gather_done[r], turn * (16 * H) + 16 * H)
                since(dve, msg_done, n - 1)
                nc.vector.tensor_tensor(edge[:, h, :, :].rearrange("p j c -> p (j c)"), gathered[:, r, :, :].rearrange("p j c -> p (j c)"),
                                        edge_ps[:, h, :], ALU.add).then_inc(edge_done, 1)
                dve.wait_ge(edge_done, n + 1)
                nc.vector.scalar_tensor_tensor(out=scored[:, h, :, :], in0=edge[:, h, :, 0:D], scalar=0.0,
                                               in1=g.wa2[:, :].unsqueeze(1).broadcast_to([P, H, D]), op0=ALU.max, op1=ALU.mult).then_inc(weighed, 1)
                dve.wait_ge(weighed, n + 1)
                nc.vector.tensor_reduce(logit[:, h, :], scored[:, h, :, :], AX.X, ALU.add).then_inc(scored_done, 1)

            def add(n, h):
                blk = numbers(nc, mybir.EngineType.DVE, g.dst_tab[0:1, bass.ds(n * H, H)], B)
                dve.wait_ge(z_done, n + 1)
                for j in range(H):
                    since(dve, added, n * H + j)
                    to = node(g.sums_t, blk[j])
                    nc.vector.tensor_tensor(to, to, sum_ps[0:D, h, j * P:(j + 1) * P], ALU.add).then_inc(added, 1)

            hots(0, 0)
            hots(1, 1)
            score(0, 0, 0, 0)
            for n in (0, 1):
                hots(n + 2, n % 2)
                score(n + 1, (n + 1) % 2, n + 1, 0)
                add(n, n % 2)
            with dve.Fori(0, (N - 6) // 4) as i:
                for k in range(4):
                    n = i * 4 + (k + 2)
                    hots(n + 2, k % 2)
                    score(n + 1, (k + 1) % 2, (k + 3) % 4, i + (k + 3) // 4)
                    add(n, k % 2)
            m = (N - 6) // 4 * 4 + 2
            for n in range(m, N):
                if n + 2 < N:
                    hots(n + 2, n % 2)
                if n + 1 < N:
                    score(n + 1, (n + 1) % 2, (n + 1) % 4, (n + 1) // 4)
                add(n, n % 2)

    with ExitStack() as ctx:
        sem = lambda name: ctx.enter_context(semaphore(nc, f"l{l}_{name}"))
        back_ps = ctx.enter_context(nc.psum_tensor(f"l{l}_back_ps", [P, 4, 512], F32))
        turned = sem("sums_turned")
        block = ctx.enter_context(nc.Block())

        @block.tensor
        def _(pe):
            for m in range(B):
                nc.tensor.transpose(back_ps[:, m // 8, m % 8 * D:(m % 8 + 1) * D], g.sums_t[:, m, :], g.ident[0:D, 0:D]).then_inc(turned, 1)

        @block.vector
        def _(dve):
            for k in range(-(-B // 8)):
                m0, m1 = k * 8, min(B, k * 8 + 8)
                dve.wait_ge(turned, m1)
                nc.vector.tensor_copy(g.sums[:, m0:m1, :].rearrange("p b d -> p (b d)"), back_ps[:, k, 0:(m1 - m0) * D])


def attention_layers(nc, g, S):
    B, NT = S.blocks, S.tiles
    every = lambda row: row[:, :].unsqueeze(1).broadcast_to([P, B, D])
    with ExitStack() as ctx:
        sb = lambda name, shape, dt=F32: ctx.enter_context(nc.sbuf_tensor(name, shape, dt))
        g.dst_col = sb("dst_col", [P, S.dst_tiles])
        g.src_node = sb("src_node", [P, S.dst_tiles], U32)
        split_slots(nc, g, S)
        g.gather_done = [[nc.alloc_semaphore(name=f"l{l}_gathered_{r}") for r in range(4)] for l in range(S.layers)]
        g.h = sb("h", [P, B, D])
        g.dst_parts = sb("dst_parts", [P, B + 1, 3, D], BF16)
        g.sums_t = sb("sums_turned", [D, B + 1, P])
        g.sums = sb("sums", [P, B, D])
        normed = sb("normed", [P, B, D])
        g.w_node, g.w_ai, g.w_aj = (sb(n, [D, D]) for n in ("w_node", "w_ai", "w_aj"))
        g.w_edge = sb("w_edge", [D + 4, 2 * D])
        g.w_e1 = sb("w_e1", [S.split_used, D])
        g.w_e1_parts = sb("w_e1_parts", [S.split_used, D], BF16)
        g.wa2, g.bias, g.ln_g, g.ln_b = (sb(n, [P, D]) for n in ("wa2", "bias", "ln_g", "ln_b"))
        g.ba2 = sb("ba2", [P, 1])
        g.select = sb("select", [S.split_used, P], BF16)
        with nc.Block() as block:
            @block.vector
            def _(dve):
                nc.vector.tensor_copy(g.h[:, :, :], g.x[:, :, :])
                nc.vector.tensor_copy(g.select[:, :], g.ident[0:S.split_used, 0:1].broadcast_to([S.split_used, P]))
        for l in range(S.layers):
            node_tables(nc, g, S, l)
            edge_layer(nc, g, S, l)

            def add_bias(step):
                step(nc.vector.tensor_tensor(g.sums[:, :, :], g.sums[:, :, :], every(g.bias), ALU.add))

            def affine(step):
                step(nc.vector.tensor_tensor(normed[:, :, :], normed[:, :, :], every(g.ln_g), ALU.mult))
                step(nc.vector.tensor_tensor(normed[:, :, :], normed[:, :, :], every(g.ln_b), ALU.add))
                if l < S.layers - 1:
                    step(nc.vector.tensor_scalar(normed[:, :, :], normed[:, :, :], 0.0, None, ALU.max))
                step(nc.vector.tensor_tensor(g.h[:, :, :], g.h[:, :, :], normed[:, :, :], ALU.add))

            layer_norm(nc, g, S, f"l{l}_norm", g.sums, normed, add_bias, affine)

        def add_x(step):
            step(nc.vector.tensor_tensor(g.h[:, :, :], g.h[:, :, :], g.x[:, :, :], ALU.add))

        layer_norm(nc, g, S, "norm2", g.h, g.x, add_x)


def last_layer(nc, g, S):
    B = S.blocks
    K = 3
    with ExitStack() as ctx:
        sb = lambda name, shape, dt=F32: ctx.enter_context(nc.sbuf_tensor(name, shape, dt))
        w_inv2 = sb("w_inv_squared", [P, B])
        scaled = [sb("scaled_even", [P, B, D]), sb("scaled_odd", [P, B, D])]
        hop = [g.x] + [sb(f"hop_{k}", [P, B, D]) for k in (1, 2, 3)]
        with nc.Block() as block:
            @block.vector
            def _(dve):
                nc.vector.tensor_tensor(w_inv2[:, :], g.w_inv[:, :], g.w_inv[:, :], ALU.mult)
                nc.vector.tensor_tensor(scaled[0][:, :, :], g.x[:, :, :], spread(g.w_inv[:, :], D), ALU.mult)

        def finish(p, m, product):
            nc.vector.tensor_scalar(node(hop[p + 1], m), product, node_scale(g.w_inv, m), None, ALU.mult)
            return nc.vector.tensor_scalar(node(scaled[1 - p % 2], m), product, node_scale(w_inv2, m), None, ALU.mult)

        sweeps(nc, g, S, "normed", g.weights, 1, [(scaled[p % 2], scaled[1 - p % 2]) for p in range(K)], finish)
        with ExitStack() as ctx2:
            sem = lambda name: ctx2.enter_context(semaphore(nc, name))
            theta = ctx2.enter_context(nc.sbuf_tensor("theta", [D, 2, K, D], F32))
            hop_t = ctx2.enter_context(nc.sbuf_tensor("hop_turned", [D, 2, 4 * P], F32))
            z = scaled[0]
            t_ps = ctx2.enter_context(nc.psum_tensor("hop_turn_ps", [P, 2, 512], F32))
            o_ps = ctx2.enter_context(nc.psum_tensor("theta_ps", [P, 2, 512], F32))
            landed, turned, copied, done, read = (sem(n) for n in (
                "thetas_landed", "hops_turned", "hops_copied", "thetas_summed", "thetas_read"))
            block = ctx2.enter_context(nc.Block())

            @block.sync
            def _(sp):
                for w, src in ((0, g.theta_f), (1, g.theta_b)):
                    sp.dma_start(theta[:, w, :, :], src[:, :, :].rearrange("k i o -> i k o")).then_inc(landed, 16)

            terms = [(0, 0, 0), (1, 1, 0), (2, 0, 1), (1, 1, 1), (3, 0, 2), (2, 1, 2)]

            @block.tensor
            def _(pe):
                def turn(m):
                    if m >= 2:
                        pe.wait_ge(copied, m - 1)
                    for k in range(4):
                        mm = nc.tensor.transpose(t_ps[0:D, m % 2, k * P:(k + 1) * P], hop[k][:, m, :], g.ident[:, :])
                    mm.then_inc(turned, 1)

                turn(0)
                pe.wait_ge(landed, 32)
                for m in range(B):
                    if m + 1 < B:
                        turn(m + 1)
                    pe.wait_ge(copied, m + 1)
                    if m >= 2:
                        pe.wait_ge(read, m - 1)
                    for t, (k, w, i) in enumerate(terms):
                        mm = nc.tensor.matmul(o_ps[:, m % 2, 0:D], hop_t[:, m % 2, k * P:(k + 1) * P], theta[:, w, i, :],
                                              start=(t == 0), stop=(t == len(terms) - 1))
                    mm.then_inc(done, 1)

            @block.scalar
            def _(act):
                for m in range(B):
                    act.wait_ge(turned, m + 1)
                    if m >= 2:
                        act.wait_ge(done, m - 1)
                    nc.scalar.copy(hop_t[:, m % 2, :], t_ps[0:D, m % 2, :]).then_inc(copied, 1)

            @block.vector
            def _(dve):
                for m in range(B):
                    dve.wait_ge(done, m + 1)
                    nc.vector.tensor_tensor(z[:, m, :], o_ps[:, m % 2, 0:D], g.x[:, m, :], ALU.add).then_inc(read, 1)

        layer_norm(nc, g, S, "norm3", scaled[0], g.x)


def store_features(nc, g, S):
    full = (S.blocks - 1) * P
    with semaphore(nc, "out_stored") as stored, nc.Block() as block:
        @block.sync
        def _(sp):
            sp.dma_start(g.out[0:full, :].rearrange("(b p) d -> p b d", p=P), g.x[:, 0:S.blocks - 1, :]).then_inc(stored, 16)
            sp.dma_start(g.out[full:S.n, :], g.x[0:S.last_rows, S.blocks - 1, :]).then_inc(stored, 16)
            sp.wait_ge(stored, 32)


class Arrays:
    pass


def graph_network(nc, x, src, dst, edge_attr_3, edge_weight, L1_gnn_eps, L2_gnn_W_node, L2_gnn_W_e1, L2_gnn_b_e1,
                  L2_gnn_W_e2, L2_gnn_b_e2, L2_gnn_Wa1, L2_gnn_ba1, L2_gnn_Wa2, L2_gnn_ba2, L2_gnn_bias, L2_gnn_ln_g,
                  L2_gnn_ln_b, L3_gnn_theta_forward, L3_gnn_theta_backward, out):
    g = Arrays()
    g.x_in, g.eps1_in, g.out = x, L1_gnn_eps, out
    g.src, g.dst, g.w = src, dst, edge_weight
    g.ea = edge_attr_3.rearrange("e k -> (e k)")
    g.W_node, g.W_e1, g.b_e1, g.W_e2, g.b_e2 = L2_gnn_W_node, L2_gnn_W_e1, L2_gnn_b_e1, L2_gnn_W_e2, L2_gnn_b_e2
    g.Wa1, g.ba1, g.Wa2, g.ba2_in = L2_gnn_Wa1, L2_gnn_ba1, L2_gnn_Wa2, L2_gnn_ba2
    g.bias_in, g.ln_g_in, g.ln_b_in = L2_gnn_bias, L2_gnn_ln_g, L2_gnn_ln_b
    g.theta_f, g.theta_b = L3_gnn_theta_forward, L3_gnn_theta_backward
    S = Shapes(x.shape[0], src.shape[0])
    B, T, NT = S.blocks, S.in_tiles, S.tiles
    dram = lambda name, shape, dt=F32: nc.dram_tensor(name, shape, dt).ap()
    g.key_rows = dram("key_rows", [T, P])
    g.blk_rows = dram("blk_rows", [T, P])
    g.slots = dram("slots", [P * NT, S.rec])
    g.first_tiles = dram("first_tiles", [B * B + 1])
    g.counts = dram("counts", [(B + S.body) * P, (B + 1) * P])
    g.weights = dram("weights", [(B + S.body) * P, (B + 1) * P])
    g.dst_slots = dram("dst_slots", [P * S.dst_tiles, S.rec])
    g.dst_firsts = dram("dst_firsts", [B + 1])
    g.attr_rows = dram("attr_rows", [S.rec, S.dst_tiles * P])
    g.split_rows = dram("split_rows", [S.split, S.dst_tiles * P], BF16)
    g.src_table = dram("src_table", [B * P, 2 * D])
    g.bucket_of = dram("bucket_of", [-(-(NT + 2) // P) * P])
    with ExitStack() as ctx:
        sb = lambda name, shape, dt=F32: ctx.enter_context(nc.sbuf_tensor(name, shape, dt))
        g.ident = sb("ident", [P, P])
        g.iota_free = sb("iota_free", [P, P])
        g.iota_part = sb("iota_part", [P, 1])
        g.earlier = sb("earlier", [P, P])
        g.before = sb("before", [P, P])
        g.off_diagonal = sb("off_diagonal", [P, P])
        g.same = sb("same_bucket", [P, NT + 1])
        g.tab = sb("tab", [1, 4, NT], I32)
        g.dst_tab = sb("dst_tab", [1, S.dst_tiles], I32)
        g.deg = sb("degrees", [P, B + 1, 3])
        constants(nc, g, S)
        with ExitStack() as ctx1:
            sb1 = lambda name, shape, dt=F32: ctx1.enter_context(nc.sbuf_tensor(name, shape, dt))
            g.rec = sb1("rec", [P, T, S.rec])
            g.src_blk = sb1("src_blk", [P, T])
            g.dst_blk = sb1("dst_blk", [P, T])
            g.key_col = sb1("key_col", [P, T])
            g.dst_index = sb1("dst_index", [P, T], U32)
            edges_in(nc, g, S)
            with ExitStack() as ctx2:
                g.src_hot = ctx2.enter_context(nc.sbuf_tensor("src_hot", [P, T, B], BF16))
                g.start = ctx2.enter_context(nc.sbuf_tensor("start", [B, T + 1, B], F32))
                g.shift = ctx2.enter_context(nc.sbuf_tensor("shift", [B, B], F32))
                count_buckets(nc, g, S)
                slot_edges(nc, g, S)
            tile_tables(nc, g, S)
            g.recs = sb1("recs", [P, NT, S.rec])
            load_slots(nc, g, S)
            build_matrices(nc, g, S)
        g.x = sb("x", [P, B, D])
        g.w_inv = sb("w_inv", [P, B])
        load_features(nc, g, S)
        first_layers(nc, g, S)
        attention_layers(nc, g, S)
        last_layer(nc, g, S)
        store_features(nc, g, S)


_INS = ["x", "src", "dst", "edge_attr_3", "edge_weight", "L1_gnn_eps", "L2_gnn_W_node", "L2_gnn_W_e1", "L2_gnn_b_e1",
        "L2_gnn_W_e2", "L2_gnn_b_e2", "L2_gnn_Wa1", "L2_gnn_ba1", "L2_gnn_Wa2", "L2_gnn_ba2", "L2_gnn_bias", "L2_gnn_ln_g",
        "L2_gnn_ln_b", "L3_gnn_theta_forward", "L3_gnn_theta_backward"]


def kernel(**inputs):
    import numpy as _np
    import concourse.bacc as _bacc
    from concourse.bass_utils import run_bass_kernel_spmd as _run

    nc = _bacc.Bacc("TRN2", target_bir_lowering=False, num_devices=1)
    arrays, args = {}, []
    for name in _INS:
        a = _np.ascontiguousarray(inputs[name])
        arrays[f"in_{name}_dram"] = a
        args.append(nc.dram_tensor(f"in_{name}_dram", a.shape, mybir.dt.from_np(a.dtype), kind="ExternalInput").ap())
    shape = inputs["x"].shape
    args.append(nc.dram_tensor("out_0_dram", shape, F32, kind="ExternalOutput").ap())
    graph_network(nc, *args)
    r = _run(nc, [arrays], core_ids=[0])
    return r.results[0]["out_0_dram"]
```

```python
from contextlib import ExitStack, contextmanager

import concourse.bass as bass
from concourse import mybir

ALU = mybir.AluOpType
ACT = mybir.ActivationFunctionType
AX = mybir.AxisListType
F32 = mybir.dt.float32
BF16 = mybir.dt.bfloat16
I32 = mybir.dt.int32
U32 = mybir.dt.uint32

P = 128
D = 64


@contextmanager
def semaphore(nc, name):
    handle = nc.alloc_semaphore(name=name)
    yield handle
    nc.gpsimd.sem_clear(handle)
    nc.release_semaphore(handle)


def since(engine, sem, value):
    if not isinstance(value, int) or value > 0:
        engine.wait_ge(sem, value)


def rounds(engine, count, body, ahead=1):
    for i in range(ahead):
        body(i)
    with engine.Fori(ahead, count) as i:
        body(i)


class Shapes:

    def __init__(self, n_nodes, n_edges):
        self.n = n_nodes
        self.e = n_edges
        self.blocks = -(-n_nodes // P)
        self.last_rows = n_nodes - (self.blocks - 1) * P
        self.in_tiles = -(-n_edges // P)
        self.groups = 4
        self.group_rows = -(-self.in_tiles // self.groups)
        self.last_edges = n_edges - (self.in_tiles - 1) * P
        assert self.groups * self.group_rows == self.in_tiles and self.last_edges < P
        self.buckets = self.blocks * self.blocks
        self.body = 8
        tiles = n_edges // P + self.buckets
        self.tiles = -(-tiles // self.body) * self.body
        self.rec = 8
        self.dst_tiles = n_edges // P + self.blocks
        assert self.dst_tiles % self.body == 0
        self.split = 32
        self.split_used = 22
        self.ring = 5
        assert self.blocks % self.ring == 0
        self.hops = 10
        self.layers = 3
        self.keep = 0.9
        self.eps = 1e-5
        self.rank_half = 13
        assert self.in_tiles % (4 * self.rank_half) == 0
        self.div_mul, self.div_shift = 1311, 15
        assert all(q * self.div_mul >> self.div_shift == q // self.blocks for q in range(self.buckets + 1))


def edges_in(nc, g, S):
    R, NG, B = S.group_rows, S.groups, S.blocks
    with ExitStack() as ctx:
        sb = lambda name, shape, dt: ctx.enter_context(nc.sbuf_tensor(name, shape, dt))
        sem = lambda name: ctx.enter_context(semaphore(nc, name))
        ends = [sb("src_rows", [R, NG, P], I32), sb("dst_rows", [R, NG, P], I32)]
        w_rows = sb("w_rows", [R, NG, P], F32)
        ea_rows = sb("ea_rows", [R, NG, 3 * P], F32)
        blk_i = [sb("src_blk_i", [R, NG * P], I32), sb("dst_blk_i", [R, NG * P], I32)]
        loc_i = [sb("src_loc_i", [R, NG * P], I32), sb("dst_loc_i", [R, NG * P], I32)]
        blk_f = [sb("src_blk_f", [R, NG, P], F32), sb("dst_blk_f", [R, NG, P], F32)]
        loc_f = [sb("src_loc_f", [R, NG, P], F32), sb("dst_loc_f", [R, NG, P], F32)]
        key_f = sb("key_f", [R, NG, P], F32)
        src_f = sb("src_f", [R, NG, P], F32)
        fill = sb("fill", [P, S.tiles * S.rec], F32)
        turned = ctx.enter_context(nc.psum_tensor("turned", [P, 8, 512], F32))

        padded = sem("padded")
        s_in = sem("edges_landed")
        own = sem("split_steps")
        split = sem("rows_split")
        s_store = sem("rows_stored")
        s_turn = sem("field_turned")
        taken = sem("field_taken")
        filled = sem("fill_ready")

        block = ctx.enter_context(nc.Block())
        last = NG - 1
        full = S.last_edges

        @block.sync
        def _(sp):
            sp.wait_ge(padded, 4)
            for x, rows, k in ((g.src, ends[0], 1), (g.dst, ends[1], 1), (g.w, w_rows, 1), (g.ea, ea_rows, 3)):
                n = last * R * P * k
                sp.dma_start(rows[:, 0:last, :], x[0:n].rearrange("(j r e) -> r j e", j=last, r=R)).then_inc(s_in, 16)
                m = n + (R - 1) * P * k
                sp.dma_start(rows[0:R - 1, last, :], x[n:m].rearrange("(r e) -> r e", r=R - 1)).then_inc(s_in, 16)
                sp.dma_start(rows[R - 1:R, last, 0:full * k], x[m:m + full * k].rearrange("(r e) -> r e", r=1)).then_inc(s_in, 16)
            sp.wait_ge(split, 1)
            sp.dma_start(g.key_rows[:, :].rearrange("(j r) e -> r j e", j=NG), key_f[:, :, :]).then_inc(s_store, 16)
            sp.dma_start(g.blk_rows[:, :].rearrange("(j r) e -> r j e", j=NG), blk_f[1][:, :, :]).then_inc(s_store, 16)
            sp.wait_ge(filled, 1)
            sp.dma_start(g.slots[:, :].rearrange("(p t) f -> p (t f)", p=P), fill[:, :]).then_inc(s_store, 16)
            sp.dma_start(g.dst_slots[:, :].rearrange("(p t) f -> p (t f)", p=P),
                         fill[:, 0:S.dst_tiles * S.rec]).then_inc(s_store, 16)
            sp.wait_ge(s_store, 64)

        @block.gpsimd
        def _(pool):
            nc.gpsimd.memset(fill[:, :], -1.0).then_inc(filled, 1)

        @block.vector
        def _(dve):
            for rows in ends:
                nc.vector.memset(rows[:, last, :], -P).then_inc(padded, 1)
            for rows in (w_rows, ea_rows):
                nc.vector.memset(rows[:, last, :], 0.0).then_inc(padded, 1)
            nc.vector.memset(g.rec[:, :, 3:4], 1.0)
            dve.wait_ge(s_in, 16 * 12)
            for k in range(2):
                flat = ends[k][:, :, :].rearrange("r j e -> r (j e)")
                nc.vector.tensor_scalar(blk_i[k][:, :], flat, 7, None, ALU.arith_shift_right).then_inc(own, 1)
                nc.vector.tensor_scalar(loc_i[k][:, :], flat, P - 1, None, ALU.bitwise_and).then_inc(own, 1)
            dve.wait_ge(own, 4)
            nc.vector.tensor_copy(src_f[:, :, :], ends[0][:, :, :])
            for k in range(2):
                nc.vector.tensor_copy(blk_f[k][:, :, :].rearrange("r j e -> r (j e)"), blk_i[k][:, :]).then_inc(own, 1)
                nc.vector.tensor_copy(loc_f[k][:, :, :].rearrange("r j e -> r (j e)"), loc_i[k][:, :]).then_inc(own, 1)
            dve.wait_ge(own, 8)
            nc.vector.scalar_tensor_tensor(
                out=key_f[:, :, :].rearrange("r j e -> r (j e)"), in0=blk_f[1][:, :, :].rearrange("r j e -> r (j e)"),
                scalar=float(B), in1=blk_f[0][:, :, :].rearrange("r j e -> r (j e)"), op0=ALU.mult, op1=ALU.add,
            ).then_inc(split, 1)
            for f, out in enumerate((g.src_blk[:, :], g.dst_blk[:, :], g.rec[:, :, 0], g.rec[:, :, 1], g.rec[:, :, 2],
                                     g.rec[:, :, 4], g.rec[:, :, 5], g.rec[:, :, 6], g.rec[:, :, 7])):
                dve.wait_ge(s_turn, f + 1)
                nc.vector.tensor_copy(out, turned[:, f % 8, 0:S.in_tiles]).then_inc(taken, 1)

        @block.tensor
        def _(pe):
            pe.wait_ge(split, 1)
            fields = [blk_f[0][:, j, :] for j in range(NG)], [blk_f[1][:, j, :] for j in range(NG)], \
                [loc_f[0][:, j, :] for j in range(NG)], [loc_f[1][:, j, :] for j in range(NG)], \
                [w_rows[:, j, :] for j in range(NG)], \
                *[[ea_rows[:, j, k:3 * P:3] for j in range(NG)] for k in range(3)], [src_f[:, j, :] for j in range(NG)]
            for f, rows in enumerate(fields):
                if f >= 8:
                    pe.wait_ge(taken, f - 7)
                for j in range(NG):
                    mm = nc.tensor.transpose(turned[:, f % 8, j * R:(j + 1) * R], rows[j], g.ident[0:R, 0:R])
                mm.then_inc(s_turn, 1)


def constants(nc, g, S):
    with ExitStack() as ctx:
        made = ctx.enter_context(semaphore(nc, "constants_made"))
        block = ctx.enter_context(nc.Block())

        @block.gpsimd
        def _(pool):
            nc.gpsimd.iota(g.iota_free[:, :], pattern=[[1, P]], base=0, channel_multiplier=0,
                           allow_small_or_imprecise_dtypes=True).then_inc(made, 1)
            nc.gpsimd.iota(g.iota_part[:, :], pattern=[[0, 1]], base=0, channel_multiplier=1,
                           allow_small_or_imprecise_dtypes=True).then_inc(made, 1)

        @block.vector
        def _(dve):
            dve.wait_ge(made, 2)
            nc.vector.tensor_scalar(g.ident[:, :], g.iota_free[:, :], g.iota_part[:, 0:1], None, ALU.is_equal)
            nc.vector.tensor_scalar(g.off_diagonal[:, :], g.iota_free[:, :], g.iota_part[:, 0:1], None, ALU.not_equal)
            nc.vector.tensor_scalar(g.earlier[:, :], g.iota_free[:, :], g.iota_part[:, 0:1], None, ALU.is_lt)
            nc.vector.tensor_scalar(g.before[:, :], g.iota_free[:, :], g.iota_part[:, 0:1], None, ALU.is_gt)



def count_buckets(nc, g, S):
    B, T = S.blocks, S.in_tiles
    CH = S.rank_half
    NB = T // CH
    with ExitStack() as ctx:
        sb = lambda name, shape, dt: ctx.enter_context(nc.sbuf_tensor(name, shape, dt))
        sem = lambda name: ctx.enter_context(semaphore(nc, name))
        dst_hot = sb("dst_hot", [P, T, B], BF16)
        tile_counts = sb("tile_counts", [B, T, B], F32)
        ones = sb("ones_row", [B, T], F32)
        n_int = sb("n_int", [B, 2, B], I32)
        n_tiles = sb("n_tiles", [B, B], F32)
        upto = sb("tiles_upto", [B, B], F32)
        ahead = sb("tiles_ahead", [B, B], F32)
        first = sb("first_tile", [B, B], F32)
        end = sb("end_tile", [B, B], F32)
        first_slot = sb("first_slot", [B, B], F32)
        edges_upto = sb("edges_upto", [B, B], F32)
        edges_ahead = sb("edges_ahead", [B, B], F32)
        d_int = sb("dst_tiles_int", [B, 2], I32)
        d_tiles = sb("dst_tiles", [B, 1], F32)
        d_first = sb("dst_first", [B, 2], F32)
        d_slot = sb("dst_first_slot", [B, 1], F32)
        count_ps = ctx.enter_context(nc.psum_tensor("count_ps", [B, 2, 512], F32))
        base_ps = ctx.enter_context(nc.psum_tensor("base_ps", [B, 512], F32))
        hot = sem("one_hots")
        counted = sem("tiles_counted")
        copied = sem("counts_copied")
        own = sem("count_steps")
        upto_ready = sem("tiles_upto_ready")
        d_ready = sem("dst_tiles_ready")
        d_base = sem("dst_base_ready")
        d_first_ready = sem("dst_first_ready")
        base_ready = sem("row_base_ready")
        first_ready = sem("first_tile_ready")
        s_store = sem("first_tile_stored")
        block = ctx.enter_context(nc.Block())

        @block.tensor
        def _(pe):
            pe.wait_ge(hot, 2)
            for n in range(NB):
                if n >= 2:
                    pe.wait_ge(copied, n - 1)
                for j in range(CH):
                    c = n * CH + j
                    mm = nc.tensor.matmul(count_ps[:, n % 2, j * B:(j + 1) * B], dst_hot[:, c, :], g.src_hot[:, c, :],
                                          start=True, stop=True)
                mm.then_inc(counted, 1)
            pe.wait_ge(upto_ready, 1)
            nc.tensor.matmul(base_ps[:, 0:1], g.before[0:B, 0:B], upto[:, B - 1:B], start=True, stop=True).then_inc(base_ready, 1)
            pe.wait_ge(d_ready, 1)
            nc.tensor.matmul(base_ps[:, 1:2], g.before[0:B, 0:B], d_tiles[:, :], start=True, stop=True).then_inc(d_base, 1)

        @block.vector
        def _(dve):
            steps = [0]

            def step(ins):
                steps[0] += 1
                ins.then_inc(own, 1)
                dve.wait_ge(own, steps[0])

            io = g.iota_free[:, 0:B].unsqueeze(1).broadcast_to([P, T, B])
            for hots, blk in ((g.src_hot, g.src_blk), (dst_hot, g.dst_blk)):
                nc.vector.tensor_tensor(hots[:, :, :], blk[:, :].unsqueeze(2).broadcast_to([P, T, B]), io,
                                        ALU.is_equal).then_inc(hot, 1)
            step(nc.vector.memset(ones[:, :], 1.0))
            step(nc.vector.memset(g.start[:, 0, :], 0.0))
            nc.vector.scalar_tensor_tensor(out=g.key_col[:, :], in0=g.dst_blk[:, :], scalar=float(B), in1=g.src_blk[:, :],
                                           op0=ALU.mult, op1=ALU.add)
            for n in range(NB):
                dve.wait_ge(counted, n + 1)
                nc.vector.tensor_copy(tile_counts[:, n * CH:(n + 1) * CH, :].rearrange("b t a -> b (t a)"),
                                      count_ps[:, n % 2, 0:CH * B]).then_inc(copied, 1)
            dve.wait_ge(copied, NB)
            for a in range(B):
                scan = nc.vector.tensor_tensor_scan(g.start[:, 1:T + 1, a], ones[:, :], tile_counts[:, :, a], 0.0,
                                                    ALU.mult, ALU.add)
                scan.then_inc(own, 1)
            steps[0] += B
            dve.wait_ge(own, steps[0])
            step(nc.vector.tensor_scalar(n_int[:, 0, :], g.start[:, T, :], float(P - 1), None, ALU.add))
            step(nc.vector.tensor_scalar(n_int[:, 1, :], n_int[:, 0, :], 7, None, ALU.arith_shift_right))
            step(nc.vector.tensor_scalar(n_tiles[:, :], n_int[:, 1, :], 1.0, None, ALU.max))
            nc.vector.tensor_tensor_scan(upto[:, :], ones[:, 0:B], n_tiles[:, :], 0.0, ALU.mult, ALU.add).then_inc(upto_ready, 1)
            dve.wait_ge(upto_ready, 1)
            step(nc.vector.tensor_tensor(ahead[:, :], upto[:, :], n_tiles[:, :], ALU.subtract))
            dve.wait_ge(base_ready, 1)
            nc.vector.tensor_scalar(end[:, :], upto[:, :], base_ps[:, 0:1], None, ALU.add).then_inc(first_ready, 1)
            nc.vector.tensor_scalar(first[:, :], ahead[:, :], base_ps[:, 0:1], None, ALU.add).then_inc(first_ready, 1)
            dve.wait_ge(first_ready, 2)
            step(nc.vector.tensor_scalar(first_slot[:, :], first[:, :], float(P), None, ALU.mult))
            step(nc.vector.tensor_tensor_scan(edges_upto[:, :], ones[:, 0:B], g.start[:, T, :], 0.0, ALU.mult, ALU.add))
            step(nc.vector.tensor_tensor(edges_ahead[:, :], edges_upto[:, :], g.start[:, T, :], ALU.subtract))
            step(nc.vector.tensor_scalar(d_int[:, 0:1], edges_upto[:, B - 1:B], float(P - 1), None, ALU.add))
            step(nc.vector.tensor_scalar(d_int[:, 1:2], d_int[:, 0:1], 7, None, ALU.arith_shift_right))
            nc.vector.tensor_copy(d_tiles[:, :], d_int[:, 1:2]).then_inc(d_ready, 1)
            dve.wait_ge(d_base, 1)
            nc.vector.tensor_copy(d_first[:, 0:1], base_ps[:, 1:2]).then_inc(d_first_ready, 1)
            nc.vector.tensor_tensor(d_first[:, 1:2], d_tiles[:, :], base_ps[:, 1:2], ALU.add).then_inc(d_first_ready, 1)
            dve.wait_ge(d_first_ready, 2)
            step(nc.vector.tensor_scalar(d_slot[:, :], d_first[:, 0:1], float(P), None, ALU.mult))
            step(nc.vector.tensor_tensor(edges_ahead[:, :], edges_ahead[:, :], first_slot[:, :], ALU.subtract))
            step(nc.vector.tensor_scalar(g.shift[:, :], edges_ahead[:, :], d_slot[:, 0:1], None, ALU.add))
            nc.vector.tensor_tensor(g.start[:, 0:T, :], g.start[:, 0:T, :],
                                    first_slot[:, :].unsqueeze(1).broadcast_to([B, T, B]), ALU.add)

        @block.sync
        def _(sp):
            sp.wait_ge(first_ready, 2)
            sp.dma_start(g.first_tiles[0:B * B].rearrange("(b a) -> b a", b=B), first[:, :]).then_inc(s_store, 16)
            sp.dma_start(g.first_tiles[B * B:B * B + 1].rearrange("(b a) -> b a", b=1), end[B - 1:B, B - 1:B]).then_inc(s_store, 16)
            sp.wait_ge(d_first_ready, 2)
            with nc.allow_non_contiguous_dma("one number per block"):
                sp.dma_start(g.dst_firsts[0:B].rearrange("(b a) -> b a", a=1), d_first[:, 0:1]).then_inc(s_store, 16)
            sp.dma_start(g.dst_firsts[B:B + 1].rearrange("(b a) -> b a", a=1), d_first[B - 1:B, 1:2]).then_inc(s_store, 16)
            sp.wait_ge(s_store, 64)


def tile_tables(nc, g, S):
    B, NT, ND = S.blocks, S.tiles, S.dst_tiles
    NC = -(-(NT + 2) // P)
    with ExitStack() as ctx:
        sb = lambda name, shape, dt: ctx.enter_context(nc.sbuf_tensor(name, shape, dt))
        sem = lambda name: ctx.enter_context(semaphore(nc, name))
        firsts = sb("firsts", [P, B * B + 1], F32)
        le = sb("begun", [P, B * B + 1], F32)
        num = sb("tile_num", [P, NC], F32)
        cnt = sb("buckets_begun", [P, NC], F32)
        bucket = sb("bucket_row", [P, NC * P], F32)
        d_firsts = sb("dst_firsts_sb", [1, B + 1], F32)
        d_num = sb("dst_tile_num", [1, ND], F32)
        d_begun = sb("dst_begun", [1, ND, B + 1], F32)
        d_cnt = sb("dst_cnt", [1, ND], F32)
        blk_i = sb("tile_blk_i", [P, 2, NC], I32)
        q_f = sb("q_f", [1, 2, NT], F32)
        landed = sem("firsts_landed")
        numbered = sem("tiles_numbered")
        own = sem("table_steps")
        cnt_ready = sem("buckets_found")
        bucket_back = sem("bucket_row_landed")
        turned = sem("bucket_row_stored")
        block = ctx.enter_context(nc.Block())

        @block.gpsimd
        def _(pool):
            nc.gpsimd.iota(num[:, :], pattern=[[P, NC]], base=0, channel_multiplier=1,
                           allow_small_or_imprecise_dtypes=True).then_inc(numbered, 1)
            nc.gpsimd.iota(d_num[:, :], pattern=[[1, ND]], base=0, channel_multiplier=0,
                           allow_small_or_imprecise_dtypes=True).then_inc(numbered, 1)

        @block.sync
        def _(sp):
            sp.dma_start(firsts[:, :], g.first_tiles[:].unsqueeze(0).broadcast_to([P, B * B + 1])).then_inc(landed, 16)
            sp.dma_start(d_firsts[:, :], g.dst_firsts[:].unsqueeze(0)).then_inc(landed, 16)
            sp.wait_ge(cnt_ready, 1)
            with nc.allow_non_contiguous_dma("one number per tile"):
                sp.dma_start(g.bucket_of[:].rearrange("(c p) -> p c", p=P), cnt[:, :]).then_inc(turned, 16)
            sp.wait_ge(turned, 16)
            sp.dma_start(bucket[:, :], g.bucket_of[:].unsqueeze(0).broadcast_to([P, NC * P])).then_inc(bucket_back, 16)

        @block.vector
        def _(dve):
            steps = [0]

            def step(ins):
                steps[0] += 1
                ins.then_inc(own, 1)
                dve.wait_ge(own, steps[0])

            dve.wait_ge(landed, 32)
            dve.wait_ge(numbered, 2)
            for c in range(NC):
                ins = nc.vector.tensor_scalar(le[:, :], firsts[:, :], num[:, c:c + 1], 0.0, ALU.is_le, ALU.add,
                                              accum_out=cnt[:, c:c + 1])
                if c < NC - 1:
                    step(ins)
            ins.then_inc(cnt_ready, 1)
            dve.wait_ge(cnt_ready, 1)
            src_blk, dst_blk = g.tile_blk[:, 0, :], g.tile_blk[:, 1, :]
            step(nc.vector.tensor_scalar(src_blk, cnt[:, :], -1.0, None, ALU.add))
            step(nc.vector.tensor_scalar(blk_i[:, 0, :], src_blk, float(S.div_mul), None, ALU.mult))
            step(nc.vector.tensor_scalar(blk_i[:, 1, :], blk_i[:, 0, :], S.div_shift, None, ALU.arith_shift_right))
            step(nc.vector.tensor_copy(dst_blk, blk_i[:, 1, :]))
            step(nc.vector.scalar_tensor_tensor(out=src_blk, in0=dst_blk, scalar=-float(B), in1=src_blk, op0=ALU.mult, op1=ALU.add))
            step(nc.vector.tensor_tensor(d_begun[:, :, :], d_firsts[:, :].unsqueeze(1).broadcast_to([1, ND, B + 1]),
                                         d_num[:, :].unsqueeze(2).broadcast_to([1, ND, B + 1]), ALU.is_le))
            step(nc.vector.tensor_reduce(d_cnt[:, :], d_begun[:, :, :], AX.X, ALU.add))
            step(nc.vector.tensor_scalar(g.dst_tab[:, :], d_cnt[:, :], -1.0, None, ALU.add))
            dve.wait_ge(bucket_back, 16)
            step(nc.vector.memset(g.same[:, :], 0.0))
            step(nc.vector.tensor_tensor(g.same[:, 1:NT + 1], bucket[:, 1:NT + 1], bucket[:, 0:NT], ALU.is_equal))
            q, spare = q_f[:, 0, :], q_f[:, 1, :]
            step(nc.vector.tensor_scalar(q, bucket[0:1, 0:NT], -1.0, None, ALU.add))
            step(nc.vector.tensor_copy(spare.rearrange("o (n s) -> o n s", s=S.body),
                                       g.iota_free[0:1, 0:S.body].unsqueeze(1).broadcast_to([1, NT // S.body, S.body])))
            step(nc.vector.tensor_scalar(spare, spare, float(B * B + 1), None, ALU.add))
            step(nc.vector.tensor_tensor(spare, spare, q, ALU.subtract))
            step(nc.vector.tensor_tensor(spare, spare, g.same[0:1, 1:NT + 1], ALU.mult))
            step(nc.vector.tensor_tensor(g.tab[:, :], q, spare, ALU.add))


def slot_edges(nc, g, S):
    B, T, CH = S.blocks, S.in_tiles, S.rank_half
    C2 = 2 * CH
    NCH = T // C2
    with ExitStack() as ctx:
        sb = lambda name, shape, dt: ctx.enter_context(nc.sbuf_tensor(name, shape, dt))
        sem = lambda name: ctx.enter_context(semaphore(nc, name))
        keys = sb("keys_spread", [P, 2, C2 * P], F32)
        blks = sb("blks_spread", [B, 2, C2 * P], F32)
        hot_t = sb("dst_hot_turned", [B, 2, C2 * P], F32)
        start_ring = sb("start_ring", [B, 2, C2 * B], F32)
        rec_ring = sb("rec_ring", [P, 2, C2, S.rec], F32)
        picked = sb("picked", [P, C2, B], F32)
        base = sb("base_slot", [P, C2], F32)
        shifted = sb("shifted", [P, C2, B], F32)
        shift = sb("shift_of_edge", [P, C2], F32)
        rank = sb("rank_in_tile", [P, C2], F32)
        off = sb("no_edge", [P, C2], F32)
        slot_i = sb("slot_i", [P, 3, C2], I32)
        dslot_i = sb("dst_slot_i", [P, 3, C2], I32)
        drow_f = sb("dst_row_f", [P, C2], F32)
        row_f = sb("row_f", [P, C2], F32)
        index = sb("slot_index", [P, 2, C2], U32)
        look_ps = ctx.enter_context(nc.psum_tensor("look_ps", [P, 4, 512], F32))
        shift_ps = ctx.enter_context(nc.psum_tensor("shift_ps", [P, 4, 512], F32))
        spread_free = sem("spread_free")
        landed = [sem("even_chunk_landed"), sem("odd_chunk_landed")]
        hot_ready = sem("turned_hot_ready")
        looked = sem("bases_looked_up")
        look_free = sem("look_ps_free")
        own = sem("slot_steps")
        ring_free = sem("record_ring_free")
        indexed = sem("slots_indexed")
        sent = nc.alloc_semaphore(name="records_sent")
        g.sent = nc.alloc_semaphore(name="records_sent_by_dst")
        block = ctx.enter_context(nc.Block())
        NS = 12
        no_slot = float(4 * S.tiles * P)

        @block.sync
        def _(sp):
            with sp.Fori(0, NCH // 2) as i:
                for h in range(2):
                    q = i * 2 + h
                    sp.wait_ge(spread_free, q + 1)
                    rows = bass.ds(q * C2, C2)
                    sp.dma_start(keys[:, h, :], g.key_rows[rows, :].rearrange("t e -> (t e)").unsqueeze(0).broadcast_to([P, C2 * P])).then_inc(landed[h], 16)
                    sp.dma_start(blks[:, h, :], g.blk_rows[rows, :].rearrange("t e -> (t e)").unsqueeze(0).broadcast_to([B, C2 * P])).then_inc(landed[h], 16)

        @block.tensor
        def _(pe):
            with pe.Fori(0, NCH // 2) as i:
                for h in range(2):
                    q = i * 2 + h
                    pe.wait_ge(hot_ready, 2 * q + 2)
                    pe.wait_ge(look_free, q + 1)
                    for j in range(C2):
                        mm = nc.tensor.matmul(look_ps[:, 2 * h + j // CH, (j % CH) * B:(j % CH + 1) * B],
                                              hot_t[:, h, j * P:(j + 1) * P], start_ring[:, h, j * B:(j + 1) * B],
                                              start=True, stop=True)
                        mm = nc.tensor.matmul(shift_ps[:, 2 * h + j // CH, (j % CH) * B:(j % CH + 1) * B],
                                              hot_t[:, h, j * P:(j + 1) * P], g.shift[:, :], start=True, stop=True)
                    mm.then_inc(looked, 1)

        @block.vector
        def _(dve):
            dve.sem_inc(spread_free, 2)
            dve.sem_inc(look_free, 2)

            def pair(i):
                for h in range(2):
                    q = i * 2 + h
                    steps = [0]

                    def step(ins):
                        steps[0] += 1
                        ins.then_inc(own, 1)
                        dve.wait_ge(own, q * NS + steps[0])

                    cols = bass.ds(q * C2, C2)
                    dve.wait_ge(landed[h], i * 32 + 32)
                    nc.vector.tensor_scalar(hot_t[:, h, :], blks[:, h, :], g.iota_part[0:B, 0:1], None, ALU.is_equal).then_inc(hot_ready, 1)
                    nc.vector.tensor_copy(start_ring[:, h, :].rearrange("b (t a) -> b t a", a=B), g.start[:, cols, :]).then_inc(hot_ready, 1)
                    for j in range(C2):
                        ins = nc.vector.scalar_tensor_tensor(
                            out=keys[:, h, j * P:(j + 1) * P], in0=keys[:, h, j * P:(j + 1) * P], scalar=g.key_col[:, bass.ds(q * C2 + j, 1)],
                            in1=g.earlier[:, :], op0=ALU.is_equal, op1=ALU.mult, accum_out=rank[:, j:j + 1])
                    ins.then_inc(spread_free, 1)
                    dve.wait_ge(spread_free, q + 3)
                    dve.wait_ge(looked, q + 1)
                    for k in range(2):
                        hot = g.src_hot[:, bass.ds(q * C2 + k * CH, CH), :]
                        nc.vector.tensor_tensor(picked[:, k * CH:(k + 1) * CH, :],
                                                look_ps[:, 2 * h + k, 0:CH * B].rearrange("p (t a) -> p t a", a=B),
                                                hot, ALU.mult)
                        ins = nc.vector.tensor_tensor(shifted[:, k * CH:(k + 1) * CH, :],
                                                      shift_ps[:, 2 * h + k, 0:CH * B].rearrange("p (t a) -> p t a", a=B),
                                                      hot, ALU.mult)
                    ins.then_inc(look_free, 1)
                    dve.wait_ge(look_free, q + 3)
                    step(nc.vector.tensor_reduce(base[:, :], picked[:, :, :], AX.X, ALU.add))
                    step(nc.vector.tensor_tensor(slot_i[:, 0, :], base[:, :], rank[:, :], ALU.add))
                    step(nc.vector.tensor_scalar(slot_i[:, 1, :], slot_i[:, 0, :], 7, None, ALU.arith_shift_right))
                    step(nc.vector.tensor_scalar(slot_i[:, 2, :], slot_i[:, 0, :], P - 1, None, ALU.bitwise_and))
                    step(nc.vector.scalar_tensor_tensor(out=row_f[:, :], in0=slot_i[:, 2, :], scalar=float(S.tiles),
                                                        in1=slot_i[:, 1, :], op0=ALU.mult, op1=ALU.add))
                    step(nc.vector.tensor_scalar(off[:, :], g.key_col[:, cols], 0.0, no_slot, ALU.is_lt, ALU.mult))
                    step(nc.vector.tensor_reduce(shift[:, :], shifted[:, :, :], AX.X, ALU.add))
                    step(nc.vector.tensor_tensor(dslot_i[:, 0, :], slot_i[:, 0, :], shift[:, :], ALU.add))
                    step(nc.vector.tensor_scalar(dslot_i[:, 1, :], dslot_i[:, 0, :], 7, None, ALU.arith_shift_right))
                    step(nc.vector.tensor_scalar(dslot_i[:, 2, :], dslot_i[:, 0, :], P - 1, None, ALU.bitwise_and))
                    step(nc.vector.scalar_tensor_tensor(out=drow_f[:, :], in0=dslot_i[:, 2, :], scalar=float(S.dst_tiles),
                                                        in1=dslot_i[:, 1, :], op0=ALU.mult, op1=ALU.add))
                    nc.vector.tensor_tensor(g.dst_index[:, cols], drow_f[:, :], off[:, :], ALU.add)
                    since(dve, ring_free, q)
                    nc.vector.tensor_copy(rec_ring[:, h, :, :], g.rec[:, cols, :]).then_inc(indexed, 1)
                    step(nc.vector.tensor_tensor(index[:, h, :], row_f[:, :], off[:, :], ALU.add))
                    assert steps[0] == NS

            rounds(dve, NCH // 2, pair)

        @block.gpsimd
        def _(pool):
            last_row = pool.to_reg(S.tiles * P - 1)

            def pair(i):
                for h in range(2):
                    q = i * 2 + h
                    since(pool, sent, q * (16 * C2))
                    pool.wait_ge(indexed, q + 1)
                    pool.wait_ge(own, q * NS + NS)
                    pool.sem_inc(ring_free, 1)
                    for j in range(C2):
                        nc.gpsimd.indirect_dma_start(
                            out=g.slots[:, :], out_offset=bass.IndirectOffsetOnAxis(ap=index[:, h, j:j + 1], axis=0),
                            in_=rec_ring[:, h, j, :], in_offset=None, bounds_check=last_row, oob_is_err=False,
                        ).then_inc(sent, 16)

            rounds(pool, NCH // 2, pair)
            pool.wait_ge(sent, NCH * 16 * C2)


def load_slots(nc, g, S):
    with ExitStack() as ctx:
        landed = ctx.enter_context(semaphore(nc, "slots_landed"))
        block = ctx.enter_context(nc.Block())

        @block.sync
        def _(sp):
            sp.dma_start(g.recs[:, :, :].rearrange("p t f -> p (t f)"),
                         g.slots[:, :].rearrange("(p t) f -> p (t f)", p=P)).then_inc(landed, 16)
            sp.wait_ge(landed, 16)


def send_by_dst(nc, g, S, pool, C2, rec_stage, index_stage, sent, copied, begun):
    last_row = pool.to_reg(S.dst_tiles * P - 1)

    def chunk(i):
        since(pool, sent, i * (16 * C2))
        cols = bass.ds(i * C2, C2)
        nc.gpsimd.tensor_copy(rec_stage[:, :, :], g.rec[:, cols, :]).then_inc(copied, 1)
        nc.gpsimd.tensor_copy(index_stage[:, :], g.dst_index[:, cols]).then_inc(copied, 1)
        pool.wait_ge(copied, i * 2 + 2)
        pool.sem_inc(begun, 1)
        for j in range(C2):
            nc.gpsimd.indirect_dma_start(
                out=g.dst_slots[:, :], out_offset=bass.IndirectOffsetOnAxis(ap=index_stage[:, j:j + 1], axis=0),
                in_=rec_stage[:, j, :], in_offset=None, bounds_check=last_row, oob_is_err=False,
            ).then_inc(sent, 16)

    rounds(pool, S.in_tiles // C2, chunk)
    pool.wait_ge(sent, S.in_tiles * 16)


def numbers(nc, engine, ap, top):
    _, values = nc.values_load_multi_w_load_instructions(
        ap, engines=[engine], min_val=0, max_val=top,
        skip_runtime_bounds_check_because="stage 3 makes the row from counts of buckets, all of them in this range")
    return values


def build_matrices(nc, g, S):
    B, NT, U = S.blocks, S.tiles, S.body
    H = U // 2
    with ExitStack() as ctx:
        sb = lambda name, shape, dt=F32: ctx.enter_context(nc.sbuf_tensor(name, shape, dt))
        sem = lambda name: ctx.enter_context(semaphore(nc, name))
        src_hot = sb("src_hot_e", [P, U, P])
        dst_hot = sb("dst_hot_e", [P, U, P + 2])
        wsrc_hot = sb("wsrc_hot_e", [P, U, P + 1])
        done = sb("block_done", [P, U, 2, P])
        ps = ctx.enter_context(nc.psum_tensor("block_ps", [P, U, 512], F32))
        hot = sem("hots_ready")
        weighed = sem("weights_on_hot")
        mult = sem("blocks_multiplied")
        ready = sem("blocks_ready")
        summed = sem("sums_taken")
        zero = sem("sums_zeroed")
        out = [sem(f"block_out_{s}") for s in range(U)]
        C2 = 2 * S.rank_half
        rec_stage = sb("rec_stage", [P, C2, S.rec])
        index_stage = sb("index_stage", [P, C2], U32)
        copied = sem("records_staged")
        begun = sem("chunk_begun")
        block = ctx.enter_context(nc.Block())

        @block.gpsimd
        def _(pool):
            send_by_dst(nc, g, S, pool, C2, rec_stage, index_stage, g.sent, copied, begun)

        @block.vector
        def _(dve):
            nc.vector.memset(done[:, U - 1, :, :], 0.0).then_inc(zero, 1)
            nc.vector.memset(wsrc_hot[:, :, P:P + 1], 1.0).then_inc(zero, 1)
            dve.wait_ge(zero, 2)

            def make(i, h):
                four = slice(h * H, (h + 1) * H)
                tiles = bass.ds(i * U + h * H, H)
                rec = lambda f: g.recs[:, tiles, f].unsqueeze(2).broadcast_to([P, H, P])
                io = g.iota_free[:, :].unsqueeze(1).broadcast_to([P, H, P])
                since(dve, mult, (i - 1) * U + h * H + H)
                nc.vector.tensor_tensor(src_hot[:, four, :], io, rec(0), ALU.is_equal).then_inc(hot, 1)
                nc.vector.tensor_tensor(dst_hot[:, four, 0:P], io, rec(1), ALU.is_equal).then_inc(hot, 1)
                nc.vector.tensor_copy(dst_hot[:, four, P:P + 2], g.recs[:, tiles, 2:4]).then_inc(hot, 1)

            def take(i, h):
                for k in range(H):
                    s = h * H + k
                    n = i * U + s
                    dve.wait_ge(mult, n + 1)
                    since(dve, out[s], i * 16)
                    since(dve, ready, n)
                    both = ps[:, s, :].rearrange("p (t c) -> p t c", t=2)[:, :, 0:P]
                    nc.vector.scalar_tensor_tensor(out=done[:, s, :, :], in0=done[:, (s - 1) % U, :, :],
                                                   scalar=g.same[:, bass.ds(n, 1)], in1=both,
                                                   op0=ALU.mult, op1=ALU.add).then_inc(ready, 1)

            make(0, 0)

            def eight(i):
                make(i, 1)
                take(i, 0)
                make(i + 1, 0)
                take(i, 1)

            eight(0)
            with dve.Fori(1, NT // U - 1) as i:
                eight(i)
            make(NT // U - 1, 1)
            take(NT // U - 1, 0)
            take(NT // U - 1, 1)

        @block.scalar
        def _(act):
            def weigh(i, h):
                act.wait_ge(hot, i * 6 + h * 3 + 1)
                for k in range(H):
                    s = h * H + k
                    nc.scalar.activation(wsrc_hot[:, s, 0:P], src_hot[:, s, :], ACT.Copy,
                                         scale=g.recs[:, bass.ds(i * U + s, 1), 2]).then_inc(weighed, 1)

            def take_sums(i, h):
                act.wait_ge(ready, i * U + h * H + H)
                tiles = bass.ds(i * U + h * H, H)
                four = slice(h * H, (h + 1) * H)
                nc.scalar.copy(g.sums[:, 0:2, tiles], ps[:, four, P:P + 2].rearrange("p n c -> p c n")).then_inc(summed, 1)
                nc.scalar.copy(g.sums[:, 2, tiles], ps[:, four, 3 * P]).then_inc(summed, 1)

            def eight(i):
                weigh(i, 0)
                if not isinstance(i, int) or i > 0:
                    take_sums(i - 1, 1)
                weigh(i, 1)
                take_sums(i, 0)

            rounds(act, NT // U, eight)
            take_sums(NT // U - 1, 1)

        @block.tensor
        def _(pe):
            pe.wait_ge(zero, 2)

            def eight(i):
                for h in range(2):
                    pe.wait_ge(hot, i * 6 + h * 3 + 3)
                    since(pe, ready, (i - 1) * U + h * H + H)
                    since(pe, summed, (i - 1) * 4 + h * 2 + 2)
                    for s in range(h * H, (h + 1) * H):
                        n = i * U + s
                        nc.tensor.matmul(ps[:, s, 0:P + 2], src_hot[:, s, :], dst_hot[:, s, :], start=True, stop=True)
                        pe.wait_ge(weighed, n + 1)
                        nc.tensor.matmul(ps[:, s, 2 * P:3 * P + 1], dst_hot[:, s, 0:P], wsrc_hot[:, s, :],
                                         start=True, stop=True).then_inc(mult, 1)

            rounds(pe, NT // U, eight)

        @block.sync
        def _(sp):
            with sp.Fori(0, NT // U) as i:
                for h in range(2):
                    places = numbers(nc, mybir.EngineType.SP, g.tab[0:1, bass.ds(i * U + h * H, H)], B * B + U)
                    for k in range(H):
                        s = h * H + k
                        sp.wait_ge(ready, i * U + s + 1)
                        sp.dma_start(g.blocks[bass.ds(places[k] * P, P), :],
                                     done[:, s, :, :].rearrange("p k c -> p (k c)")).then_inc(out[s], 16)
            for s in range(U):
                sp.wait_ge(out[s], 16 * (NT // U))


def degrees(nc, g, S):
    B, NT = S.blocks, S.tiles
    NC = -(-NT // P)
    with ExitStack() as ctx:
        sb = lambda name, shape, dt=F32: ctx.enter_context(nc.sbuf_tensor(name, shape, dt))
        sem = lambda name: ctx.enter_context(semaphore(nc, name))
        hots = sb("tile_blk_hot", [P, 2, NC, B])
        by_tile = sb("sums_by_tile", [P, NC, 3, P])
        turn_ps = ctx.enter_context(nc.psum_tensor("sums_ps", [P, 4, 512], F32))
        deg_ps = ctx.enter_context(nc.psum_tensor("degrees_ps", [P, 3, 512], F32))
        turned = sem("sums_turned")
        kept = sem("sums_kept")
        added = sem("degrees_added")
        tiles = lambda c: min(P, NT - c * P)
        block = ctx.enter_context(nc.Block())

        @block.tensor
        def _(pe):
            for c in range(NC):
                n = tiles(c)
                since(pe, kept, c - 3)
                for k in range(3):
                    mm = nc.tensor.transpose(turn_ps[0:n, c % 4, k * P:(k + 1) * P], g.sums[:, k, c * P:c * P + n], g.ident[:, :])
                mm.then_inc(turned, 1)
            pe.wait_ge(kept, NC + 1)
            for k, end in ((0, 0), (1, 0), (2, 1)):
                for c in range(NC):
                    n = tiles(c)
                    mm = nc.tensor.matmul(deg_ps[:, k, 0:B], by_tile[0:n, c, k, :], hots[0:n, end, c, :],
                                          start=(c == 0), stop=(c == NC - 1))
            mm.then_inc(added, 1)

        @block.vector
        def _(dve):
            for c in range(NC):
                dve.wait_ge(turned, c + 1)
                n = tiles(c)
                nc.vector.tensor_copy(by_tile[0:n, c, :, :].rearrange("p k n -> p (k n)"), turn_ps[0:n, c % 4, 0:3 * P]).then_inc(kept, 1)
            nc.vector.tensor_tensor(hots[:, :, :, :], g.tile_blk[:, :, 0:NC].unsqueeze(3).broadcast_to([P, 2, NC, B]),
                                    g.iota_free[:, 0:B].unsqueeze(1).unsqueeze(1).broadcast_to([P, 2, NC, B]),
                                    ALU.is_equal).then_inc(kept, 1)
            dve.wait_ge(added, 1)
            nc.vector.tensor_copy(g.deg[:, :, :].rearrange("p b k -> p k b"), deg_ps[:, :, 0:B])


def load_features(nc, g, S):
    with ExitStack() as ctx:
        zero = ctx.enter_context(semaphore(nc, "x_zeroed"))
        landed = ctx.enter_context(semaphore(nc, "x_landed"))
        block = ctx.enter_context(nc.Block())
        full = (S.blocks - 1) * P

        @block.vector
        def _(dve):
            nc.vector.memset(g.x[:, S.blocks - 1, :], 0.0).then_inc(zero, 1)

        @block.sync
        def _(sp):
            sp.wait_ge(zero, 1)
            sp.dma_start(g.x[:, 0:S.blocks - 1, :], g.x_in[0:full, :].rearrange("(b p) d -> p b d", p=P)).then_inc(landed, 16)
            sp.dma_start(g.x[0:S.last_rows, S.blocks - 1, :], g.x_in[full:S.n, :]).then_inc(landed, 16)
            sp.wait_ge(landed, 32)


def spread(ap, n):
    return ap.unsqueeze(2).broadcast_to([ap.shape[0], ap.shape[1], n])


def degree_scales(nc, g, S):
    B = S.blocks
    with ExitStack() as ctx:
        sb = lambda name, shape, dt=F32: ctx.enter_context(nc.sbuf_tensor(name, shape, dt))
        sem = lambda name: ctx.enter_context(semaphore(nc, name))
        clipped = sb("clipped", [P, 3, B])
        root = sb("root", [P, 3, B])
        inv = sb("inverse_root", [P, 3, B])
        there = sb("has_weight", [P, B])
        own = sem("scale_steps")
        clip_ready = sem("clipped_ready")
        most = sb("most_of_place", [P, 1])
        most_ps = ctx.enter_context(nc.psum_tensor("most_ps", [P, 512], F32))
        most_ready = sem("most_ready")
        most_turned = sem("most_turned")
        root_ready = sem("roots_ready")
        block = ctx.enter_context(nc.Block())

        @block.scalar
        def _(act):
            act.wait_ge(clip_ready, 1)
            nc.scalar.activation(root[:, :, :], clipped[:, :, :], ACT.Sqrt).then_inc(root_ready, 1)

        @block.vector
        def _(dve):
            steps = [0]

            def step(ins):
                steps[0] += 1
                ins.then_inc(own, 1)
                dve.wait_ge(own, steps[0])

            step(nc.vector.tensor_scalar(clipped[:, 0, :], g.deg[:, 0:B, 1], 1.0, None, ALU.max))
            step(nc.vector.tensor_scalar(clipped[:, 1, :], g.deg[:, 0:B, 2], 1.0, None, ALU.max))
            step(nc.vector.tensor_scalar(there[:, :], g.deg[:, 0:B, 0], 0.0, None, ALU.is_gt))
            step(nc.vector.tensor_tensor(clipped[:, 2, :], g.deg[:, 0:B, 0], there[:, :], ALU.mult))
            step(nc.vector.scalar_tensor_tensor(out=clipped[:, 2, :], in0=clipped[:, 2, :], scalar=1.0, in1=there[:, :],
                                                op0=ALU.add, op1=ALU.subtract))
            clip = nc.vector.memset(inv[:, :, :], 0.0)
            clip.then_inc(clip_ready, 1)
            dve.wait_ge(root_ready, 1)
            step(nc.vector.reciprocal(inv[:, :, :], root[:, :, :]))
            step(nc.vector.tensor_tensor(g.w_inv[:, :], inv[:, 2, :], there[:, :], ALU.mult))
            step(nc.vector.tensor_scalar(g.hop_last[:, :], inv[:, 1, :], S.keep, None, ALU.mult))
            step(nc.vector.tensor_tensor(g.hop[:, :], g.hop_last[:, :], inv[:, 0, :], ALU.mult))
            step(nc.vector.tensor_tensor(g.hs[:, :, :], g.x[:, :, :], spread(inv[:, 0, :], D), ALU.mult))
            step(nc.vector.tensor_scalar(g.rest[:, :, :], g.hs[:, :, :], 1.0 - S.keep, None, ALU.mult))
            nc.vector.tensor_reduce(most[:, :], g.deg[:, 0:B, 1], AX.X, ALU.max).then_inc(most_ready, 1)
            dve.wait_ge(most_turned, 1)
            step(nc.vector.tensor_reduce(g.most[:, :], most_ps[0:1, 0:P], AX.X, ALU.max))

        @block.tensor
        def _(pe):
            pe.wait_ge(most_ready, 1)
            nc.tensor.transpose(most_ps[0:1, 0:P], most[:, :], g.ident[:, :]).then_inc(most_turned, 1)


def sweeps(nc, g, S, name, matrix, repeats, places, finish, clear_diagonal=False):
    B = S.blocks
    RING = S.ring
    with ExitStack() as ctx:
        sem = lambda n: ctx.enter_context(semaphore(nc, f"{name}_{n}"))
        rows = ctx.enter_context(nc.sbuf_tensor(f"{name}_rows", [P, RING, B * P], F32))
        prod = ctx.enter_context(nc.sbuf_tensor(f"{name}_product", [D, RING, P], F32))
        prod_ps = ctx.enter_context(nc.psum_tensor(f"{name}_product_ps", [D, RING, 512], F32))
        back_ps = ctx.enter_context(nc.psum_tensor(f"{name}_back_ps", [P, 3, 512], F32))
        prod_at = lambda s: prod_ps[:, s, 0:P]
        back_at = lambda s: back_ps[:, s % 3, 0:D]
        landed = [sem(f"row_landed_{s}") for s in range(RING)]
        free = sem("row_free")
        cleared = sem("diagonal_cleared")
        summed = sem("product_summed")
        copied = sem("product_copied")
        turned = sem("product_turned")
        begun = sem("turn_begun")
        block = ctx.enter_context(nc.Block())
        NP = len(places)

        @block.sync
        def _(sp):
            with sp.Fori(0, repeats) as r:
                for p in range(NP):
                    with sp.Fori(0, B // RING) as i:
                        for s in range(RING):
                            n = (r * NP + p) * B + i * RING + s
                            sp.wait_ge(free, n + 1)
                            row = matrix[bass.ds(i * RING + s, 1)].rearrange("o p b c -> (o p) b c")
                            sp.dma_start(rows[:, s, :].rearrange("p (b c) -> p b c", c=P), row).then_inc(landed[s], 16)

        @block.tensor
        def _(pe):
            def turn(n, s):
                pe.wait_ge(free, n + RING - 1)
                pe.wait_ge(copied, n + 1)
                pe.sem_inc(begun, 1)
                nc.tensor.transpose(back_at(s), prod[:, s, :], g.ident[0:D, 0:D]).then_inc(turned, 1)

            with pe.Fori(0, repeats) as r:
                for p in range(NP):
                    h = places[p][0]
                    with pe.Fori(0, B // RING) as i:
                        for s in range(RING):
                            n = (r * NP + p) * B + i * RING + s
                            pe.wait_ge(landed[s], (r * NP + p) * (16 * B // RING) + i * 16 + 16)
                            pe.wait_ge(free, n + 1)
                            if s == 0:
                                pe.wait_ge(free, (r * NP + p) * B + RING)
                            if clear_diagonal:
                                pe.wait_ge(cleared, n + 1)
                            for k in range(B):
                                mm = nc.tensor.matmul(prod_at(s), h[:, k, :], rows[:, s, k * P:(k + 1) * P],
                                                      start=(k == 0), stop=(k == B - 1))
                            mm.then_inc(summed, 1)
                            if s:
                                turn(n - 1, s - 1)
                        turn(n, s)

        @block.scalar
        def _(act):
            with act.Fori(0, repeats * NP * B // RING) as i:
                for s in range(RING):
                    act.wait_ge(summed, i * RING + s + 1)
                    nc.scalar.copy(prod[:, s, :], prod_at(s)).then_inc(copied, 1)

        @block.vector
        def _(dve):
            dve.sem_inc(free, RING)
            with dve.Fori(0, repeats) as r:
                for p in range(NP):
                    with dve.Fori(0, B // RING) as i:
                        def clear(s):
                            if clear_diagonal:
                                dve.wait_ge(landed[s], (r * NP + p) * (16 * B // RING) + i * 16 + 16)
                                own_block = rows[:, s, bass.ds((i * RING + s) * P, P)]
                                nc.vector.tensor_tensor(own_block, own_block, g.off_diagonal[:, :], ALU.mult).then_inc(cleared, 1)

                        clear(0)
                        for s in range(RING):
                            n = (r * NP + p) * B + i * RING + s
                            if s + 1 < RING:
                                clear(s + 1)
                            dve.wait_ge(turned, n + 1)
                            finish(p, i * RING + s, back_at(s)).then_inc(free, 1)


def node(ap, m):
    return ap[:, bass.ds(m, 1), :].rearrange("p o d -> p (o d)")


def node_scale(ap, m):
    return ap[:, bass.ds(m, 1)]


def hops_from_dram(nc, g, S):
    with ExitStack() as ctx:
        other = ctx.enter_context(nc.sbuf_tensor("hs_other", [P, S.blocks, D], F32))
        rest_last = ctx.enter_context(nc.sbuf_tensor("rest_last", [P, S.blocks, D], F32))
        hs = [g.hs, other]
        with nc.Block() as block:
            @block.vector
            def _(dve):
                nc.vector.tensor_scalar(rest_last[:, :, :], g.x[:, :, :], 1.0 - S.keep, None, ALU.mult)

        def even_odd(p, m, product):
            return nc.vector.scalar_tensor_tensor(out=node(hs[1 - p], m), in0=product, scalar=node_scale(g.hop, m),
                                                  in1=node(g.rest, m), op0=ALU.mult, op1=ALU.add)

        def last(p, m, product):
            if p == 0:
                return even_odd(p, m, product)
            return nc.vector.scalar_tensor_tensor(out=node(g.hs, m), in0=product, scalar=node_scale(g.hop_last, m),
                                                  in1=node(rest_last, m), op0=ALU.mult, op1=ALU.add)

        pairs = [(hs[0], hs[1]), (hs[1], hs[0])]
        sweeps(nc, g, S, "hop", g.counts, S.hops // 2 - 1, pairs, even_odd)
        sweeps(nc, g, S, "lasthop", g.counts, 1, pairs, last)


def hops_on_chip(nc, g, S):
    B, G = S.blocks, S.ring
    NG = B // G
    with ExitStack() as ctx:
        counts = ctx.enter_context(nc.sbuf_tensor("counts_on_chip", [P, B, B * P], BF16))
        half = B * P // 2
        with ExitStack() as ctx2:
            stage = ctx2.enter_context(nc.sbuf_tensor("counts_stage", [P, 2, B * P], F32))
            landed = [ctx2.enter_context(semaphore(nc, f"counts_landed_{s}")) for s in range(2)]
            by_act = ctx2.enter_context(semaphore(nc, "left_half_converted"))
            by_dve = ctx2.enter_context(semaphore(nc, "right_half_converted"))
            block = ctx2.enter_context(nc.Block())

            @block.sync
            def _(sp):
                for m in range(B):
                    since(sp, by_act, m - 1)
                    since(sp, by_dve, m - 1)
                    sp.dma_start(stage[:, m % 2, :].rearrange("p (b c) -> p b c", c=P), g.counts[m]).then_inc(landed[m % 2], 16)

            @block.scalar
            def _(act):
                for m in range(B):
                    act.wait_ge(landed[m % 2], m // 2 * 16 + 16)
                    nc.scalar.copy(counts[:, m, 0:half], stage[:, m % 2, 0:half]).then_inc(by_act, 1)

            @block.vector
            def _(dve):
                for m in range(B):
                    dve.wait_ge(landed[m % 2], m // 2 * 16 + 16)
                    nc.vector.tensor_copy(counts[:, m, half:], stage[:, m % 2, half:]).then_inc(by_dve, 1)

        sb = lambda n, shape, dt=F32: ctx.enter_context(nc.sbuf_tensor(n, shape, dt))
        sem = lambda n: ctx.enter_context(semaphore(nc, n))
        parts = [sb("parts_even", [P, B, 3, D], BF16), sb("parts_odd", [P, B, 3, D], BF16)]
        total = sb("hop_total", [P, G, D])
        left = sb("hop_left", [P, G, D])
        rest = sb("hop_rest", [P, G, D])
        ps = ctx.enter_context(nc.psum_tensor("hop_ps", [P, 8 * 512], F32))
        summed = sem("block_summed")
        read = sem("group_read")
        h_done = sem("group_split")
        own = sem("hop_steps")
        first = sem("first_split_steps")
        block = ctx.enter_context(nc.Block())

        def place(m):
            return slice(m * 256, m * 256 + 3 * D)

        @block.tensor
        def _(pe):
            with pe.Fori(0, S.hops // 2) as r:
                for p in range(2):
                    for q in range(NG):
                        n = (r * 2 + p) * NG + q
                        pe.wait_ge(read, n + 1)
                        for m in range(G):
                            for k in range(B):
                                if q == 0 and m == 0 and k % G == 0:
                                    pe.wait_ge(h_done, n + k // G + 1)
                                mm = nc.tensor.matmul(ps[:, place(m + (p + q) % 2 * 8)],
                                                      counts[:, q * G + m, k * P:(k + 1) * P],
                                                      parts[p][:, k, :, :].rearrange("p t d -> p (t d)"),
                                                      start=(k == 0), stop=(k == B - 1))
                            mm.then_inc(summed, 1)

        @block.vector
        def _(dve):
            NS = 6

            def split(value, to, step):
                step(nc.vector.tensor_copy(to[:, :, 0, :], value))
                step(nc.vector.tensor_tensor(left[:, :, :], value, to[:, :, 0, :], ALU.subtract))
                step(nc.vector.tensor_copy(to[:, :, 1, :], left[:, :, :]))
                step(nc.vector.tensor_tensor(left[:, :, :], left[:, :, :], to[:, :, 1, :], ALU.subtract))
                nc.vector.tensor_copy(to[:, :, 2, :], left[:, :, :]).then_inc(h_done, 1)

            steps = [0]

            def first_step(ins):
                steps[0] += 1
                ins.then_inc(first, 1)
                dve.wait_ge(first, steps[0])

            dve.sem_inc(read, 2)
            for q in range(NG):
                since(dve, h_done, q)
                split(g.hs[:, q * G:(q + 1) * G, :], parts[0][:, q * G:(q + 1) * G, :, :], first_step)

            def group(w, p, q, last=False):
                n = w * NG + q
                steps[0] = 0

                def step(ins):
                    steps[0] += 1
                    ins.then_inc(own, 1)
                    before = (S.hops - 1) * NG * NS + q * 2 if last else n * NS
                    dve.wait_ge(own, before + steps[0])

                blocks = slice(q * G, (q + 1) * G)
                dve.wait_ge(h_done, n + NG)
                dve.wait_ge(summed, n * G + G)
                places = ps[:, (p + q) % 2 * 2048:(p + q) % 2 * 2048 + G * 256].rearrange("p (m c) -> p m c", c=256)
                nc.vector.tensor_reduce(total[:, :, :], places[:, :, 0:3 * D].rearrange("p m (t d) -> p m d t", d=D),
                                        AX.X, ALU.add).then_inc(read, 1)
                dve.wait_ge(read, n + 3)
                scale = g.hop_last if last else g.hop
                step(nc.vector.tensor_tensor(total[:, :, :], total[:, :, :], spread(scale[:, blocks], D), ALU.mult))
                if last:
                    step(nc.vector.tensor_scalar(rest[:, :, :], g.x[:, blocks, :], 1.0 - S.keep, None, ALU.mult))
                    nc.vector.tensor_tensor(g.hs[:, blocks, :], total[:, :, :], rest[:, :, :], ALU.add).then_inc(h_done, 1)
                    return
                step(nc.vector.tensor_tensor(total[:, :, :], total[:, :, :], g.rest[:, blocks, :], ALU.add))
                split(total[:, :, :], parts[1 - p][:, blocks, :, :], step)

            def sweep(w, p, last=False):
                for q in range(NG):
                    group(w, p, q, last)

            def pair(r):
                sweep(r * 2, 0)
                sweep(r * 2 + 1, 1)

            rounds(dve, S.hops // 2 - 1, pair)
            sweep(S.hops - 2, 0)
            sweep(S.hops - 1, 1, last=True)


def enter_branch(nc):
    with semaphore(nc, "branch_entered") as entered, nc.Block() as block:
        @block.sync
        def _(sp):
            sp.sem_inc(entered, 1)

        @block.tensor
        def _(pe):
            pe.sem_inc(entered, 1)

        @block.scalar
        def _(act):
            act.sem_inc(entered, 1)

        @block.vector
        def _(dve):
            dve.sem_inc(entered, 1)

        @block.gpsimd
        def _(pool):
            pool.sem_inc(entered, 1)


def hops(nc, g, S):
    most = nc.values_load(g.most[0:1, 0:1], min_val=0, max_val=S.e,
                          skip_runtime_bounds_check_because="a count of edges")
    with nc.If(most > 256):
        enter_branch(nc)
        hops_from_dram(nc, g, S)
    with nc.Else():
        enter_branch(nc)
        hops_on_chip(nc, g, S)


def layer_norm(nc, g, S, name, z_in, out, before=None, after=None):
    B = S.blocks
    with ExitStack() as ctx:
        sb = lambda n, shape, dt=F32: ctx.enter_context(nc.sbuf_tensor(f"{name}_{n}", shape, dt))
        sem = lambda n: ctx.enter_context(semaphore(nc, f"{name}_{n}"))
        mean = sb("mean", [P, B])
        var = sb("var", [P, B])
        root = sb("root", [P, B])
        inv = sb("inv", [P, B])
        sq = sb("squares", [P, B, D])
        own = sem("steps")
        var_ready = sem("variance_ready")
        root_ready = sem("root_ready")
        block = ctx.enter_context(nc.Block())

        @block.scalar
        def _(act):
            act.wait_ge(var_ready, 1)
            nc.scalar.activation(root[:, :], var[:, :], ACT.Sqrt).then_inc(root_ready, 1)

        @block.vector
        def _(dve):
            steps = [0]

            def step(ins):
                steps[0] += 1
                ins.then_inc(own, 1)
                dve.wait_ge(own, steps[0])

            if before:
                before(step)
            step(nc.vector.tensor_reduce(mean[:, :], z_in[:, :, :], AX.X, ALU.add))
            step(nc.vector.tensor_scalar(mean[:, :], mean[:, :], 1.0 / D, None, ALU.mult))
            step(nc.vector.tensor_tensor(out[:, :, :], z_in[:, :, :], spread(mean[:, :], D), ALU.subtract))
            step(nc.vector.tensor_tensor(sq[:, :, :], out[:, :, :], out[:, :, :], ALU.mult))
            step(nc.vector.tensor_reduce(var[:, :], sq[:, :, :], AX.X, ALU.add))
            nc.vector.tensor_scalar(var[:, :], var[:, :], 1.0 / D, S.eps, ALU.mult, ALU.add).then_inc(var_ready, 1)
            dve.wait_ge(root_ready, 1)
            step(nc.vector.reciprocal(inv[:, :], root[:, :]))
            step(nc.vector.tensor_tensor(out[:, :, :], out[:, :, :], spread(inv[:, :], D), ALU.mult))
            if after:
                after(step)


def first_layers(nc, g, S):
    B = S.blocks
    with ExitStack() as ctx:
        sb = lambda name, shape, dt=F32: ctx.enter_context(nc.sbuf_tensor(name, shape, dt))
        g.rest = sb("rest", [P, B, D])
        g.hs = sb("hs", [P, B, D])
        g.hop = sb("hop", [P, B])
        g.hop_last = sb("hop_last", [P, B])
        g.most = sb("most", [1, 1], I32)
        eps1 = sb("one_plus_eps", [P, 1])
        degree_scales(nc, g, S)
        hops(nc, g, S)

        def add_x(step):
            step(nc.vector.tensor_tensor(g.hs[:, :, :], g.hs[:, :, :], g.x[:, :, :], ALU.add))

        layer_norm(nc, g, S, "norm0", g.hs, g.x, add_x)
        with semaphore(nc, "eps_landed") as landed, nc.Block() as block:
            @block.sync
            def _(sp):
                sp.dma_start(eps1[:, :], g.eps1_in[:].unsqueeze(0).broadcast_to([P, 1])).then_inc(landed, 16)

            @block.vector
            def _(dve):
                dve.wait_ge(landed, 16)
                nc.vector.tensor_scalar(eps1[:, :], eps1[:, :], 1.0, None, ALU.add)

        def neighbours(p, m, product):
            return nc.vector.scalar_tensor_tensor(out=node(g.hs, m), in0=node(g.x, m), scalar=eps1[:, 0:1],
                                                  in1=product, op0=ALU.mult, op1=ALU.add)

        sweeps(nc, g, S, "weighted", g.weights, 1, [(g.x, g.hs)], neighbours, clear_diagonal=True)
        layer_norm(nc, g, S, "norm1", g.hs, g.x, add_x)


def split_slots(nc, g, S):
    ND, R, F = S.dst_tiles, S.rec, S.split
    G = 4
    N = ND // G
    with ExitStack() as ctx:
        sb = lambda name, shape, dt=F32: ctx.enter_context(nc.sbuf_tensor(name, shape, dt))
        sem = lambda name: ctx.enter_context(semaphore(nc, name))
        recs = sb("dst_recs", [P, ND, R])
        left = sb("attr_left", [P, ND, 3])
        parts = sb("split_records", [P, ND, F], BF16)
        ident_b = sb("ident_b", [P, P], BF16)
        node_f = sb("src_node_f", [P, ND])
        taken = sb("records_taken", [P, 2, G * R])
        taken_b = sb("split_taken", [P, 2, G * F], BF16)
        out = sb("attr_turned", [G * R, 2, P])
        out_b = sb("split_turned", [G * F, 2, P], BF16)
        ps = ctx.enter_context(nc.psum_tensor("records_ps", [P, 2, 512], F32))
        ps_b = ctx.enter_context(nc.psum_tensor("split_ps", [P, 2, 1024], BF16))
        landed = sem("dst_records_landed")
        own = sem("split_steps")
        copied = sem("records_copied")
        tr = sem("records_transposed")
        ready = sem("turned_ready")
        ready_b = sem("split_turned_ready")
        stored = [sem("even_turned_stored"), sem("odd_turned_stored")]
        block = ctx.enter_context(nc.Block())

        @block.sync
        def _(sp):
            sp.dma_start(recs[:, :, :].rearrange("p t f -> p (t f)"),
                         g.dst_slots[:, :].rearrange("(p t) f -> p (t f)", p=P)).then_inc(landed, 16)

            def pair(i):
                for h in range(2):
                    n = i * 2 + h
                    sp.wait_ge(ready, n + 1)
                    sp.wait_ge(ready_b, n + 1)
                    cols = bass.ds(n * (G * P), G * P)
                    sp.dma_start(g.attr_rows[:, cols].rearrange("f (t e) -> t f e", e=P), out[:, h, :]).then_inc(stored[h], 16)
                    sp.dma_start(g.split_rows[:, cols].rearrange("f (t e) -> t f e", e=P), out_b[:, h, :]).then_inc(stored[h], 16)

            rounds(sp, N // 2, pair)
            for h in range(2):
                sp.wait_ge(stored[h], N // 2 * 32)

        @block.vector
        def _(dve):
            steps = [0]

            def step(ins):
                steps[0] += 1
                ins.then_inc(own, 1)
                dve.wait_ge(own, steps[0])

            step(nc.vector.memset(parts[:, :, :], 0.0))
            nc.vector.memset(parts[:, :, 1:4], 1.0)
            nc.vector.tensor_copy(ident_b[:, :], g.ident[:, :])
            dve.wait_ge(landed, 16)
            nc.vector.tensor_copy(parts[:, :, 0], recs[:, :, 1])
            nc.vector.tensor_copy(g.dst_col[:, :], recs[:, :, 1])
            step(nc.vector.tensor_scalar(node_f[:, :], recs[:, :, 7], 0.0, None, ALU.max))
            nc.vector.tensor_copy(g.src_node[:, :], node_f[:, :])
            hi, mid, low = parts[:, :, 4:7], parts[:, :, 7:10], parts[:, :, 10:13]
            step(nc.vector.tensor_copy(hi, recs[:, :, 4:7]))
            step(nc.vector.tensor_tensor(left[:, :, :], recs[:, :, 4:7], hi, ALU.subtract))
            step(nc.vector.tensor_copy(mid, left[:, :, :]))
            step(nc.vector.tensor_tensor(left[:, :, :], left[:, :, :], mid, ALU.subtract))
            nc.vector.tensor_copy(low, left[:, :, :])
            nc.vector.tensor_copy(parts[:, :, 13:19], parts[:, :, 4:10])
            step(nc.vector.tensor_copy(parts[:, :, 19:22], hi))

            def pair(i):
                for h in range(2):
                    n = i * 2 + h
                    since(dve, tr, n - 1)
                    tiles = bass.ds(n * G, G)
                    nc.vector.tensor_copy(taken[:, h, :].rearrange("p (t f) -> p t f", f=R), recs[:, tiles, :]).then_inc(copied, 1)
                    nc.vector.tensor_copy(taken_b[:, h, :].rearrange("p (t f) -> p t f", f=F), parts[:, tiles, :]).then_inc(copied, 1)
                    dve.wait_ge(tr, n + 1)
                    since(dve, stored[h], i * 32)
                    nc.vector.tensor_copy(out[:, h, :], ps[0:G * R, h, 0:P]).then_inc(ready, 1)
                    nc.vector.tensor_copy(out_b[:, h, :], ps_b[:, h, 0:P]).then_inc(ready_b, 1)

            rounds(dve, N // 2, pair)

        @block.tensor
        def _(pe):
            def pair(i):
                for h in range(2):
                    n = i * 2 + h
                    pe.wait_ge(copied, n * 2 + 2)
                    since(pe, ready_b, n - 1)
                    nc.tensor.transpose(ps[0:G * R, h, 0:P], taken[:, h, :], g.ident[:, :])
                    nc.tensor.transpose(ps_b[:, h, 0:P], taken_b[:, h, :], ident_b[:, :]).then_inc(tr, 1)

            rounds(pe, N // 2, pair)


def node_tables(nc, g, S, l):
    B = S.blocks
    CH = [(c, min(4, B - c)) for c in range(0, B, 4)]
    with ExitStack() as ctx:
        sb = lambda name, shape, dt=F32: ctx.enter_context(nc.sbuf_tensor(f"l{l}_{name}", shape, dt))
        sem = lambda name: ctx.enter_context(semaphore(nc, f"l{l}_{name}"))
        h_t = sb("h_turned", [D, B * P])
        hx_t = sb("hx_turned", [D, B * P])
        w_att = sb("w_attention", [D, 2 * D])
        table = sb("table", [P, B, 3 * D])
        left = sb("left", [P, B, D])
        w_left = sb("w_left", [S.split_used, D])
        w_hi = sb("w_hi", [S.split_used, D], BF16)
        w_mid = sb("w_mid", [S.split_used, D], BF16)
        w_low = sb("w_low", [S.split_used, D], BF16)
        ps = lambda name: ctx.enter_context(nc.psum_tensor(f"l{l}_{name}", [P, 2, 512], F32))
        t_ps, x_ps, n_ps = ps("turn_ps"), ps("hx_ps"), ps("table_ps")
        landed = sem("weights_landed")
        e1_landed = sem("edge_weights_landed")
        zeroed = sem("weights_zeroed")
        turned = sem("h_turned")
        turned_sb = sem("h_turned_copied")
        hx = sem("hx_ready")
        hx_sb = sem("hx_copied")
        tab = sem("table_ready")
        tab_sb = sem("table_copied")
        tab_out = sem("table_stored")
        own = sem("node_steps")
        split_w = sem("edge_weights_split")
        placed = sem("edge_weights_placed")
        block = ctx.enter_context(nc.Block())

        @block.gpsimd
        def _(pool):
            nc.gpsimd.memset(g.w_edge[:, :], 0.0).then_inc(zeroed, 1)

        @block.sync
        def _(sp):
            def load(out, src, s=landed):
                sp.dma_start(out, src).then_inc(s, 16)
            row = lambda v: v.unsqueeze(0)
            sp.wait_ge(zeroed, 2)
            for k in range(1, 4):
                load(g.w_e1[k:k + 1, :], row(g.b_e1[l]), e1_landed)
            for k in range(6):
                load(g.w_e1[4 + 3 * k:7 + 3 * k, :], g.W_e1[l], e1_landed)
            load(g.w_node[:, :], g.W_node[l])
            load(w_att[:, 0:D], g.Wa1[l, D:2 * D, :])
            load(w_att[:, D:2 * D], g.Wa1[l, 0:D, :])
            load(g.wa2[:, :], g.Wa2[l].rearrange("d o -> (d o)").unsqueeze(0).broadcast_to([P, D]))
            load(g.ba2[:, :], row(g.ba2_in[l]).broadcast_to([P, 1]))
            load(g.bias[:, :], row(g.bias_in[l]).broadcast_to([P, D]))
            load(g.ln_g[:, :], row(g.ln_g_in[l]).broadcast_to([P, D]))
            load(g.ln_b[:, :], row(g.ln_b_in[l]).broadcast_to([P, D]))
            load(g.w_edge[0:D, D:2 * D], g.W_e2[l])
            load(g.w_edge[D:D + 1, D:2 * D], row(g.b_e2[l]))
            load(g.w_edge[D:D + 1, 0:D], row(g.ba1[l]))
            load(g.w_edge[D + 1:D + 4, 0:D], g.Wa1[l, 2 * D:2 * D + 3, :])
            sp.wait_ge(split_w, 3)
            for part, rows in ((w_hi, (1, 2)), (w_hi, (4, 13)), (w_mid, (2, 3)), (w_mid, (13, 19)), (w_low, (3, 4)), (w_low, (19, 22))):
                sp.dma_start(g.w_e1_parts[rows[0]:rows[1], :], part[rows[0]:rows[1], :]).then_inc(placed, 16)
            sp.wait_ge(tab_sb, B)
            sp.dma_start(g.src_table[:, :].rearrange("(b p) c -> p b c", p=P), table[:, :, 0:2 * D]).then_inc(tab_out, 16)
            sp.wait_ge(tab_out, 16)
            sp.wait_ge(placed, 16 * 6)
            sp.wait_ge(landed, 16 * 12)

        @block.tensor
        def _(pe):
            for c, (m0, k) in enumerate(CH):
                if c >= 2:
                    pe.wait_ge(turned_sb, c - 1)
                for m in range(k):
                    mm = nc.tensor.transpose(t_ps[0:D, c % 2, m * P:(m + 1) * P], g.h[:, m0 + m, :], g.ident[:, :])
                mm.then_inc(turned, 1)
            pe.wait_ge(landed, 16 * 12)
            for c, (m0, k) in enumerate(CH):
                pe.wait_ge(turned_sb, c + 1)
                if c >= 2:
                    pe.wait_ge(hx_sb, c - 1)
                nc.tensor.matmul(x_ps[0:D, c % 2, 0:k * P], g.w_node[:, :], h_t[:, m0 * P:(m0 + k) * P],
                                 start=True, stop=True).then_inc(hx, 1)
            for m in range(B):
                pe.wait_ge(hx_sb, m // 4 + 1)
                if m >= 2:
                    pe.wait_ge(tab_sb, m - 1)
                cols = slice(m * P, (m + 1) * P)
                nc.tensor.matmul(n_ps[:, m % 2, 0:2 * D], hx_t[:, cols], w_att[:, :], start=True, stop=True)
                nc.tensor.matmul(n_ps[:, m % 2, 2 * D:3 * D], h_t[:, cols], g.w_node[:, :], start=True, stop=True).then_inc(tab, 1)

        @block.vector
        def _(dve):
            steps = [0]

            def step(ins):
                steps[0] += 1
                ins.then_inc(own, 1)
                dve.wait_ge(own, steps[0])

            nc.vector.memset(g.w_e1[:, :], 0.0).then_inc(zeroed, 1)
            nc.vector.memset(g.sums_t[:, :, :], 0.0)
            nc.vector.memset(g.dst_parts[:, B, :, :], 0.0)
            nc.vector.memset(g.w_e1_parts[:, :], 0.0)
            for c, (m0, k) in enumerate(CH):
                dve.wait_ge(turned, c + 1)
                nc.vector.tensor_copy(h_t[:, m0 * P:(m0 + k) * P], t_ps[0:D, c % 2, 0:k * P]).then_inc(turned_sb, 1)
            dve.wait_ge(e1_landed, 16 * 9)
            nc.vector.tensor_copy(w_hi[:, :], g.w_e1[:, :]).then_inc(split_w, 1)
            dve.wait_ge(split_w, 1)
            step(nc.vector.tensor_tensor(w_left[:, :], g.w_e1[:, :], w_hi[:, :], ALU.subtract))
            nc.vector.tensor_copy(w_mid[:, :], w_left[:, :]).then_inc(split_w, 1)
            dve.wait_ge(split_w, 2)
            step(nc.vector.tensor_tensor(w_left[:, :], w_left[:, :], w_mid[:, :], ALU.subtract))
            nc.vector.tensor_copy(w_low[:, :], w_left[:, :]).then_inc(split_w, 1)
            for m in range(B):
                dve.wait_ge(tab, m + 1)
                nc.vector.tensor_copy(table[:, m, 0:D], n_ps[:, m % 2, 0:D])
                nc.vector.tensor_copy(table[:, m, 2 * D:3 * D], n_ps[:, m % 2, D:2 * D])
                nc.vector.tensor_copy(table[:, m, D:2 * D], n_ps[:, m % 2, 2 * D:3 * D]).then_inc(tab_sb, 1)
            dve.wait_ge(tab_sb, B)
            of_dst = table[:, :, 2 * D:3 * D]
            parts = [g.dst_parts[:, 0:B, k, :] for k in range(3)]
            step(nc.vector.tensor_copy(parts[0], of_dst))
            step(nc.vector.tensor_tensor(left[:, :, :], of_dst, parts[0], ALU.subtract))
            step(nc.vector.tensor_copy(parts[1], left[:, :, :]))
            step(nc.vector.tensor_tensor(left[:, :, :], left[:, :, :], parts[1], ALU.subtract))
            step(nc.vector.tensor_copy(parts[2], left[:, :, :]))

        @block.scalar
        def _(act):
            for c, (m0, k) in enumerate(CH):
                act.wait_ge(hx, c + 1)
                nc.scalar.copy(hx_t[:, m0 * P:(m0 + k) * P], x_ps[0:D, c % 2, 0:k * P]).then_inc(hx_sb, 1)


def edge_layer(nc, g, S, l):
    B, ND = S.blocks, S.dst_tiles
    H = 4
    K1 = S.split_used
    with ExitStack() as ctx:
        sb = lambda name, shape, dt=F32: ctx.enter_context(nc.sbuf_tensor(f"l{l}_{name}", shape, dt))
        sem = lambda name: ctx.enter_context(semaphore(nc, f"l{l}_{name}"))
        ps = lambda name, k: ctx.enter_context(nc.psum_tensor(f"l{l}_{name}", [P, k, 512], F32))
        split = sb("split", [K1, 4, H * P], BF16)
        hidden = sb("hidden", [D + 4, 4, H * P])
        index = sb("gather_index", [P, 4, H], U32)
        gathered = sb("gathered", [P, 4, H, 2 * D])
        node_hot = sb("node_hot", [P, 2, H * P], BF16)
        edge_hot = sb("edge_hot", [P, 2, H, P])
        edge = sb("edge", [P, 2, H, 2 * D])
        scored = sb("scored", [P, 2, H, D])
        logit = sb("logit", [P, 2, H])
        att = sb("attention", [P, 2, H])
        msg = sb("message", [P, 2, H, D])
        spread_ps = ps("spread_ps", 1)
        hidden_ps = ps("hidden_ps", 1)
        edge_ps = ps("edge_ps", 2)
        sum_ps = ps("sum_ps", 2)
        landed = [sem(f"rows_landed_{r}") for r in range(4)]
        gather_done = g.gather_done[l]
        indexed = sem("gather_index_ready")
        begun = sem("gather_begun")
        spread_done = sem("spread_done")
        x_done = sem("x_done")
        hot_done = sem("node_hot_done")
        relu_done = sem("hidden_done")
        y_done = sem("y_done")
        edge_done = sem("edge_sums_done")
        weighed = sem("scores_weighed")
        scored_done = sem("scored_done")
        att_done = sem("attention_done")
        msg_done = sem("message_done")
        edge_hot_done = sem("edge_hot_done")
        z_done = sem("z_done")
        added = sem("sums_added")
        block = ctx.enter_context(nc.Block())
        N = ND // H
        assert N % 2 == 0

        @block.sync
        def _(sp):
            def load(n, r):
                since(sp, x_done, n - 3)
                since(sp, y_done, n - 3)
                cols = bass.ds(n * (H * P), H * P)
                sp.dma_start(split[:, r, :], g.split_rows[0:K1, cols]).then_inc(landed[r], 16)
                sp.dma_start(hidden[D:D + 4, r, :], g.attr_rows[3:7, cols]).then_inc(landed[r], 16)

            def four(i):
                for r in range(4):
                    load(i * 4 + r, r)

            rounds(sp, N // 4, four)
            for r in range(N % 4):
                load(N // 4 * 4 + r, r)

        @block.gpsimd
        def _(pool):
            def gather(n, r):
                since(pool, edge_done, n - 3)
                nc.gpsimd.tensor_copy(index[:, r, :], g.src_node[:, bass.ds(n * H, H)]).then_inc(indexed, 1)
                pool.wait_ge(indexed, n + 1)
                pool.sem_inc(begun, 1)
                for j in range(H):
                    nc.gpsimd.indirect_dma_start(
                        out=gathered[:, r, j, :], out_offset=None, in_=g.src_table[:, :],
                        in_offset=bass.IndirectOffsetOnAxis(ap=index[:, r, j:j + 1], axis=0),
                    ).then_inc(gather_done[r], 16)

            def four(i):
                for r in range(4):
                    gather(i * 4 + r, r)

            rounds(pool, N // 4, four)
            for r in range(N % 4):
                gather(N // 4 * 4 + r, r)

        @block.tensor
        def _(pe):
            def x(n, r, turn):
                pe.wait_ge(landed[r], turn * 32 + 32)
                since(pe, hot_done, n)
                nc.tensor.matmul(spread_ps[:, 0, :], g.select[:, :], split[:, r, :], start=True, stop=True).then_inc(spread_done, 1)
                since(pe, relu_done, n)
                nc.tensor.matmul(hidden_ps[0:D, 0, :], g.w_e1_parts[:, :], split[:, r, :], start=True, stop=True).then_inc(x_done, 1)

            def y(n, r):
                h = r % 2
                blk = numbers(nc, mybir.EngineType.PE, g.dst_tab[0:1, bass.ds(n * H, H)], B)
                pe.wait_ge(hot_done, n + 1)
                pe.wait_ge(relu_done, n + 1)
                since(pe, edge_done, n - 1)
                for j in range(H):
                    cols = slice(j * P, (j + 1) * P)
                    att_cols = slice(j * P, j * P + D)
                    nc.tensor.matmul(edge_ps[:, h, cols], hidden[:, r, cols], g.w_edge[:, :], start=True, stop=False, skip_group_check=True)
                    for k in range(3):
                        mm = nc.tensor.matmul(edge_ps[:, h, att_cols], node_hot[:, h, cols],
                                              g.dst_parts[:, bass.ds(blk[j], 1), k, :].rearrange("p o d -> p (o d)"),
                                              start=False, stop=(k == 2), skip_group_check=True)
                mm.then_inc(y_done, 1)

            def z(n, h):
                pe.wait_ge(msg_done, n + 1)
                pe.wait_ge(edge_hot_done, n + 1)
                since(pe, added, (n - 1) * H)
                for j in range(H):
                    mm = nc.tensor.matmul(sum_ps[0:D, h, j * P:(j + 1) * P], msg[:, h, j, :], edge_hot[:, h, j, :],
                                          start=True, stop=True)
                mm.then_inc(z_done, 1)

            x(0, 0, 0)
            x(1, 1, 0)
            y(0, 0)
            for n in (1, 2):
                x(n + 1, n + 1, 0)
                y(n, n)
                z(n - 1, (n - 1) % 2)
            with pe.Fori(0, (N - 4) // 4) as i:
                for k in range(4):
                    n = i * 4 + (k + 3)
                    x(n + 1, k, i + 1)
                    y(n, (k + 3) % 4)
                    z(n - 1, k % 2)
            for n in range((N - 4) // 4 * 4 + 3, N):
                if n + 1 < N:
                    x(n + 1, (n + 1) % 4, (n + 1) // 4)
                y(n, n % 4)
                z(n - 1, (n - 1) % 2)
            z(N - 1, (N - 1) % 2)

        @block.scalar
        def _(act):
            def relu(n, r):
                act.wait_ge(x_done, n + 1)
                since(act, y_done, n - 3)
                nc.scalar.activation(hidden[0:D, r, :], hidden_ps[0:D, 0, :], ACT.Relu).then_inc(relu_done, 1)

            def message(n, h):
                act.wait_ge(scored_done, n + 1)
                since(act, msg_done, n - 1)
                nc.scalar.activation(att[:, h, :], logit[:, h, :], ACT.Sigmoid, bias=g.ba2[:, 0:1]).then_inc(att_done, 1)
                act.wait_ge(att_done, n + 1)
                since(act, z_done, n - 1)
                for j in range(H):
                    ins = nc.scalar.activation(msg[:, h, j, :], edge[:, h, j, D:2 * D], ACT.Copy, scale=att[:, h, j:j + 1])
                ins.then_inc(msg_done, 1)

            relu(0, 0)
            relu(1, 1)
            message(0, 0)
            for n in (1, 2):
                relu(n + 1, n + 1)
                message(n, n % 2)
            with act.Fori(0, (N - 4) // 4) as i:
                for k in range(4):
                    n = i * 4 + (k + 3)
                    relu(n + 1, k)
                    message(n, (k + 1) % 2)
            for n in range((N - 4) // 4 * 4 + 3, N):
                if n + 1 < N:
                    relu(n + 1, (n + 1) % 4)
                message(n, n % 2)

        @block.vector
        def _(dve):
            def hots(n, h):
                dve.wait_ge(spread_done, n + 1)
                since(dve, y_done, n - 1)
                nc.vector.tensor_scalar(node_hot[:, h, :], spread_ps[:, 0, :], g.iota_part[:, 0:1], None,
                                        ALU.is_equal).then_inc(hot_done, 1)

            def score(n, h, r, turn):
                since(dve, z_done, n - 1)
                nc.vector.tensor_tensor(edge_hot[:, h, :, :], g.iota_free[:, :].unsqueeze(1).broadcast_to([P, H, P]),
                                        g.dst_col[:, bass.ds(n * H, H)].unsqueeze(2).broadcast_to([P, H, P]),
                                        ALU.is_equal).then_inc(edge_hot_done, 1)
                dve.wait_ge(y_done, n + 1)
                dve.wait_ge(gather_done[r], turn * (16 * H) + 16 * H)
                since(dve, msg_done, n - 1)
                nc.vector.tensor_tensor(edge[:, h, :, :].rearrange("p j c -> p (j c)"), gathered[:, r, :, :].rearrange("p j c -> p (j c)"),
                                        edge_ps[:, h, :], ALU.add).then_inc(edge_done, 1)
                dve.wait_ge(edge_done, n + 1)
                nc.vector.scalar_tensor_tensor(out=scored[:, h, :, :], in0=edge[:, h, :, 0:D], scalar=0.0,
                                               in1=g.wa2[:, :].unsqueeze(1).broadcast_to([P, H, D]), op0=ALU.max, op1=ALU.mult).then_inc(weighed, 1)
                dve.wait_ge(weighed, n + 1)
                nc.vector.tensor_reduce(logit[:, h, :], scored[:, h, :, :], AX.X, ALU.add).then_inc(scored_done, 1)

            def add(n, h):
                blk = numbers(nc, mybir.EngineType.DVE, g.dst_tab[0:1, bass.ds(n * H, H)], B)
                dve.wait_ge(z_done, n + 1)
                for j in range(H):
                    since(dve, added, n * H + j)
                    to = node(g.sums_t, blk[j])
                    nc.vector.tensor_tensor(to, to, sum_ps[0:D, h, j * P:(j + 1) * P], ALU.add).then_inc(added, 1)

            hots(0, 0)
            hots(1, 1)
            score(0, 0, 0, 0)
            for n in (0, 1):
                hots(n + 2, n % 2)
                score(n + 1, (n + 1) % 2, n + 1, 0)
                add(n, n % 2)
            with dve.Fori(0, (N - 6) // 4) as i:
                for k in range(4):
                    n = i * 4 + (k + 2)
                    hots(n + 2, k % 2)
                    score(n + 1, (k + 1) % 2, (k + 3) % 4, i + (k + 3) // 4)
                    add(n, k % 2)
            m = (N - 6) // 4 * 4 + 2
            for n in range(m, N):
                if n + 2 < N:
                    hots(n + 2, n % 2)
                if n + 1 < N:
                    score(n + 1, (n + 1) % 2, (n + 1) % 4, (n + 1) // 4)
                add(n, n % 2)

    with ExitStack() as ctx:
        sem = lambda name: ctx.enter_context(semaphore(nc, f"l{l}_{name}"))
        back_ps = ctx.enter_context(nc.psum_tensor(f"l{l}_back_ps", [P, 4, 512], F32))
        turned = sem("sums_turned")
        block = ctx.enter_context(nc.Block())

        @block.tensor
        def _(pe):
            for m in range(B):
                nc.tensor.transpose(back_ps[:, m // 8, m % 8 * D:(m % 8 + 1) * D], g.sums_t[:, m, :], g.ident[0:D, 0:D]).then_inc(turned, 1)

        @block.vector
        def _(dve):
            for k in range(-(-B // 8)):
                m0, m1 = k * 8, min(B, k * 8 + 8)
                dve.wait_ge(turned, m1)
                nc.vector.tensor_copy(g.sums[:, m0:m1, :].rearrange("p b d -> p (b d)"), back_ps[:, k, 0:(m1 - m0) * D])


def attention_layers(nc, g, S):
    B, NT = S.blocks, S.tiles
    every = lambda row: row[:, :].unsqueeze(1).broadcast_to([P, B, D])
    with ExitStack() as ctx:
        sb = lambda name, shape, dt=F32: ctx.enter_context(nc.sbuf_tensor(name, shape, dt))
        g.dst_col = sb("dst_col", [P, S.dst_tiles])
        g.src_node = sb("src_node", [P, S.dst_tiles], U32)
        split_slots(nc, g, S)
        g.gather_done = [[nc.alloc_semaphore(name=f"l{l}_gathered_{r}") for r in range(4)] for l in range(S.layers)]
        g.h = sb("h", [P, B, D])
        g.dst_parts = sb("dst_parts", [P, B + 1, 3, D], BF16)
        g.sums_t = sb("sums_turned", [D, B + 1, P])
        g.sums = sb("sums", [P, B, D])
        normed = sb("normed", [P, B, D])
        g.w_node, g.w_ai, g.w_aj = (sb(n, [D, D]) for n in ("w_node", "w_ai", "w_aj"))
        g.w_edge = sb("w_edge", [D + 4, 2 * D])
        g.w_e1 = sb("w_e1", [S.split_used, D])
        g.w_e1_parts = sb("w_e1_parts", [S.split_used, D], BF16)
        g.wa2, g.bias, g.ln_g, g.ln_b = (sb(n, [P, D]) for n in ("wa2", "bias", "ln_g", "ln_b"))
        g.ba2 = sb("ba2", [P, 1])
        g.select = sb("select", [S.split_used, P], BF16)
        with nc.Block() as block:
            @block.vector
            def _(dve):
                nc.vector.tensor_copy(g.h[:, :, :], g.x[:, :, :])
                nc.vector.tensor_copy(g.select[:, :], g.ident[0:S.split_used, 0:1].broadcast_to([S.split_used, P]))
        for l in range(S.layers):
            node_tables(nc, g, S, l)
            edge_layer(nc, g, S, l)

            def add_bias(step):
                step(nc.vector.tensor_tensor(g.sums[:, :, :], g.sums[:, :, :], every(g.bias), ALU.add))

            def affine(step):
                step(nc.vector.tensor_tensor(normed[:, :, :], normed[:, :, :], every(g.ln_g), ALU.mult))
                step(nc.vector.tensor_tensor(normed[:, :, :], normed[:, :, :], every(g.ln_b), ALU.add))
                if l < S.layers - 1:
                    step(nc.vector.tensor_scalar(normed[:, :, :], normed[:, :, :], 0.0, None, ALU.max))
                step(nc.vector.tensor_tensor(g.h[:, :, :], g.h[:, :, :], normed[:, :, :], ALU.add))

            layer_norm(nc, g, S, f"l{l}_norm", g.sums, normed, add_bias, affine)

        def add_x(step):
            step(nc.vector.tensor_tensor(g.h[:, :, :], g.h[:, :, :], g.x[:, :, :], ALU.add))

        layer_norm(nc, g, S, "norm2", g.h, g.x, add_x)


def last_layer(nc, g, S):
    B = S.blocks
    K = 3
    with ExitStack() as ctx:
        sb = lambda name, shape, dt=F32: ctx.enter_context(nc.sbuf_tensor(name, shape, dt))
        w_inv2 = sb("w_inv_squared", [P, B])
        scaled = [sb("scaled_even", [P, B, D]), sb("scaled_odd", [P, B, D])]
        hop = [g.x] + [sb(f"hop_{k}", [P, B, D]) for k in (1, 2, 3)]
        with nc.Block() as block:
            @block.vector
            def _(dve):
                nc.vector.tensor_tensor(w_inv2[:, :], g.w_inv[:, :], g.w_inv[:, :], ALU.mult)
                nc.vector.tensor_tensor(scaled[0][:, :, :], g.x[:, :, :], spread(g.w_inv[:, :], D), ALU.mult)

        def finish(p, m, product):
            nc.vector.tensor_scalar(node(hop[p + 1], m), product, node_scale(g.w_inv, m), None, ALU.mult)
            return nc.vector.tensor_scalar(node(scaled[1 - p % 2], m), product, node_scale(w_inv2, m), None, ALU.mult)

        sweeps(nc, g, S, "normed", g.weights, 1, [(scaled[p % 2], scaled[1 - p % 2]) for p in range(K)], finish)
        with ExitStack() as ctx2:
            sem = lambda name: ctx2.enter_context(semaphore(nc, name))
            theta = ctx2.enter_context(nc.sbuf_tensor("theta", [D, 2, K, D], F32))
            hop_t = ctx2.enter_context(nc.sbuf_tensor("hop_turned", [D, 2, 4 * P], F32))
            z = scaled[0]
            t_ps = ctx2.enter_context(nc.psum_tensor("hop_turn_ps", [P, 2, 512], F32))
            o_ps = ctx2.enter_context(nc.psum_tensor("theta_ps", [P, 2, 512], F32))
            landed, turned, copied, done, read = (sem(n) for n in (
                "thetas_landed", "hops_turned", "hops_copied", "thetas_summed", "thetas_read"))
            block = ctx2.enter_context(nc.Block())

            @block.sync
            def _(sp):
                for w, src in ((0, g.theta_f), (1, g.theta_b)):
                    sp.dma_start(theta[:, w, :, :], src[:, :, :].rearrange("k i o -> i k o")).then_inc(landed, 16)

            terms = [(0, 0, 0), (1, 1, 0), (2, 0, 1), (1, 1, 1), (3, 0, 2), (2, 1, 2)]

            @block.tensor
            def _(pe):
                def turn(m):
                    if m >= 2:
                        pe.wait_ge(copied, m - 1)
                    for k in range(4):
                        mm = nc.tensor.transpose(t_ps[0:D, m % 2, k * P:(k + 1) * P], hop[k][:, m, :], g.ident[:, :])
                    mm.then_inc(turned, 1)

                turn(0)
                pe.wait_ge(landed, 32)
                for m in range(B):
                    if m + 1 < B:
                        turn(m + 1)
                    pe.wait_ge(copied, m + 1)
                    if m >= 2:
                        pe.wait_ge(read, m - 1)
                    for t, (k, w, i) in enumerate(terms):
                        mm = nc.tensor.matmul(o_ps[:, m % 2, 0:D], hop_t[:, m % 2, k * P:(k + 1) * P], theta[:, w, i, :],
                                              start=(t == 0), stop=(t == len(terms) - 1))
                    mm.then_inc(done, 1)

            @block.scalar
            def _(act):
                for m in range(B):
                    act.wait_ge(turned, m + 1)
                    if m >= 2:
                        act.wait_ge(done, m - 1)
                    nc.scalar.copy(hop_t[:, m % 2, :], t_ps[0:D, m % 2, :]).then_inc(copied, 1)

            @block.vector
            def _(dve):
                for m in range(B):
                    dve.wait_ge(done, m + 1)
                    nc.vector.tensor_tensor(z[:, m, :], o_ps[:, m % 2, 0:D], g.x[:, m, :], ALU.add).then_inc(read, 1)

        layer_norm(nc, g, S, "norm3", scaled[0], g.x)


def store_features(nc, g, S):
    full = (S.blocks - 1) * P
    with semaphore(nc, "out_stored") as stored, nc.Block() as block:
        @block.sync
        def _(sp):
            sp.dma_start(g.out[0:full, :].rearrange("(b p) d -> p b d", p=P), g.x[:, 0:S.blocks - 1, :]).then_inc(stored, 16)
            sp.dma_start(g.out[full:S.n, :], g.x[0:S.last_rows, S.blocks - 1, :]).then_inc(stored, 16)
            sp.wait_ge(stored, 32)


class Arrays:
    pass


def graph_network(nc, x, src, dst, edge_attr_3, edge_weight, L1_gnn_eps, L2_gnn_W_node, L2_gnn_W_e1, L2_gnn_b_e1,
                  L2_gnn_W_e2, L2_gnn_b_e2, L2_gnn_Wa1, L2_gnn_ba1, L2_gnn_Wa2, L2_gnn_ba2, L2_gnn_bias, L2_gnn_ln_g,
                  L2_gnn_ln_b, L3_gnn_theta_forward, L3_gnn_theta_backward, out):
    g = Arrays()
    g.x_in, g.eps1_in, g.out = x, L1_gnn_eps, out
    g.src, g.dst, g.w = src, dst, edge_weight
    g.ea = edge_attr_3.rearrange("e k -> (e k)")
    g.W_node, g.W_e1, g.b_e1, g.W_e2, g.b_e2 = L2_gnn_W_node, L2_gnn_W_e1, L2_gnn_b_e1, L2_gnn_W_e2, L2_gnn_b_e2
    g.Wa1, g.ba1, g.Wa2, g.ba2_in = L2_gnn_Wa1, L2_gnn_ba1, L2_gnn_Wa2, L2_gnn_ba2
    g.bias_in, g.ln_g_in, g.ln_b_in = L2_gnn_bias, L2_gnn_ln_g, L2_gnn_ln_b
    g.theta_f, g.theta_b = L3_gnn_theta_forward, L3_gnn_theta_backward
    S = Shapes(x.shape[0], src.shape[0])
    B, T, NT = S.blocks, S.in_tiles, S.tiles
    dram = lambda name, shape, dt=F32: nc.dram_tensor(name, shape, dt).ap()
    g.key_rows = dram("key_rows", [T, P])
    g.blk_rows = dram("blk_rows", [T, P])
    g.slots = dram("slots", [P * NT, S.rec])
    g.first_tiles = dram("first_tiles", [B * B + 1])
    blocks = dram("blocks", [B * B + 1 + S.body, P, 2, P])
    g.blocks = blocks.rearrange("q p k c -> (q p) (k c)")
    g.counts = blocks[0:B * B, :, 0, :].rearrange("(b a) p c -> b p a c", a=B)
    g.weights = blocks[0:B * B, :, 1, :].rearrange("(b a) p c -> a p b c", a=B)
    g.dst_slots = dram("dst_slots", [P * S.dst_tiles, S.rec])
    g.dst_firsts = dram("dst_firsts", [B + 1])
    g.attr_rows = dram("attr_rows", [S.rec, S.dst_tiles * P])
    g.split_rows = dram("split_rows", [S.split, S.dst_tiles * P], BF16)
    g.src_table = dram("src_table", [B * P, 2 * D])
    g.bucket_of = dram("bucket_of", [-(-(NT + 2) // P) * P])
    with ExitStack() as ctx:
        sb = lambda name, shape, dt=F32: ctx.enter_context(nc.sbuf_tensor(name, shape, dt))
        g.ident = sb("ident", [P, P])
        g.iota_free = sb("iota_free", [P, P])
        g.iota_part = sb("iota_part", [P, 1])
        g.earlier = sb("earlier", [P, P])
        g.before = sb("before", [P, P])
        g.off_diagonal = sb("off_diagonal", [P, P])
        g.dst_tab = sb("dst_tab", [1, S.dst_tiles], I32)
        g.deg = sb("degrees", [P, B, 3])
        constants(nc, g, S)
        with ExitStack() as ctx1:
            sb1 = lambda name, shape, dt=F32: ctx1.enter_context(nc.sbuf_tensor(name, shape, dt))
            g.rec = sb1("rec", [P, T, S.rec])
            g.src_blk = sb1("src_blk", [P, T])
            g.dst_blk = sb1("dst_blk", [P, T])
            g.key_col = sb1("key_col", [P, T])
            g.dst_index = sb1("dst_index", [P, T], U32)
            edges_in(nc, g, S)
            with ExitStack() as ctx2:
                g.src_hot = ctx2.enter_context(nc.sbuf_tensor("src_hot", [P, T, B], BF16))
                g.start = ctx2.enter_context(nc.sbuf_tensor("start", [B, T + 1, B], F32))
                g.shift = ctx2.enter_context(nc.sbuf_tensor("shift", [B, B], F32))
                count_buckets(nc, g, S)
                slot_edges(nc, g, S)
            g.same = sb1("same_bucket", [P, NT + 1])
            g.tab = sb1("tab", [1, NT], I32)
            g.tile_blk = sb1("tile_blk", [P, 2, -(-(NT + 2) // P)])
            g.sums = sb1("tile_sums", [P, 3, NT])
            tile_tables(nc, g, S)
            g.recs = sb1("recs", [P, NT, S.rec])
            load_slots(nc, g, S)
            build_matrices(nc, g, S)
            degrees(nc, g, S)
        g.x = sb("x", [P, B, D])
        g.w_inv = sb("w_inv", [P, B])
        load_features(nc, g, S)
        first_layers(nc, g, S)
        attention_layers(nc, g, S)
        last_layer(nc, g, S)
        store_features(nc, g, S)


_INS = ["x", "src", "dst", "edge_attr_3", "edge_weight", "L1_gnn_eps", "L2_gnn_W_node", "L2_gnn_W_e1", "L2_gnn_b_e1",
        "L2_gnn_W_e2", "L2_gnn_b_e2", "L2_gnn_Wa1", "L2_gnn_ba1", "L2_gnn_Wa2", "L2_gnn_ba2", "L2_gnn_bias", "L2_gnn_ln_g",
        "L2_gnn_ln_b", "L3_gnn_theta_forward", "L3_gnn_theta_backward"]


def kernel(**inputs):
    import numpy as _np
    import concourse.bacc as _bacc
    from concourse.bass_utils import run_bass_kernel_spmd as _run

    nc = _bacc.Bacc("TRN2", target_bir_lowering=False, num_devices=1)
    arrays, args = {}, []
    for name in _INS:
        a = _np.ascontiguousarray(inputs[name])
        arrays[f"in_{name}_dram"] = a
        args.append(nc.dram_tensor(f"in_{name}_dram", a.shape, mybir.dt.from_np(a.dtype), kind="ExternalInput").ap())
    shape = inputs["x"].shape
    args.append(nc.dram_tensor("out_0_dram", shape, F32, kind="ExternalOutput").ap())
    graph_network(nc, *args)
    r = _run(nc, [arrays], core_ids=[0])
    return r.results[0]["out_0_dram"]
```

```python
from contextlib import ExitStack, contextmanager

import concourse.bass as bass
from concourse import mybir

ALU = mybir.AluOpType
ACT = mybir.ActivationFunctionType
AX = mybir.AxisListType
F32 = mybir.dt.float32
BF16 = mybir.dt.bfloat16
I32 = mybir.dt.int32
U32 = mybir.dt.uint32

P = 128
D = 64


@contextmanager
def semaphore(nc, name):
    handle = nc.alloc_semaphore(name=name)
    yield handle
    nc.gpsimd.sem_clear(handle)
    nc.release_semaphore(handle)


def since(engine, sem, value):
    if not isinstance(value, int) or value > 0:
        engine.wait_ge(sem, value)


def rounds(engine, count, body, ahead=1):
    for i in range(ahead):
        body(i)
    with engine.Fori(ahead, count) as i:
        body(i)


class Shapes:

    def __init__(self, n_nodes, n_edges):
        self.n = n_nodes
        self.e = n_edges
        self.blocks = -(-n_nodes // P)
        self.last_rows = n_nodes - (self.blocks - 1) * P
        self.in_tiles = -(-n_edges // P)
        self.groups = 4
        self.group_rows = -(-self.in_tiles // self.groups)
        self.last_edges = n_edges - (self.in_tiles - 1) * P
        assert self.groups * self.group_rows == self.in_tiles and self.last_edges < P
        self.buckets = self.blocks * self.blocks
        self.body = 8
        tiles = n_edges // P + self.buckets
        self.tiles = -(-tiles // self.body) * self.body
        self.rec = 8
        self.dst_tiles = n_edges // P + self.blocks
        assert self.dst_tiles % self.body == 0
        self.split = 32
        self.split_used = 22
        self.ring = 5
        assert self.blocks % self.ring == 0
        self.hops = 10
        self.layers = 3
        self.keep = 0.9
        self.eps = 1e-5
        self.rank_half = 13
        assert self.in_tiles % (4 * self.rank_half) == 0
        self.div_mul, self.div_shift = 1311, 15
        assert all(q * self.div_mul >> self.div_shift == q // self.blocks for q in range(self.buckets + 1))


def edges_in(nc, g, S):
    R, NG, B = S.group_rows, S.groups, S.blocks
    with ExitStack() as ctx:
        sb = lambda name, shape, dt: ctx.enter_context(nc.sbuf_tensor(name, shape, dt))
        sem = lambda name: ctx.enter_context(semaphore(nc, name))
        ends = [sb("src_rows", [R, NG, P], I32), sb("dst_rows", [R, NG, P], I32)]
        w_rows = sb("w_rows", [R, NG, P], F32)
        ea_rows = sb("ea_rows", [R, NG, 3 * P], F32)
        blk_i = [sb("src_blk_i", [R, NG * P], I32), sb("dst_blk_i", [R, NG * P], I32)]
        loc_i = [sb("src_loc_i", [R, NG * P], I32), sb("dst_loc_i", [R, NG * P], I32)]
        blk_f = [sb("src_blk_f", [R, NG, P], F32), sb("dst_blk_f", [R, NG, P], F32)]
        loc_f = [sb("src_loc_f", [R, NG, P], F32), sb("dst_loc_f", [R, NG, P], F32)]
        key_f = sb("key_f", [R, NG, P], F32)
        src_f = sb("src_f", [R, NG, P], F32)
        fill = sb("fill", [P, S.tiles * S.rec], F32)
        turned = ctx.enter_context(nc.psum_tensor("turned", [P, 8, 512], F32))

        padded = sem("padded")
        s_in = sem("edges_landed")
        own = sem("split_steps")
        split = sem("rows_split")
        s_store = sem("rows_stored")
        s_turn = sem("field_turned")
        taken = sem("field_taken")
        filled = sem("fill_ready")

        block = ctx.enter_context(nc.Block())
        last = NG - 1
        full = S.last_edges

        @block.sync
        def _(sp):
            sp.wait_ge(padded, 4)
            for x, rows, k in ((g.src, ends[0], 1), (g.dst, ends[1], 1), (g.w, w_rows, 1), (g.ea, ea_rows, 3)):
                n = last * R * P * k
                sp.dma_start(rows[:, 0:last, :], x[0:n].rearrange("(j r e) -> r j e", j=last, r=R)).then_inc(s_in, 16)
                m = n + (R - 1) * P * k
                sp.dma_start(rows[0:R - 1, last, :], x[n:m].rearrange("(r e) -> r e", r=R - 1)).then_inc(s_in, 16)
                sp.dma_start(rows[R - 1:R, last, 0:full * k], x[m:m + full * k].rearrange("(r e) -> r e", r=1)).then_inc(s_in, 16)
            sp.wait_ge(split, 1)
            sp.dma_start(g.key_rows[:, :].rearrange("(j r) e -> r j e", j=NG), key_f[:, :, :]).then_inc(s_store, 16)
            sp.dma_start(g.blk_rows[:, :].rearrange("(j r) e -> r j e", j=NG), blk_f[1][:, :, :]).then_inc(s_store, 16)
            sp.wait_ge(filled, 1)
            sp.dma_start(g.slots[:, :].rearrange("(p t) f -> p (t f)", p=P), fill[:, :]).then_inc(s_store, 16)
            sp.dma_start(g.dst_slots[:, :].rearrange("(p t) f -> p (t f)", p=P),
                         fill[:, 0:S.dst_tiles * S.rec]).then_inc(s_store, 16)
            sp.wait_ge(s_store, 64)

        @block.gpsimd
        def _(pool):
            nc.gpsimd.memset(fill[:, :], -1.0).then_inc(filled, 1)

        @block.vector
        def _(dve):
            for rows in ends:
                nc.vector.memset(rows[:, last, :], -P).then_inc(padded, 1)
            for rows in (w_rows, ea_rows):
                nc.vector.memset(rows[:, last, :], 0.0).then_inc(padded, 1)
            nc.vector.memset(g.rec[:, :, 3:4], 1.0)
            dve.wait_ge(s_in, 16 * 12)
            for k in range(2):
                flat = ends[k][:, :, :].rearrange("r j e -> r (j e)")
                nc.vector.tensor_scalar(blk_i[k][:, :], flat, 7, None, ALU.arith_shift_right).then_inc(own, 1)
                nc.vector.tensor_scalar(loc_i[k][:, :], flat, P - 1, None, ALU.bitwise_and).then_inc(own, 1)
            dve.wait_ge(own, 4)
            nc.vector.tensor_copy(src_f[:, :, :], ends[0][:, :, :])
            for k in range(2):
                nc.vector.tensor_copy(blk_f[k][:, :, :].rearrange("r j e -> r (j e)"), blk_i[k][:, :]).then_inc(own, 1)
                nc.vector.tensor_copy(loc_f[k][:, :, :].rearrange("r j e -> r (j e)"), loc_i[k][:, :]).then_inc(own, 1)
            dve.wait_ge(own, 8)
            nc.vector.scalar_tensor_tensor(
                out=key_f[:, :, :].rearrange("r j e -> r (j e)"), in0=blk_f[1][:, :, :].rearrange("r j e -> r (j e)"),
                scalar=float(B), in1=blk_f[0][:, :, :].rearrange("r j e -> r (j e)"), op0=ALU.mult, op1=ALU.add,
            ).then_inc(split, 1)
            for f, out in enumerate((g.src_blk[:, :], g.dst_blk[:, :], g.rec[:, :, 0], g.rec[:, :, 1], g.rec[:, :, 2],
                                     g.rec[:, :, 4], g.rec[:, :, 5], g.rec[:, :, 6], g.rec[:, :, 7])):
                dve.wait_ge(s_turn, f + 1)
                nc.vector.tensor_copy(out, turned[:, f % 8, 0:S.in_tiles]).then_inc(taken, 1)

        @block.tensor
        def _(pe):
            pe.wait_ge(split, 1)
            fields = [blk_f[0][:, j, :] for j in range(NG)], [blk_f[1][:, j, :] for j in range(NG)], \
                [loc_f[0][:, j, :] for j in range(NG)], [loc_f[1][:, j, :] for j in range(NG)], \
                [w_rows[:, j, :] for j in range(NG)], \
                *[[ea_rows[:, j, k:3 * P:3] for j in range(NG)] for k in range(3)], [src_f[:, j, :] for j in range(NG)]
            for f, rows in enumerate(fields):
                if f >= 8:
                    pe.wait_ge(taken, f - 7)
                for j in range(NG):
                    mm = nc.tensor.transpose(turned[:, f % 8, j * R:(j + 1) * R], rows[j], g.ident[0:R, 0:R])
                mm.then_inc(s_turn, 1)


def constants(nc, g, S):
    with ExitStack() as ctx:
        made = ctx.enter_context(semaphore(nc, "constants_made"))
        block = ctx.enter_context(nc.Block())

        @block.gpsimd
        def _(pool):
            nc.gpsimd.iota(g.iota_free[:, :], pattern=[[1, P]], base=0, channel_multiplier=0,
                           allow_small_or_imprecise_dtypes=True).then_inc(made, 1)
            nc.gpsimd.iota(g.iota_part[:, :], pattern=[[0, 1]], base=0, channel_multiplier=1,
                           allow_small_or_imprecise_dtypes=True).then_inc(made, 1)

        @block.vector
        def _(dve):
            dve.wait_ge(made, 2)
            nc.vector.tensor_scalar(g.ident[:, :], g.iota_free[:, :], g.iota_part[:, 0:1], None, ALU.is_equal)
            nc.vector.tensor_scalar(g.off_diagonal[:, :], g.iota_free[:, :], g.iota_part[:, 0:1], None, ALU.not_equal)
            nc.vector.tensor_scalar(g.earlier[:, :], g.iota_free[:, :], g.iota_part[:, 0:1], None, ALU.is_lt)
            nc.vector.tensor_scalar(g.before[:, :], g.iota_free[:, :], g.iota_part[:, 0:1], None, ALU.is_gt)



def count_buckets(nc, g, S):
    B, T = S.blocks, S.in_tiles
    CH = S.rank_half
    NB = T // CH
    with ExitStack() as ctx:
        sb = lambda name, shape, dt: ctx.enter_context(nc.sbuf_tensor(name, shape, dt))
        sem = lambda name: ctx.enter_context(semaphore(nc, name))
        dst_hot = sb("dst_hot", [P, T, B], BF16)
        tile_counts = sb("tile_counts", [B, T, B], F32)
        ones = sb("ones_row", [B, T], F32)
        n_int = sb("n_int", [B, 2, B], I32)
        n_tiles = sb("n_tiles", [B, B], F32)
        upto = sb("tiles_upto", [B, B], F32)
        ahead = sb("tiles_ahead", [B, B], F32)
        first = sb("first_tile", [B, B], F32)
        end = sb("end_tile", [B, B], F32)
        first_slot = sb("first_slot", [B, B], F32)
        edges_upto = sb("edges_upto", [B, B], F32)
        edges_ahead = sb("edges_ahead", [B, B], F32)
        d_int = sb("dst_tiles_int", [B, 2], I32)
        d_tiles = sb("dst_tiles", [B, 1], F32)
        d_first = sb("dst_first", [B, 2], F32)
        d_slot = sb("dst_first_slot", [B, 1], F32)
        count_ps = ctx.enter_context(nc.psum_tensor("count_ps", [B, 2, 512], F32))
        base_ps = ctx.enter_context(nc.psum_tensor("base_ps", [B, 512], F32))
        hot = sem("one_hots")
        counted = sem("tiles_counted")
        copied = sem("counts_copied")
        own = sem("count_steps")
        upto_ready = sem("tiles_upto_ready")
        d_ready = sem("dst_tiles_ready")
        d_base = sem("dst_base_ready")
        d_first_ready = sem("dst_first_ready")
        base_ready = sem("row_base_ready")
        first_ready = sem("first_tile_ready")
        s_store = sem("first_tile_stored")
        block = ctx.enter_context(nc.Block())

        @block.tensor
        def _(pe):
            pe.wait_ge(hot, 2)
            for n in range(NB):
                if n >= 2:
                    pe.wait_ge(copied, n - 1)
                for j in range(CH):
                    c = n * CH + j
                    mm = nc.tensor.matmul(count_ps[:, n % 2, j * B:(j + 1) * B], dst_hot[:, c, :], g.src_hot[:, c, :],
                                          start=True, stop=True)
                mm.then_inc(counted, 1)
            pe.wait_ge(upto_ready, 1)
            nc.tensor.matmul(base_ps[:, 0:1], g.before[0:B, 0:B], upto[:, B - 1:B], start=True, stop=True).then_inc(base_ready, 1)
            pe.wait_ge(d_ready, 1)
            nc.tensor.matmul(base_ps[:, 1:2], g.before[0:B, 0:B], d_tiles[:, :], start=True, stop=True).then_inc(d_base, 1)

        @block.vector
        def _(dve):
            steps = [0]

            def step(ins):
                steps[0] += 1
                ins.then_inc(own, 1)
                dve.wait_ge(own, steps[0])

            io = g.iota_free[:, 0:B].unsqueeze(1).broadcast_to([P, T, B])
            for hots, blk in ((g.src_hot, g.src_blk), (dst_hot, g.dst_blk)):
                nc.vector.tensor_tensor(hots[:, :, :], blk[:, :].unsqueeze(2).broadcast_to([P, T, B]), io,
                                        ALU.is_equal).then_inc(hot, 1)
            step(nc.vector.memset(ones[:, :], 1.0))
            step(nc.vector.memset(g.start[:, 0, :], 0.0))
            nc.vector.scalar_tensor_tensor(out=g.key_col[:, :], in0=g.dst_blk[:, :], scalar=float(B), in1=g.src_blk[:, :],
                                           op0=ALU.mult, op1=ALU.add)
            for n in range(NB):
                dve.wait_ge(counted, n + 1)
                nc.vector.tensor_copy(tile_counts[:, n * CH:(n + 1) * CH, :].rearrange("b t a -> b (t a)"),
                                      count_ps[:, n % 2, 0:CH * B]).then_inc(copied, 1)
            dve.wait_ge(copied, NB)
            for a in range(B):
                scan = nc.vector.tensor_tensor_scan(g.start[:, 1:T + 1, a], ones[:, :], tile_counts[:, :, a], 0.0,
                                                    ALU.mult, ALU.add)
                scan.then_inc(own, 1)
            steps[0] += B
            dve.wait_ge(own, steps[0])
            step(nc.vector.tensor_scalar(n_int[:, 0, :], g.start[:, T, :], float(P - 1), None, ALU.add))
            step(nc.vector.tensor_scalar(n_int[:, 1, :], n_int[:, 0, :], 7, None, ALU.arith_shift_right))
            step(nc.vector.tensor_scalar(n_tiles[:, :], n_int[:, 1, :], 1.0, None, ALU.max))
            nc.vector.tensor_tensor_scan(upto[:, :], ones[:, 0:B], n_tiles[:, :], 0.0, ALU.mult, ALU.add).then_inc(upto_ready, 1)
            dve.wait_ge(upto_ready, 1)
            step(nc.vector.tensor_tensor(ahead[:, :], upto[:, :], n_tiles[:, :], ALU.subtract))
            dve.wait_ge(base_ready, 1)
            nc.vector.tensor_scalar(end[:, :], upto[:, :], base_ps[:, 0:1], None, ALU.add).then_inc(first_ready, 1)
            nc.vector.tensor_scalar(first[:, :], ahead[:, :], base_ps[:, 0:1], None, ALU.add).then_inc(first_ready, 1)
            dve.wait_ge(first_ready, 2)
            step(nc.vector.tensor_scalar(first_slot[:, :], first[:, :], float(P), None, ALU.mult))
            step(nc.vector.tensor_tensor_scan(edges_upto[:, :], ones[:, 0:B], g.start[:, T, :], 0.0, ALU.mult, ALU.add))
            step(nc.vector.tensor_tensor(edges_ahead[:, :], edges_upto[:, :], g.start[:, T, :], ALU.subtract))
            step(nc.vector.tensor_scalar(d_int[:, 0:1], edges_upto[:, B - 1:B], float(P - 1), None, ALU.add))
            step(nc.vector.tensor_scalar(d_int[:, 1:2], d_int[:, 0:1], 7, None, ALU.arith_shift_right))
            nc.vector.tensor_copy(d_tiles[:, :], d_int[:, 1:2]).then_inc(d_ready, 1)
            dve.wait_ge(d_base, 1)
            nc.vector.tensor_copy(d_first[:, 0:1], base_ps[:, 1:2]).then_inc(d_first_ready, 1)
            nc.vector.tensor_tensor(d_first[:, 1:2], d_tiles[:, :], base_ps[:, 1:2], ALU.add).then_inc(d_first_ready, 1)
            dve.wait_ge(d_first_ready, 2)
            step(nc.vector.tensor_scalar(d_slot[:, :], d_first[:, 0:1], float(P), None, ALU.mult))
            step(nc.vector.tensor_tensor(edges_ahead[:, :], edges_ahead[:, :], first_slot[:, :], ALU.subtract))
            step(nc.vector.tensor_scalar(g.shift[:, :], edges_ahead[:, :], d_slot[:, 0:1], None, ALU.add))
            nc.vector.tensor_tensor(g.start[:, 0:T, :], g.start[:, 0:T, :],
                                    first_slot[:, :].unsqueeze(1).broadcast_to([B, T, B]), ALU.add)

        @block.sync
        def _(sp):
            sp.wait_ge(first_ready, 2)
            sp.dma_start(g.first_tiles[0:B * B].rearrange("(b a) -> b a", b=B), first[:, :]).then_inc(s_store, 16)
            sp.dma_start(g.first_tiles[B * B:B * B + 1].rearrange("(b a) -> b a", b=1), end[B - 1:B, B - 1:B]).then_inc(s_store, 16)
            sp.wait_ge(d_first_ready, 2)
            with nc.allow_non_contiguous_dma("one number per block"):
                sp.dma_start(g.dst_firsts[0:B].rearrange("(b a) -> b a", a=1), d_first[:, 0:1]).then_inc(s_store, 16)
            sp.dma_start(g.dst_firsts[B:B + 1].rearrange("(b a) -> b a", a=1), d_first[B - 1:B, 1:2]).then_inc(s_store, 16)
            sp.wait_ge(s_store, 64)


def tile_tables(nc, g, S):
    B, NT, ND = S.blocks, S.tiles, S.dst_tiles
    NC = -(-(NT + 2) // P)
    with ExitStack() as ctx:
        sb = lambda name, shape, dt: ctx.enter_context(nc.sbuf_tensor(name, shape, dt))
        sem = lambda name: ctx.enter_context(semaphore(nc, name))
        firsts = sb("firsts", [P, B * B + 1], F32)
        le = sb("begun", [P, B * B + 1], F32)
        num = sb("tile_num", [P, NC], F32)
        cnt = sb("buckets_begun", [P, NC], F32)
        bucket = sb("bucket_row", [P, NC * P], F32)
        d_firsts = sb("dst_firsts_sb", [1, B + 1], F32)
        d_num = sb("dst_tile_num", [1, ND], F32)
        d_begun = sb("dst_begun", [1, ND, B + 1], F32)
        d_cnt = sb("dst_cnt", [1, ND], F32)
        blk_i = sb("tile_blk_i", [P, 2, NC], I32)
        q_f = sb("q_f", [1, 2, NT], F32)
        landed = sem("firsts_landed")
        numbered = sem("tiles_numbered")
        own = sem("table_steps")
        cnt_ready = sem("buckets_found")
        bucket_back = sem("bucket_row_landed")
        turned = sem("bucket_row_stored")
        block = ctx.enter_context(nc.Block())

        @block.gpsimd
        def _(pool):
            nc.gpsimd.iota(num[:, :], pattern=[[P, NC]], base=0, channel_multiplier=1,
                           allow_small_or_imprecise_dtypes=True).then_inc(numbered, 1)
            nc.gpsimd.iota(d_num[:, :], pattern=[[1, ND]], base=0, channel_multiplier=0,
                           allow_small_or_imprecise_dtypes=True).then_inc(numbered, 1)

        @block.sync
        def _(sp):
            sp.dma_start(firsts[:, :], g.first_tiles[:].unsqueeze(0).broadcast_to([P, B * B + 1])).then_inc(landed, 16)
            sp.dma_start(d_firsts[:, :], g.dst_firsts[:].unsqueeze(0)).then_inc(landed, 16)
            sp.wait_ge(cnt_ready, 1)
            with nc.allow_non_contiguous_dma("one number per tile"):
                sp.dma_start(g.bucket_of[:].rearrange("(c p) -> p c", p=P), cnt[:, :]).then_inc(turned, 16)
            sp.wait_ge(turned, 16)
            sp.dma_start(bucket[:, :], g.bucket_of[:].unsqueeze(0).broadcast_to([P, NC * P])).then_inc(bucket_back, 16)

        @block.vector
        def _(dve):
            steps = [0]

            def step(ins):
                steps[0] += 1
                ins.then_inc(own, 1)
                dve.wait_ge(own, steps[0])

            dve.wait_ge(landed, 32)
            dve.wait_ge(numbered, 2)
            for c in range(NC):
                ins = nc.vector.tensor_scalar(le[:, :], firsts[:, :], num[:, c:c + 1], 0.0, ALU.is_le, ALU.add,
                                              accum_out=cnt[:, c:c + 1])
                if c < NC - 1:
                    step(ins)
            ins.then_inc(cnt_ready, 1)
            dve.wait_ge(cnt_ready, 1)
            src_blk, dst_blk = g.tile_blk[:, 0, :], g.tile_blk[:, 1, :]
            step(nc.vector.tensor_scalar(src_blk, cnt[:, :], -1.0, None, ALU.add))
            step(nc.vector.tensor_scalar(blk_i[:, 0, :], src_blk, float(S.div_mul), None, ALU.mult))
            step(nc.vector.tensor_scalar(blk_i[:, 1, :], blk_i[:, 0, :], S.div_shift, None, ALU.arith_shift_right))
            step(nc.vector.tensor_copy(dst_blk, blk_i[:, 1, :]))
            step(nc.vector.scalar_tensor_tensor(out=src_blk, in0=dst_blk, scalar=-float(B), in1=src_blk, op0=ALU.mult, op1=ALU.add))
            step(nc.vector.tensor_tensor(d_begun[:, :, :], d_firsts[:, :].unsqueeze(1).broadcast_to([1, ND, B + 1]),
                                         d_num[:, :].unsqueeze(2).broadcast_to([1, ND, B + 1]), ALU.is_le))
            step(nc.vector.tensor_reduce(d_cnt[:, :], d_begun[:, :, :], AX.X, ALU.add))
            step(nc.vector.tensor_scalar(g.dst_tab[:, :], d_cnt[:, :], -1.0, None, ALU.add))
            dve.wait_ge(bucket_back, 16)
            step(nc.vector.memset(g.same[:, :], 0.0))
            step(nc.vector.tensor_tensor(g.same[:, 1:NT + 1], bucket[:, 1:NT + 1], bucket[:, 0:NT], ALU.is_equal))
            q, spare = q_f[:, 0, :], q_f[:, 1, :]
            step(nc.vector.tensor_scalar(q, bucket[0:1, 0:NT], -1.0, None, ALU.add))
            step(nc.vector.tensor_copy(spare.rearrange("o (n s) -> o n s", s=S.body),
                                       g.iota_free[0:1, 0:S.body].unsqueeze(1).broadcast_to([1, NT // S.body, S.body])))
            step(nc.vector.tensor_scalar(spare, spare, float(B * B + 1), None, ALU.add))
            step(nc.vector.tensor_tensor(spare, spare, q, ALU.subtract))
            step(nc.vector.tensor_tensor(spare, spare, g.same[0:1, 1:NT + 1], ALU.mult))
            step(nc.vector.tensor_tensor(g.tab[:, :], q, spare, ALU.add))


def slot_edges(nc, g, S):
    B, T, CH = S.blocks, S.in_tiles, S.rank_half
    C2 = 2 * CH
    NCH = T // C2
    with ExitStack() as ctx:
        sb = lambda name, shape, dt: ctx.enter_context(nc.sbuf_tensor(name, shape, dt))
        sem = lambda name: ctx.enter_context(semaphore(nc, name))
        keys = sb("keys_spread", [P, 2, C2 * P], F32)
        blks = sb("blks_spread", [B, 2, C2 * P], F32)
        hot_t = sb("dst_hot_turned", [B, 2, C2 * P], F32)
        start_ring = sb("start_ring", [B, 2, C2 * B], F32)
        rec_ring = sb("rec_ring", [P, 2, C2, S.rec], F32)
        picked = sb("picked", [P, C2, B], F32)
        base = sb("base_slot", [P, C2], F32)
        shifted = sb("shifted", [P, C2, B], F32)
        shift = sb("shift_of_edge", [P, C2], F32)
        rank = sb("rank_in_tile", [P, C2], F32)
        off = sb("no_edge", [P, C2], F32)
        slot_i = sb("slot_i", [P, 3, C2], I32)
        dslot_i = sb("dst_slot_i", [P, 3, C2], I32)
        drow_f = sb("dst_row_f", [P, C2], F32)
        row_f = sb("row_f", [P, C2], F32)
        index = sb("slot_index", [P, 2, C2], U32)
        look_ps = ctx.enter_context(nc.psum_tensor("look_ps", [P, 4, 512], F32))
        shift_ps = ctx.enter_context(nc.psum_tensor("shift_ps", [P, 4, 512], F32))
        spread_free = sem("spread_free")
        landed = [sem("even_chunk_landed"), sem("odd_chunk_landed")]
        hot_ready = sem("turned_hot_ready")
        looked = sem("bases_looked_up")
        look_free = sem("look_ps_free")
        own = sem("slot_steps")
        ring_free = sem("record_ring_free")
        indexed = sem("slots_indexed")
        sent = nc.alloc_semaphore(name="records_sent")
        g.sent = nc.alloc_semaphore(name="records_sent_by_dst")
        block = ctx.enter_context(nc.Block())
        NS = 12
        no_slot = float(4 * S.tiles * P)

        @block.sync
        def _(sp):
            with sp.Fori(0, NCH // 2) as i:
                for h in range(2):
                    q = i * 2 + h
                    sp.wait_ge(spread_free, q + 1)
                    rows = bass.ds(q * C2, C2)
                    sp.dma_start(keys[:, h, :], g.key_rows[rows, :].rearrange("t e -> (t e)").unsqueeze(0).broadcast_to([P, C2 * P])).then_inc(landed[h], 16)
                    sp.dma_start(blks[:, h, :], g.blk_rows[rows, :].rearrange("t e -> (t e)").unsqueeze(0).broadcast_to([B, C2 * P])).then_inc(landed[h], 16)

        @block.tensor
        def _(pe):
            with pe.Fori(0, NCH // 2) as i:
                for h in range(2):
                    q = i * 2 + h
                    pe.wait_ge(hot_ready, 2 * q + 2)
                    pe.wait_ge(look_free, q + 1)
                    for j in range(C2):
                        mm = nc.tensor.matmul(look_ps[:, 2 * h + j // CH, (j % CH) * B:(j % CH + 1) * B],
                                              hot_t[:, h, j * P:(j + 1) * P], start_ring[:, h, j * B:(j + 1) * B],
                                              start=True, stop=True)
                        mm = nc.tensor.matmul(shift_ps[:, 2 * h + j // CH, (j % CH) * B:(j % CH + 1) * B],
                                              hot_t[:, h, j * P:(j + 1) * P], g.shift[:, :], start=True, stop=True)
                    mm.then_inc(looked, 1)

        @block.vector
        def _(dve):
            dve.sem_inc(spread_free, 2)
            dve.sem_inc(look_free, 2)

            def pair(i):
                for h in range(2):
                    q = i * 2 + h
                    steps = [0]

                    def step(ins):
                        steps[0] += 1
                        ins.then_inc(own, 1)
                        dve.wait_ge(own, q * NS + steps[0])

                    cols = bass.ds(q * C2, C2)
                    dve.wait_ge(landed[h], i * 32 + 32)
                    nc.vector.tensor_scalar(hot_t[:, h, :], blks[:, h, :], g.iota_part[0:B, 0:1], None, ALU.is_equal).then_inc(hot_ready, 1)
                    nc.vector.tensor_copy(start_ring[:, h, :].rearrange("b (t a) -> b t a", a=B), g.start[:, cols, :]).then_inc(hot_ready, 1)
                    for j in range(C2):
                        ins = nc.vector.scalar_tensor_tensor(
                            out=keys[:, h, j * P:(j + 1) * P], in0=keys[:, h, j * P:(j + 1) * P], scalar=g.key_col[:, bass.ds(q * C2 + j, 1)],
                            in1=g.earlier[:, :], op0=ALU.is_equal, op1=ALU.mult, accum_out=rank[:, j:j + 1])
                    ins.then_inc(spread_free, 1)
                    dve.wait_ge(spread_free, q + 3)
                    dve.wait_ge(looked, q + 1)
                    for k in range(2):
                        hot = g.src_hot[:, bass.ds(q * C2 + k * CH, CH), :]
                        nc.vector.tensor_tensor(picked[:, k * CH:(k + 1) * CH, :],
                                                look_ps[:, 2 * h + k, 0:CH * B].rearrange("p (t a) -> p t a", a=B),
                                                hot, ALU.mult)
                        ins = nc.vector.tensor_tensor(shifted[:, k * CH:(k + 1) * CH, :],
                                                      shift_ps[:, 2 * h + k, 0:CH * B].rearrange("p (t a) -> p t a", a=B),
                                                      hot, ALU.mult)
                    ins.then_inc(look_free, 1)
                    dve.wait_ge(look_free, q + 3)
                    step(nc.vector.tensor_reduce(base[:, :], picked[:, :, :], AX.X, ALU.add))
                    step(nc.vector.tensor_tensor(slot_i[:, 0, :], base[:, :], rank[:, :], ALU.add))
                    step(nc.vector.tensor_scalar(slot_i[:, 1, :], slot_i[:, 0, :], 7, None, ALU.arith_shift_right))
                    step(nc.vector.tensor_scalar(slot_i[:, 2, :], slot_i[:, 0, :], P - 1, None, ALU.bitwise_and))
                    step(nc.vector.scalar_tensor_tensor(out=row_f[:, :], in0=slot_i[:, 2, :], scalar=float(S.tiles),
                                                        in1=slot_i[:, 1, :], op0=ALU.mult, op1=ALU.add))
                    step(nc.vector.tensor_scalar(off[:, :], g.key_col[:, cols], 0.0, no_slot, ALU.is_lt, ALU.mult))
                    step(nc.vector.tensor_reduce(shift[:, :], shifted[:, :, :], AX.X, ALU.add))
                    step(nc.vector.tensor_tensor(dslot_i[:, 0, :], slot_i[:, 0, :], shift[:, :], ALU.add))
                    step(nc.vector.tensor_scalar(dslot_i[:, 1, :], dslot_i[:, 0, :], 7, None, ALU.arith_shift_right))
                    step(nc.vector.tensor_scalar(dslot_i[:, 2, :], dslot_i[:, 0, :], P - 1, None, ALU.bitwise_and))
                    step(nc.vector.scalar_tensor_tensor(out=drow_f[:, :], in0=dslot_i[:, 2, :], scalar=float(S.dst_tiles),
                                                        in1=dslot_i[:, 1, :], op0=ALU.mult, op1=ALU.add))
                    nc.vector.tensor_tensor(g.dst_index[:, cols], drow_f[:, :], off[:, :], ALU.add)
                    since(dve, ring_free, q)
                    nc.vector.tensor_copy(rec_ring[:, h, :, :], g.rec[:, cols, :]).then_inc(indexed, 1)
                    step(nc.vector.tensor_tensor(index[:, h, :], row_f[:, :], off[:, :], ALU.add))
                    assert steps[0] == NS

            rounds(dve, NCH // 2, pair)

        @block.gpsimd
        def _(pool):
            last_row = pool.to_reg(S.tiles * P - 1)

            def pair(i):
                for h in range(2):
                    q = i * 2 + h
                    since(pool, sent, q * (16 * C2))
                    pool.wait_ge(indexed, q + 1)
                    pool.wait_ge(own, q * NS + NS)
                    pool.sem_inc(ring_free, 1)
                    for j in range(C2):
                        nc.gpsimd.indirect_dma_start(
                            out=g.slots[:, :], out_offset=bass.IndirectOffsetOnAxis(ap=index[:, h, j:j + 1], axis=0),
                            in_=rec_ring[:, h, j, :], in_offset=None, bounds_check=last_row, oob_is_err=False,
                        ).then_inc(sent, 16)

            rounds(pool, NCH // 2, pair)
            pool.wait_ge(sent, NCH * 16 * C2)


def load_slots(nc, g, S):
    with ExitStack() as ctx:
        landed = ctx.enter_context(semaphore(nc, "slots_landed"))
        block = ctx.enter_context(nc.Block())

        @block.sync
        def _(sp):
            sp.dma_start(g.recs[:, :, :].rearrange("p t f -> p (t f)"),
                         g.slots[:, :].rearrange("(p t) f -> p (t f)", p=P)).then_inc(landed, 16)
            sp.wait_ge(landed, 16)


def send_by_dst(nc, g, S, pool, C2, rec_stage, index_stage, sent, copied, begun):
    last_row = pool.to_reg(S.dst_tiles * P - 1)

    def chunk(i):
        since(pool, sent, i * (16 * C2))
        cols = bass.ds(i * C2, C2)
        nc.gpsimd.tensor_copy(rec_stage[:, :, :], g.rec[:, cols, :]).then_inc(copied, 1)
        nc.gpsimd.tensor_copy(index_stage[:, :], g.dst_index[:, cols]).then_inc(copied, 1)
        pool.wait_ge(copied, i * 2 + 2)
        pool.sem_inc(begun, 1)
        for j in range(C2):
            nc.gpsimd.indirect_dma_start(
                out=g.dst_slots[:, :], out_offset=bass.IndirectOffsetOnAxis(ap=index_stage[:, j:j + 1], axis=0),
                in_=rec_stage[:, j, :], in_offset=None, bounds_check=last_row, oob_is_err=False,
            ).then_inc(sent, 16)

    rounds(pool, S.in_tiles // C2, chunk)
    pool.wait_ge(sent, S.in_tiles * 16)


def numbers(nc, engine, ap, top):
    _, values = nc.values_load_multi_w_load_instructions(
        ap, engines=[engine], min_val=0, max_val=top,
        skip_runtime_bounds_check_because="stage 3 makes the row from counts of buckets, all of them in this range")
    return values


def build_matrices(nc, g, S):
    B, NT, U = S.blocks, S.tiles, S.body
    H = U // 2
    with ExitStack() as ctx:
        sb = lambda name, shape, dt=F32: ctx.enter_context(nc.sbuf_tensor(name, shape, dt))
        sem = lambda name: ctx.enter_context(semaphore(nc, name))
        src_hot = sb("src_hot_e", [P, U, P])
        dst_hot = sb("dst_hot_e", [P, U, P + 2])
        wsrc_hot = sb("wsrc_hot_e", [P, U, P + 1])
        done = sb("block_done", [P, U, 2, P])
        ps = ctx.enter_context(nc.psum_tensor("block_ps", [P, U, 512], F32))
        hot = sem("hots_ready")
        columns = sem("weight_columns_ready")
        weighed = sem("weights_on_hot")
        mult = sem("blocks_multiplied")
        ready = sem("blocks_ready")
        summed = sem("sums_taken")
        zero = sem("sums_zeroed")
        out = [sem(f"block_out_{s}") for s in range(U)]
        C2 = 2 * S.rank_half
        rec_stage = sb("rec_stage", [P, C2, S.rec])
        index_stage = sb("index_stage", [P, C2], U32)
        copied = sem("records_staged")
        begun = sem("chunk_begun")
        block = ctx.enter_context(nc.Block())

        @block.gpsimd
        def _(pool):
            send_by_dst(nc, g, S, pool, C2, rec_stage, index_stage, g.sent, copied, begun)

        @block.vector
        def _(dve):
            nc.vector.memset(done[:, U - 1, :, :], 0.0).then_inc(zero, 1)
            nc.vector.memset(wsrc_hot[:, :, P:P + 1], 1.0).then_inc(zero, 1)
            dve.wait_ge(zero, 2)

            def make(i, h):
                def step(field, to, k):
                    tiles = bass.ds(i * U + (h * H + k), H // 2)
                    since(dve, mult, (i - 1) * U + h * H + H)
                    nc.vector.tensor_tensor(to[:, h * H + k:h * H + k + H // 2, 0:P],
                                            g.iota_free[:, :].unsqueeze(1).broadcast_to([P, H // 2, P]),
                                            g.recs[:, tiles, field].unsqueeze(2).broadcast_to([P, H // 2, P]),
                                            ALU.is_equal).then_inc(hot, 1)

                return [lambda f=f, to=to, k=k: step(f, to, k) for f, to in ((0, src_hot), (1, dst_hot)) for k in (0, H // 2)]

            def take(i, h, between):
                for k in range(H):
                    s = h * H + k
                    n = i * U + s
                    dve.wait_ge(mult, n + 1)
                    since(dve, out[s], i * 16)
                    since(dve, ready, n)
                    both = ps[:, s, :].rearrange("p (t c) -> p t c", t=2)[:, :, 0:P]
                    nc.vector.scalar_tensor_tensor(out=done[:, s, :, :], in0=done[:, (s - 1) % U, :, :],
                                                   scalar=g.same[:, bass.ds(n, 1)], in1=both,
                                                   op0=ALU.mult, op1=ALU.add).then_inc(ready, 1)
                    if between:
                        between[k]()

            for h in range(2):
                for step in make(0, h):
                    step()

            def eight(i):
                take(i, 0, make(i + 1, 0))
                take(i, 1, make(i + 1, 1))

            eight(0)
            with dve.Fori(1, NT // U - 1) as i:
                eight(i)
            take(NT // U - 1, 0, ())
            take(NT // U - 1, 1, ())

        @block.scalar
        def _(act):
            def weigh(i, h):
                act.wait_ge(hot, i * 8 + h * 4 + 2)
                nc.scalar.copy(dst_hot[:, h * H:(h + 1) * H, P:P + 2], g.recs[:, bass.ds(i * U + h * H, H), 2:4]).then_inc(columns, 1)
                for k in range(H):
                    s = h * H + k
                    nc.scalar.activation(wsrc_hot[:, s, 0:P], src_hot[:, s, :], ACT.Copy,
                                         scale=g.recs[:, bass.ds(i * U + s, 1), 2]).then_inc(weighed, 1)

            def take_sums(i, h):
                act.wait_ge(ready, i * U + h * H + H)
                tiles = bass.ds(i * U + h * H, H)
                four = slice(h * H, (h + 1) * H)
                nc.scalar.copy(g.sums[:, 0:2, tiles], ps[:, four, P:P + 2].rearrange("p n c -> p c n")).then_inc(summed, 1)
                nc.scalar.copy(g.sums[:, 2, tiles], ps[:, four, 3 * P]).then_inc(summed, 1)

            def eight(i):
                for h in range(2):
                    weigh(i + 1, h)
                    take_sums(i, h)

            weigh(0, 0)
            weigh(0, 1)
            rounds(act, NT // U - 1, eight)
            take_sums(NT // U - 1, 0)
            take_sums(NT // U - 1, 1)

        @block.tensor
        def _(pe):
            pe.wait_ge(zero, 2)

            def eight(i):
                for h in range(2):
                    pe.wait_ge(hot, i * 8 + h * 4 + 4)
                    pe.wait_ge(columns, i * 2 + h + 1)
                    since(pe, ready, (i - 1) * U + h * H + H)
                    since(pe, summed, (i - 1) * 4 + h * 2 + 2)
                    for s in range(h * H, (h + 1) * H):
                        n = i * U + s
                        nc.tensor.matmul(ps[:, s, 0:P + 2], src_hot[:, s, :], dst_hot[:, s, :], start=True, stop=True)
                        pe.wait_ge(weighed, n + 1)
                        nc.tensor.matmul(ps[:, s, 2 * P:3 * P + 1], dst_hot[:, s, 0:P], wsrc_hot[:, s, :],
                                         start=True, stop=True).then_inc(mult, 1)

            rounds(pe, NT // U, eight)

        @block.sync
        def _(sp):
            with sp.Fori(0, NT // U) as i:
                for h in range(2):
                    places = numbers(nc, mybir.EngineType.SP, g.tab[0:1, bass.ds(i * U + h * H, H)], B * B + U)
                    for k in range(H):
                        s = h * H + k
                        sp.wait_ge(ready, i * U + s + 1)
                        sp.dma_start(g.blocks[bass.ds(places[k] * P, P), :],
                                     done[:, s, :, :].rearrange("p k c -> p (k c)")).then_inc(out[s], 16)
            for s in range(U):
                sp.wait_ge(out[s], 16 * (NT // U))


def degrees(nc, g, S):
    B, NT = S.blocks, S.tiles
    NC = -(-NT // P)
    with ExitStack() as ctx:
        sb = lambda name, shape, dt=F32: ctx.enter_context(nc.sbuf_tensor(name, shape, dt))
        sem = lambda name: ctx.enter_context(semaphore(nc, name))
        hots = sb("tile_blk_hot", [P, 2, NC, B])
        by_tile = sb("sums_by_tile", [P, NC, 3, P])
        turn_ps = ctx.enter_context(nc.psum_tensor("sums_ps", [P, 4, 512], F32))
        deg_ps = ctx.enter_context(nc.psum_tensor("degrees_ps", [P, 3, 512], F32))
        turned = sem("sums_turned")
        kept = sem("sums_kept")
        added = sem("degrees_added")
        tiles = lambda c: min(P, NT - c * P)
        block = ctx.enter_context(nc.Block())

        @block.tensor
        def _(pe):
            for c in range(NC):
                n = tiles(c)
                since(pe, kept, c - 3)
                for k in range(3):
                    mm = nc.tensor.transpose(turn_ps[0:n, c % 4, k * P:(k + 1) * P], g.sums[:, k, c * P:c * P + n], g.ident[:, :])
                mm.then_inc(turned, 1)
            pe.wait_ge(kept, NC + 1)
            for k, end in ((0, 0), (1, 0), (2, 1)):
                for c in range(NC):
                    n = tiles(c)
                    mm = nc.tensor.matmul(deg_ps[:, k, 0:B], by_tile[0:n, c, k, :], hots[0:n, end, c, :],
                                          start=(c == 0), stop=(c == NC - 1))
            mm.then_inc(added, 1)

        @block.vector
        def _(dve):
            for c in range(NC):
                dve.wait_ge(turned, c + 1)
                n = tiles(c)
                nc.vector.tensor_copy(by_tile[0:n, c, :, :].rearrange("p k n -> p (k n)"), turn_ps[0:n, c % 4, 0:3 * P]).then_inc(kept, 1)
            nc.vector.tensor_tensor(hots[:, :, :, :], g.tile_blk[:, :, 0:NC].unsqueeze(3).broadcast_to([P, 2, NC, B]),
                                    g.iota_free[:, 0:B].unsqueeze(1).unsqueeze(1).broadcast_to([P, 2, NC, B]),
                                    ALU.is_equal).then_inc(kept, 1)
            dve.wait_ge(added, 1)
            nc.vector.tensor_copy(g.deg[:, :, :].rearrange("p b k -> p k b"), deg_ps[:, :, 0:B])


def load_features(nc, g, S):
    with ExitStack() as ctx:
        zero = ctx.enter_context(semaphore(nc, "x_zeroed"))
        landed = ctx.enter_context(semaphore(nc, "x_landed"))
        block = ctx.enter_context(nc.Block())
        full = (S.blocks - 1) * P

        @block.vector
        def _(dve):
            nc.vector.memset(g.x[:, S.blocks - 1, :], 0.0).then_inc(zero, 1)

        @block.sync
        def _(sp):
            sp.wait_ge(zero, 1)
            sp.dma_start(g.x[:, 0:S.blocks - 1, :], g.x_in[0:full, :].rearrange("(b p) d -> p b d", p=P)).then_inc(landed, 16)
            sp.dma_start(g.x[0:S.last_rows, S.blocks - 1, :], g.x_in[full:S.n, :]).then_inc(landed, 16)
            sp.wait_ge(landed, 32)


def spread(ap, n):
    return ap.unsqueeze(2).broadcast_to([ap.shape[0], ap.shape[1], n])


def degree_scales(nc, g, S):
    B = S.blocks
    with ExitStack() as ctx:
        sb = lambda name, shape, dt=F32: ctx.enter_context(nc.sbuf_tensor(name, shape, dt))
        sem = lambda name: ctx.enter_context(semaphore(nc, name))
        clipped = sb("clipped", [P, 3, B])
        root = sb("root", [P, 3, B])
        inv = sb("inverse_root", [P, 3, B])
        there = sb("has_weight", [P, B])
        own = sem("scale_steps")
        clip_ready = sem("clipped_ready")
        most = sb("most_of_place", [P, 1])
        most_ps = ctx.enter_context(nc.psum_tensor("most_ps", [P, 512], F32))
        most_ready = sem("most_ready")
        most_turned = sem("most_turned")
        root_ready = sem("roots_ready")
        block = ctx.enter_context(nc.Block())

        @block.scalar
        def _(act):
            act.wait_ge(clip_ready, 1)
            nc.scalar.activation(root[:, :, :], clipped[:, :, :], ACT.Sqrt).then_inc(root_ready, 1)

        @block.vector
        def _(dve):
            steps = [0]

            def step(ins):
                steps[0] += 1
                ins.then_inc(own, 1)
                dve.wait_ge(own, steps[0])

            step(nc.vector.tensor_scalar(clipped[:, 0, :], g.deg[:, 0:B, 1], 1.0, None, ALU.max))
            step(nc.vector.tensor_scalar(clipped[:, 1, :], g.deg[:, 0:B, 2], 1.0, None, ALU.max))
            step(nc.vector.tensor_scalar(there[:, :], g.deg[:, 0:B, 0], 0.0, None, ALU.is_gt))
            step(nc.vector.tensor_tensor(clipped[:, 2, :], g.deg[:, 0:B, 0], there[:, :], ALU.mult))
            nc.vector.scalar_tensor_tensor(out=clipped[:, 2, :], in0=clipped[:, 2, :], scalar=1.0, in1=there[:, :],
                                           op0=ALU.add, op1=ALU.subtract).then_inc(clip_ready, 1)
            dve.wait_ge(root_ready, 1)
            step(nc.vector.reciprocal(inv[:, :, :], root[:, :, :]))
            step(nc.vector.tensor_tensor(g.w_inv[:, :], inv[:, 2, :], there[:, :], ALU.mult))
            step(nc.vector.tensor_scalar(g.hop_last[:, :], inv[:, 1, :], S.keep, None, ALU.mult))
            step(nc.vector.tensor_tensor(g.hop[:, :], g.hop_last[:, :], inv[:, 0, :], ALU.mult))
            step(nc.vector.tensor_tensor(g.hs[:, :, :], g.x[:, :, :], spread(inv[:, 0, :], D), ALU.mult))
            step(nc.vector.tensor_scalar(g.rest[:, :, :], g.hs[:, :, :], 1.0 - S.keep, None, ALU.mult))
            nc.vector.tensor_reduce(most[:, :], g.deg[:, 0:B, 1], AX.X, ALU.max).then_inc(most_ready, 1)
            dve.wait_ge(most_turned, 1)
            step(nc.vector.tensor_reduce(g.most[:, :], most_ps[0:1, 0:P], AX.X, ALU.max))

        @block.tensor
        def _(pe):
            pe.wait_ge(most_ready, 1)
            nc.tensor.transpose(most_ps[0:1, 0:P], most[:, :], g.ident[:, :]).then_inc(most_turned, 1)


def sweeps(nc, g, S, name, matrix, repeats, places, finish, clear_diagonal=False):
    B = S.blocks
    RING = S.ring
    with ExitStack() as ctx:
        sem = lambda n: ctx.enter_context(semaphore(nc, f"{name}_{n}"))
        rows = ctx.enter_context(nc.sbuf_tensor(f"{name}_rows", [P, RING, B * P], F32))
        prod = ctx.enter_context(nc.sbuf_tensor(f"{name}_product", [D, RING, P], F32))
        prod_ps = ctx.enter_context(nc.psum_tensor(f"{name}_product_ps", [D, RING, 512], F32))
        back_ps = ctx.enter_context(nc.psum_tensor(f"{name}_back_ps", [P, 3, 512], F32))
        prod_at = lambda s: prod_ps[:, s, 0:P]
        back_at = lambda s: back_ps[:, s % 3, 0:D]
        landed = [sem(f"row_landed_{s}") for s in range(RING)]
        free = sem("row_free")
        cleared = sem("diagonal_cleared")
        summed = sem("product_summed")
        copied = sem("product_copied")
        turned = sem("product_turned")
        begun = sem("turn_begun")
        block = ctx.enter_context(nc.Block())
        NP = len(places)

        @block.sync
        def _(sp):
            with sp.Fori(0, repeats) as r:
                for p in range(NP):
                    with sp.Fori(0, B // RING) as i:
                        for s in range(RING):
                            n = (r * NP + p) * B + i * RING + s
                            sp.wait_ge(free, n + 1)
                            row = matrix[bass.ds(i * RING + s, 1)].rearrange("o p b c -> (o p) b c")
                            sp.dma_start(rows[:, s, :].rearrange("p (b c) -> p b c", c=P), row).then_inc(landed[s], 16)

        @block.tensor
        def _(pe):
            def turn(n, s):
                pe.wait_ge(free, n + RING - 1)
                pe.wait_ge(copied, n + 1)
                pe.sem_inc(begun, 1)
                nc.tensor.transpose(back_at(s), prod[:, s, :], g.ident[0:D, 0:D]).then_inc(turned, 1)

            with pe.Fori(0, repeats) as r:
                for p in range(NP):
                    h = places[p][0]
                    with pe.Fori(0, B // RING) as i:
                        for s in range(RING):
                            n = (r * NP + p) * B + i * RING + s
                            pe.wait_ge(landed[s], (r * NP + p) * (16 * B // RING) + i * 16 + 16)
                            pe.wait_ge(free, n + 1)
                            if s == 0:
                                pe.wait_ge(free, (r * NP + p) * B + RING)
                            if clear_diagonal:
                                pe.wait_ge(cleared, n + 1)
                            for k in range(B):
                                mm = nc.tensor.matmul(prod_at(s), h[:, k, :], rows[:, s, k * P:(k + 1) * P],
                                                      start=(k == 0), stop=(k == B - 1))
                            mm.then_inc(summed, 1)
                            if s:
                                turn(n - 1, s - 1)
                        turn(n, s)

        @block.scalar
        def _(act):
            with act.Fori(0, repeats * NP * B // RING) as i:
                for s in range(RING):
                    act.wait_ge(summed, i * RING + s + 1)
                    nc.scalar.copy(prod[:, s, :], prod_at(s)).then_inc(copied, 1)

        @block.vector
        def _(dve):
            dve.sem_inc(free, RING)
            with dve.Fori(0, repeats) as r:
                for p in range(NP):
                    with dve.Fori(0, B // RING) as i:
                        def clear(s):
                            if clear_diagonal:
                                dve.wait_ge(landed[s], (r * NP + p) * (16 * B // RING) + i * 16 + 16)
                                own_block = rows[:, s, bass.ds((i * RING + s) * P, P)]
                                nc.vector.tensor_tensor(own_block, own_block, g.off_diagonal[:, :], ALU.mult).then_inc(cleared, 1)

                        clear(0)
                        for s in range(RING):
                            n = (r * NP + p) * B + i * RING + s
                            if s + 1 < RING:
                                clear(s + 1)
                            dve.wait_ge(turned, n + 1)
                            finish(p, i * RING + s, back_at(s)).then_inc(free, 1)


def node(ap, m):
    return ap[:, bass.ds(m, 1), :].rearrange("p o d -> p (o d)")


def node_scale(ap, m):
    return ap[:, bass.ds(m, 1)]


def hops_from_dram(nc, g, S):
    with ExitStack() as ctx:
        other = ctx.enter_context(nc.sbuf_tensor("hs_other", [P, S.blocks, D], F32))
        rest_last = ctx.enter_context(nc.sbuf_tensor("rest_last", [P, S.blocks, D], F32))
        hs = [g.hs, other]
        with nc.Block() as block:
            @block.vector
            def _(dve):
                nc.vector.tensor_scalar(rest_last[:, :, :], g.x[:, :, :], 1.0 - S.keep, None, ALU.mult)

        def even_odd(p, m, product):
            return nc.vector.scalar_tensor_tensor(out=node(hs[1 - p], m), in0=product, scalar=node_scale(g.hop, m),
                                                  in1=node(g.rest, m), op0=ALU.mult, op1=ALU.add)

        def last(p, m, product):
            if p == 0:
                return even_odd(p, m, product)
            return nc.vector.scalar_tensor_tensor(out=node(g.hs, m), in0=product, scalar=node_scale(g.hop_last, m),
                                                  in1=node(rest_last, m), op0=ALU.mult, op1=ALU.add)

        pairs = [(hs[0], hs[1]), (hs[1], hs[0])]
        sweeps(nc, g, S, "hop", g.counts, S.hops // 2 - 1, pairs, even_odd)
        sweeps(nc, g, S, "lasthop", g.counts, 1, pairs, last)


def hops_on_chip(nc, g, S):
    B, G = S.blocks, S.ring
    NG = B // G
    with ExitStack() as ctx:
        counts = ctx.enter_context(nc.sbuf_tensor("counts_on_chip", [P, B, B * P], BF16))
        half = B * P // 2
        with ExitStack() as ctx2:
            stage = ctx2.enter_context(nc.sbuf_tensor("counts_stage", [P, 2, B * P], F32))
            landed = [ctx2.enter_context(semaphore(nc, f"counts_landed_{s}")) for s in range(2)]
            by_act = ctx2.enter_context(semaphore(nc, "left_half_converted"))
            by_dve = ctx2.enter_context(semaphore(nc, "right_half_converted"))
            block = ctx2.enter_context(nc.Block())

            @block.sync
            def _(sp):
                for m in range(B):
                    since(sp, by_act, m - 1)
                    since(sp, by_dve, m - 1)
                    sp.dma_start(stage[:, m % 2, :].rearrange("p (b c) -> p b c", c=P), g.counts[m]).then_inc(landed[m % 2], 16)

            @block.scalar
            def _(act):
                for m in range(B):
                    act.wait_ge(landed[m % 2], m // 2 * 16 + 16)
                    nc.scalar.copy(counts[:, m, 0:half], stage[:, m % 2, 0:half]).then_inc(by_act, 1)

            @block.vector
            def _(dve):
                for m in range(B):
                    dve.wait_ge(landed[m % 2], m // 2 * 16 + 16)
                    nc.vector.tensor_copy(counts[:, m, half:], stage[:, m % 2, half:]).then_inc(by_dve, 1)

        sb = lambda n, shape, dt=F32: ctx.enter_context(nc.sbuf_tensor(n, shape, dt))
        sem = lambda n: ctx.enter_context(semaphore(nc, n))
        parts = [sb("parts_even", [P, B, 3, D], BF16), sb("parts_odd", [P, B, 3, D], BF16)]
        total = sb("hop_total", [P, G, D])
        left = sb("hop_left", [P, G, D])
        rest = sb("hop_rest", [P, G, D])
        ps = ctx.enter_context(nc.psum_tensor("hop_ps", [P, 8 * 512], F32))
        summed = sem("block_summed")
        read = sem("group_read")
        h_done = sem("group_split")
        own = sem("hop_steps")
        first = sem("first_split_steps")
        block = ctx.enter_context(nc.Block())

        def place(m):
            return slice(m * 256, m * 256 + 3 * D)

        @block.tensor
        def _(pe):
            with pe.Fori(0, S.hops // 2) as r:
                for p in range(2):
                    for q in range(NG):
                        n = (r * 2 + p) * NG + q
                        pe.wait_ge(read, n + 1)
                        for m in range(G):
                            for k in range(B):
                                if q == 0 and m == 0 and k % G == 0:
                                    pe.wait_ge(h_done, n + k // G + 1)
                                mm = nc.tensor.matmul(ps[:, place(m + (p + q) % 2 * 8)],
                                                      counts[:, q * G + m, k * P:(k + 1) * P],
                                                      parts[p][:, k, :, :].rearrange("p t d -> p (t d)"),
                                                      start=(k == 0), stop=(k == B - 1))
                            mm.then_inc(summed, 1)

        @block.vector
        def _(dve):
            NS = 6

            def split(value, to, step):
                step(nc.vector.tensor_copy(to[:, :, 0, :], value))
                step(nc.vector.tensor_tensor(left[:, :, :], value, to[:, :, 0, :], ALU.subtract))
                step(nc.vector.tensor_copy(to[:, :, 1, :], left[:, :, :]))
                step(nc.vector.tensor_tensor(left[:, :, :], left[:, :, :], to[:, :, 1, :], ALU.subtract))
                nc.vector.tensor_copy(to[:, :, 2, :], left[:, :, :]).then_inc(h_done, 1)

            steps = [0]

            def first_step(ins):
                steps[0] += 1
                ins.then_inc(first, 1)
                dve.wait_ge(first, steps[0])

            dve.sem_inc(read, 2)
            for q in range(NG):
                since(dve, h_done, q)
                split(g.hs[:, q * G:(q + 1) * G, :], parts[0][:, q * G:(q + 1) * G, :, :], first_step)

            def group(w, p, q, last=False):
                n = w * NG + q
                steps[0] = 0

                def step(ins):
                    steps[0] += 1
                    ins.then_inc(own, 1)
                    before = (S.hops - 1) * NG * NS + q * 2 if last else n * NS
                    dve.wait_ge(own, before + steps[0])

                blocks = slice(q * G, (q + 1) * G)
                dve.wait_ge(h_done, n + NG)
                dve.wait_ge(summed, n * G + G)
                places = ps[:, (p + q) % 2 * 2048:(p + q) % 2 * 2048 + G * 256].rearrange("p (m c) -> p m c", c=256)
                nc.vector.tensor_reduce(total[:, :, :], places[:, :, 0:3 * D].rearrange("p m (t d) -> p m d t", d=D),
                                        AX.X, ALU.add).then_inc(read, 1)
                dve.wait_ge(read, n + 3)
                scale = g.hop_last if last else g.hop
                step(nc.vector.tensor_tensor(total[:, :, :], total[:, :, :], spread(scale[:, blocks], D), ALU.mult))
                if last:
                    step(nc.vector.tensor_scalar(rest[:, :, :], g.x[:, blocks, :], 1.0 - S.keep, None, ALU.mult))
                    nc.vector.tensor_tensor(g.hs[:, blocks, :], total[:, :, :], rest[:, :, :], ALU.add).then_inc(h_done, 1)
                    return
                step(nc.vector.tensor_tensor(total[:, :, :], total[:, :, :], g.rest[:, blocks, :], ALU.add))
                split(total[:, :, :], parts[1 - p][:, blocks, :, :], step)

            def sweep(w, p, last=False):
                for q in range(NG):
                    group(w, p, q, last)

            def pair(r):
                sweep(r * 2, 0)
                sweep(r * 2 + 1, 1)

            rounds(dve, S.hops // 2 - 1, pair)
            sweep(S.hops - 2, 0)
            sweep(S.hops - 1, 1, last=True)


def enter_branch(nc):
    with semaphore(nc, "branch_entered") as entered, nc.Block() as block:
        @block.sync
        def _(sp):
            sp.sem_inc(entered, 1)

        @block.tensor
        def _(pe):
            pe.sem_inc(entered, 1)

        @block.scalar
        def _(act):
            act.sem_inc(entered, 1)

        @block.vector
        def _(dve):
            dve.sem_inc(entered, 1)

        @block.gpsimd
        def _(pool):
            pool.sem_inc(entered, 1)


def hops(nc, g, S):
    most = nc.values_load(g.most[0:1, 0:1], min_val=0, max_val=S.e,
                          skip_runtime_bounds_check_because="a count of edges")
    with nc.If(most > 256):
        enter_branch(nc)
        hops_from_dram(nc, g, S)
    with nc.Else():
        enter_branch(nc)
        hops_on_chip(nc, g, S)


def layer_norm(nc, g, S, name, z_in, out, before=None, after=None):
    B = S.blocks
    with ExitStack() as ctx:
        sb = lambda n, shape, dt=F32: ctx.enter_context(nc.sbuf_tensor(f"{name}_{n}", shape, dt))
        sem = lambda n: ctx.enter_context(semaphore(nc, f"{name}_{n}"))
        mean = sb("mean", [P, B])
        var = sb("var", [P, B])
        root = sb("root", [P, B])
        inv = sb("inv", [P, B])
        sq = sb("squares", [P, B, D])
        own = sem("steps")
        var_ready = sem("variance_ready")
        root_ready = sem("root_ready")
        block = ctx.enter_context(nc.Block())

        @block.scalar
        def _(act):
            act.wait_ge(var_ready, 1)
            nc.scalar.activation(root[:, :], var[:, :], ACT.Sqrt).then_inc(root_ready, 1)

        @block.vector
        def _(dve):
            steps = [0]

            def step(ins):
                steps[0] += 1
                ins.then_inc(own, 1)
                dve.wait_ge(own, steps[0])

            if before:
                before(step)
            step(nc.vector.tensor_reduce(mean[:, :], z_in[:, :, :], AX.X, ALU.add))
            step(nc.vector.tensor_scalar(mean[:, :], mean[:, :], 1.0 / D, None, ALU.mult))
            step(nc.vector.tensor_tensor(out[:, :, :], z_in[:, :, :], spread(mean[:, :], D), ALU.subtract))
            step(nc.vector.tensor_tensor(sq[:, :, :], out[:, :, :], out[:, :, :], ALU.mult))
            step(nc.vector.tensor_reduce(var[:, :], sq[:, :, :], AX.X, ALU.add))
            nc.vector.tensor_scalar(var[:, :], var[:, :], 1.0 / D, S.eps, ALU.mult, ALU.add).then_inc(var_ready, 1)
            dve.wait_ge(root_ready, 1)
            step(nc.vector.reciprocal(inv[:, :], root[:, :]))
            step(nc.vector.tensor_tensor(out[:, :, :], out[:, :, :], spread(inv[:, :], D), ALU.mult))
            if after:
                after(step)


def first_layers(nc, g, S):
    B = S.blocks
    with ExitStack() as ctx:
        sb = lambda name, shape, dt=F32: ctx.enter_context(nc.sbuf_tensor(name, shape, dt))
        g.rest = sb("rest", [P, B, D])
        g.hs = sb("hs", [P, B, D])
        g.hop = sb("hop", [P, B])
        g.hop_last = sb("hop_last", [P, B])
        g.most = sb("most", [1, 1], I32)
        eps1 = sb("one_plus_eps", [P, 1])
        degree_scales(nc, g, S)
        hops(nc, g, S)

        def add_x(step):
            step(nc.vector.tensor_tensor(g.hs[:, :, :], g.hs[:, :, :], g.x[:, :, :], ALU.add))

        layer_norm(nc, g, S, "norm0", g.hs, g.x, add_x)
        with semaphore(nc, "eps_landed") as landed, nc.Block() as block:
            @block.sync
            def _(sp):
                sp.dma_start(eps1[:, :], g.eps1_in[:].unsqueeze(0).broadcast_to([P, 1])).then_inc(landed, 16)

            @block.vector
            def _(dve):
                dve.wait_ge(landed, 16)
                nc.vector.tensor_scalar(eps1[:, :], eps1[:, :], 1.0, None, ALU.add)

        def neighbours(p, m, product):
            return nc.vector.scalar_tensor_tensor(out=node(g.hs, m), in0=node(g.x, m), scalar=eps1[:, 0:1],
                                                  in1=product, op0=ALU.mult, op1=ALU.add)

        sweeps(nc, g, S, "weighted", g.weights, 1, [(g.x, g.hs)], neighbours, clear_diagonal=True)
        layer_norm(nc, g, S, "norm1", g.hs, g.x, add_x)


def split_slots(nc, g, S):
    ND, R, F = S.dst_tiles, S.rec, S.split
    G = 4
    N = ND // G
    RING = 10
    AHEAD = 5
    assert N % RING == 0 and RING % AHEAD == 0
    with ExitStack() as ctx:
        sb = lambda name, shape, dt=F32: ctx.enter_context(nc.sbuf_tensor(name, shape, dt))
        sem = lambda name: ctx.enter_context(semaphore(nc, name))
        recs = sb("dst_recs", [P, ND, R])
        left = sb("attr_left", [P, ND, 3])
        parts = sb("split_records", [P, ND, F], BF16)
        ident_b = sb("ident_b", [P, P], BF16)
        node_f = sb("src_node_f", [P, ND])
        taken = sb("records_taken", [P, AHEAD, G * R])
        taken_b = sb("split_taken", [P, AHEAD, G * F], BF16)
        out = sb("attr_turned", [G * R, RING, P])
        out_b = sb("split_turned", [G * F, RING, P], BF16)
        ps = ctx.enter_context(nc.psum_tensor("records_ps", [P, 2, 512], F32))
        ps_b = ctx.enter_context(nc.psum_tensor("split_ps", [P, 2, 1024], BF16))
        landed = sem("dst_records_landed")
        own = sem("split_steps")
        parted = sem("records_parted")
        copied = sem("records_copied")
        tr = sem("records_transposed")
        ready = sem("turned_ready")
        ready_b = sem("split_turned_ready")
        stored = [sem(f"turned_stored_{k}") for k in range(RING)]
        stored_b = [sem(f"split_turned_stored_{k}") for k in range(RING)]
        block = ctx.enter_context(nc.Block())

        @block.sync
        def _(sp):
            sp.dma_start(recs[:, :, :].rearrange("p t f -> p (t f)"),
                         g.dst_slots[:, :].rearrange("(p t) f -> p (t f)", p=P)).then_inc(landed, 16)

            def ring(i):
                for k in range(RING):
                    n = i * RING + k
                    sp.wait_ge(ready, n + 1)
                    cols = bass.ds(n * (G * P), G * P)
                    sp.dma_start(g.attr_rows[:, cols].rearrange("f (t e) -> t f e", e=P), out[:, k, :]).then_inc(stored[k], 16)

            rounds(sp, N // RING, ring)
            for k in range(RING):
                sp.wait_ge(stored[k], N // RING * 16)
                sp.wait_ge(stored_b[k], N // RING * 16)

        @block.vector
        def _(dve):
            steps = [0]

            def step(ins):
                steps[0] += 1
                ins.then_inc(own, 1)
                dve.wait_ge(own, steps[0])

            nc.vector.memset(parts[:, :, S.split_used:F], 0.0)
            nc.vector.memset(parts[:, :, 1:4], 1.0)
            nc.vector.tensor_copy(ident_b[:, :], g.ident[:, :])
            dve.wait_ge(landed, 16)
            nc.vector.tensor_copy(parts[:, :, 0], recs[:, :, 1])
            step(nc.vector.tensor_scalar(node_f[:, :], recs[:, :, 7], 0.0, None, ALU.max))
            nc.vector.tensor_copy(g.src_node[:, :], node_f[:, :])
            hi, mid, low = parts[:, :, 4:7], parts[:, :, 7:10], parts[:, :, 10:13]
            step(nc.vector.tensor_copy(hi, recs[:, :, 4:7]))
            step(nc.vector.tensor_tensor(left[:, :, :], recs[:, :, 4:7], hi, ALU.subtract))
            step(nc.vector.tensor_copy(mid, left[:, :, :]))
            step(nc.vector.tensor_tensor(left[:, :, :], left[:, :, :], mid, ALU.subtract))
            nc.vector.tensor_copy(low, left[:, :, :])
            nc.vector.tensor_copy(parts[:, :, 13:19], parts[:, :, 4:10])
            nc.vector.tensor_copy(parts[:, :, 19:22], hi).then_inc(parted, 1)

            def ring(i):
                for k in range(RING):
                    h = k % 2
                    dve.wait_ge(tr, i * RING + k + 1)
                    since(dve, stored[k], i * 16)
                    since(dve, stored_b[k], i * 16)
                    nc.vector.tensor_copy(out[:, k, :], ps[0:G * R, h, 0:P]).then_inc(ready, 1)
                    nc.vector.tensor_copy(out_b[:, k, :], ps_b[:, h, 0:P]).then_inc(ready_b, 1)
                    tiles = bass.ds(i * (RING * G) + k * G, G)
                    nc.vector.tensor_tensor(g.dst_hot[:, tiles, :], g.iota_free[:, :].unsqueeze(1).broadcast_to([P, G, P]),
                                            recs[:, tiles, 1].unsqueeze(2).broadcast_to([P, G, P]), ALU.is_equal)

            rounds(dve, N // RING, ring)

        @block.scalar
        def _(act):
            act.wait_ge(parted, 1)

            def store(n, k):
                act.wait_ge(ready_b, n + 1)
                cols = bass.ds(n * (G * P), G * P)
                act.dma_start(g.split_rows[:, cols].rearrange("f (t e) -> t f e", e=P), out_b[:, k, :]).then_inc(stored_b[k], 16)

            def ring(i):
                for k in range(RING):
                    a = k % AHEAD
                    n = i * RING + k
                    since(act, tr, n - AHEAD + 1)
                    tiles = bass.ds(n * G, G)
                    nc.scalar.copy(taken[:, a, :].rearrange("p (t f) -> p t f", f=R), recs[:, tiles, :]).then_inc(copied, 1)
                    nc.scalar.copy(taken_b[:, a, :].rearrange("p (t f) -> p t f", f=F), parts[:, tiles, :]).then_inc(copied, 1)
                    if not isinstance(n, int) or n >= AHEAD:
                        store(n - AHEAD, (k - AHEAD) % RING)

            rounds(act, N // RING, ring)
            for k in range(RING - AHEAD, RING):
                store(N - RING + k, k)

        @block.tensor
        def _(pe):
            def ring(i):
                for k in range(RING):
                    h, a = k % 2, k % AHEAD
                    n = i * RING + k
                    pe.wait_ge(copied, n * 2 + 2)
                    since(pe, ready_b, n - 1)
                    nc.tensor.transpose(ps[0:G * R, h, 0:P], taken[:, a, :], g.ident[:, :])
                    nc.tensor.transpose(ps_b[:, h, 0:P], taken_b[:, a, :], ident_b[:, :]).then_inc(tr, 1)

            rounds(pe, N // RING, ring)


def node_tables(nc, g, S, l):
    B = S.blocks
    CH = [(c, min(4, B - c)) for c in range(0, B, 4)]
    with ExitStack() as ctx:
        sb = lambda name, shape, dt=F32: ctx.enter_context(nc.sbuf_tensor(f"l{l}_{name}", shape, dt))
        sem = lambda name: ctx.enter_context(semaphore(nc, f"l{l}_{name}"))
        h_t = sb("h_turned", [D, B * P])
        hx_t = sb("hx_turned", [D, B * P])
        w_att = sb("w_attention", [D, 2 * D])
        table = sb("table", [P, B, 3 * D])
        left = sb("left", [P, B, D])
        w_left = sb("w_left", [S.split_used, D])
        w_hi = sb("w_hi", [S.split_used, D], BF16)
        w_mid = sb("w_mid", [S.split_used, D], BF16)
        w_low = sb("w_low", [S.split_used, D], BF16)
        ps = lambda name, k: ctx.enter_context(nc.psum_tensor(f"l{l}_{name}", [P, k, 512], F32))
        t_ps, x_ps, n_ps = ps("turn_ps", 2), ps("hx_ps", 2), ps("table_ps", 4)
        landed = sem("weights_landed")
        node_landed = sem("node_weights_landed")
        e1_landed = sem("edge_weights_landed")
        zeroed = sem("weights_zeroed")
        turned = sem("h_turned")
        turned_sb = sem("h_turned_copied")
        hx = sem("hx_ready")
        hx_sb = sem("hx_copied")
        tab = sem("table_ready")
        tab_sb = sem("table_copied")
        tab_out = sem("table_stored")
        own = sem("node_steps")
        split_w = sem("edge_weights_split")
        placed = sem("edge_weights_placed")
        block = ctx.enter_context(nc.Block())

        @block.gpsimd
        def _(pool):
            nc.gpsimd.memset(g.w_edge[:, :], 0.0).then_inc(zeroed, 1)
            nc.gpsimd.memset(g.sums[:, :, :], 0.0)

        @block.sync
        def _(sp):
            def load(out, src, s=landed):
                sp.dma_start(out, src).then_inc(s, 16)
            row = lambda v: v.unsqueeze(0)
            load(g.w_node[:, :], g.W_node[l], node_landed)
            load(w_att[:, 0:D], g.Wa1[l, 0:D, :], node_landed)
            load(w_att[:, D:2 * D], g.Wa1[l, D:2 * D, :], node_landed)
            sp.wait_ge(zeroed, 2)
            for k in range(1, 4):
                load(g.w_e1[k:k + 1, :], row(g.b_e1[l]), e1_landed)
            for k in range(6):
                load(g.w_e1[4 + 3 * k:7 + 3 * k, :], g.W_e1[l], e1_landed)
            load(g.wa2[:, :], g.Wa2[l].rearrange("d o -> (d o)").unsqueeze(0).broadcast_to([P, D]))
            load(g.ba2[:, :], row(g.ba2_in[l]).broadcast_to([P, 1]))
            load(g.bias[:, :], row(g.bias_in[l]).broadcast_to([P, D]))
            load(g.ln_g[:, :], row(g.ln_g_in[l]).broadcast_to([P, D]))
            load(g.ln_b[:, :], row(g.ln_b_in[l]).broadcast_to([P, D]))
            load(g.w_edge[0:D, D:2 * D], g.W_e2[l])
            load(g.w_edge[D:D + 1, D:2 * D], row(g.b_e2[l]))
            load(g.w_edge[D:D + 1, 0:D], row(g.ba1[l]))
            load(g.w_edge[D + 1:D + 4, 0:D], g.Wa1[l, 2 * D:2 * D + 3, :])
            sp.wait_ge(split_w, 3)
            for part, rows in ((w_hi, (1, 2)), (w_hi, (4, 13)), (w_mid, (2, 3)), (w_mid, (13, 19)), (w_low, (3, 4)), (w_low, (19, 22))):
                sp.dma_start(g.w_e1_parts[rows[0]:rows[1], :], part[rows[0]:rows[1], :]).then_inc(placed, 16)
            sp.wait_ge(tab_sb, B)
            sp.dma_start(g.src_table[:, :].rearrange("(b p) c -> p b c", p=P), table[:, :, D:3 * D]).then_inc(tab_out, 16)
            sp.wait_ge(tab_out, 16)
            sp.wait_ge(placed, 16 * 6)
            sp.wait_ge(landed, 16 * 9)

        @block.tensor
        def _(pe):
            for c, (m0, k) in enumerate(CH):
                if c >= 2:
                    pe.wait_ge(turned_sb, c - 1)
                for m in range(k):
                    mm = nc.tensor.transpose(t_ps[0:D, c % 2, m * P:(m + 1) * P], g.h[:, m0 + m, :], g.ident[:, :])
                mm.then_inc(turned, 1)
            pe.wait_ge(node_landed, 16 * 3)
            for c, (m0, k) in enumerate(CH):
                pe.wait_ge(turned_sb, c + 1)
                if c >= 2:
                    pe.wait_ge(hx_sb, c - 1)
                nc.tensor.matmul(x_ps[0:D, c % 2, 0:k * P], g.w_node[:, :], h_t[:, m0 * P:(m0 + k) * P],
                                 start=True, stop=True).then_inc(hx, 1)
            for m in range(B):
                pe.wait_ge(hx_sb, m // 4 + 1)
                since(pe, tab_sb, m - 3)
                cols = slice(m * P, (m + 1) * P)
                nc.tensor.matmul(n_ps[:, m % 4, 0:2 * D], hx_t[:, cols], w_att[:, :], start=True, stop=True)
                nc.tensor.matmul(n_ps[:, m % 4, 2 * D:3 * D], h_t[:, cols], g.w_node[:, :], start=True, stop=True).then_inc(tab, 1)

        @block.vector
        def _(dve):
            steps = [0]

            def step(ins):
                steps[0] += 1
                ins.then_inc(own, 1)
                dve.wait_ge(own, steps[0])

            nc.vector.memset(g.w_e1[:, :], 0.0).then_inc(zeroed, 1)
            nc.vector.memset(g.dst_parts[:, B, :, :], 0.0)
            nc.vector.memset(g.w_e1_parts[:, :], 0.0)
            for c, (m0, k) in enumerate(CH):
                dve.wait_ge(turned, c + 1)
                nc.vector.tensor_copy(h_t[:, m0 * P:(m0 + k) * P], t_ps[0:D, c % 2, 0:k * P]).then_inc(turned_sb, 1)
            dve.wait_ge(e1_landed, 16 * 9)
            nc.vector.tensor_copy(w_hi[:, :], g.w_e1[:, :]).then_inc(split_w, 1)
            dve.wait_ge(split_w, 1)
            step(nc.vector.tensor_tensor(w_left[:, :], g.w_e1[:, :], w_hi[:, :], ALU.subtract))
            nc.vector.tensor_copy(w_mid[:, :], w_left[:, :]).then_inc(split_w, 1)
            dve.wait_ge(split_w, 2)
            step(nc.vector.tensor_tensor(w_left[:, :], w_left[:, :], w_mid[:, :], ALU.subtract))
            nc.vector.tensor_copy(w_low[:, :], w_left[:, :]).then_inc(split_w, 1)
            for m in range(B):
                dve.wait_ge(tab, m + 1)
                nc.vector.tensor_copy(table[:, m, :], n_ps[:, m % 4, 0:3 * D]).then_inc(tab_sb, 1)
            dve.wait_ge(tab_sb, B)
            of_dst = table[:, :, 0:D]
            parts = [g.dst_parts[:, 0:B, k, :] for k in range(3)]
            step(nc.vector.tensor_copy(parts[0], of_dst))
            step(nc.vector.tensor_tensor(left[:, :, :], of_dst, parts[0], ALU.subtract))
            step(nc.vector.tensor_copy(parts[1], left[:, :, :]))
            step(nc.vector.tensor_tensor(left[:, :, :], left[:, :, :], parts[1], ALU.subtract))
            step(nc.vector.tensor_copy(parts[2], left[:, :, :]))

        @block.scalar
        def _(act):
            for c, (m0, k) in enumerate(CH):
                act.wait_ge(hx, c + 1)
                nc.scalar.copy(hx_t[:, m0 * P:(m0 + k) * P], x_ps[0:D, c % 2, 0:k * P]).then_inc(hx_sb, 1)


def edge_layer(nc, g, S, l):
    B, ND = S.blocks, S.dst_tiles
    H = 4
    K1 = S.split_used
    with ExitStack() as ctx:
        sb = lambda name, shape, dt=F32: ctx.enter_context(nc.sbuf_tensor(f"l{l}_{name}", shape, dt))
        sem = lambda name: ctx.enter_context(semaphore(nc, f"l{l}_{name}"))
        ps = lambda name, k: ctx.enter_context(nc.psum_tensor(f"l{l}_{name}", [P, k, 512], F32))
        split = sb("split", [K1, 4, H * P], BF16)
        hidden = sb("hidden", [D + 4, 4, H * P])
        index = sb("gather_index", [P, 4, H], U32)
        gathered = sb("gathered", [P, 4, H, 2 * D])
        node_hot = sb("node_hot", [P, 2, H * P], BF16)
        edge = sb("edge", [P, 2, H, 2 * D])
        scored = sb("scored", [P, 2, H, D])
        logit = sb("logit", [P, 2, H])
        att = sb("attention", [P, 2, H])
        msg = sb("message", [P, 2, H, D])
        left = sb("message_left", [P, H, D])
        parts = sb("message_parts", [P, 2, 3, H, D], BF16)
        spread_ps = ps("spread_ps", 1)
        hidden_ps = ps("hidden_ps", 1)
        edge_ps = ps("edge_ps", 2)
        sum_ps = ps("sum_ps", 2)
        landed = [sem(f"rows_landed_{r}") for r in range(4)]
        gather_done = g.gather_done[l]
        indexed = sem("gather_index_ready")
        begun = sem("gather_begun")
        spread_done = sem("spread_done")
        x_done = sem("x_done")
        hot_done = sem("node_hot_done")
        relu_done = sem("hidden_done")
        y_done = sem("y_done")
        edge_done = sem("edge_sums_done")
        weighed = sem("scores_weighed")
        scored_done = sem("scored_done")
        att_done = sem("attention_done")
        msg_done = sem("message_done")
        hi_done = sem("high_parts_done")
        parted = sem("messages_parted")
        z_done = sem("z_done")
        added = sem("sums_added")
        block = ctx.enter_context(nc.Block())
        N = ND // H
        TURNS = (N - 1) // 4

        @block.sync
        def _(sp):
            def load(n, r):
                since(sp, x_done, n - 3)
                since(sp, y_done, n - 3)
                cols = bass.ds(n * (H * P), H * P)
                sp.dma_start(split[:, r, :], g.split_rows[0:K1, cols]).then_inc(landed[r], 16)
                sp.dma_start(hidden[D:D + 4, r, :], g.attr_rows[3:7, cols]).then_inc(landed[r], 16)

            def four(i):
                for r in range(4):
                    load(i * 4 + r, r)

            rounds(sp, N // 4, four)
            for r in range(N % 4):
                load(N // 4 * 4 + r, r)

        @block.gpsimd
        def _(pool):
            def gather(n, r):
                since(pool, edge_done, n - 3)
                nc.gpsimd.tensor_copy(index[:, r, :], g.src_node[:, bass.ds(n * H, H)]).then_inc(indexed, 1)
                pool.wait_ge(indexed, n + 1)
                pool.sem_inc(begun, 1)
                for j in range(H):
                    nc.gpsimd.indirect_dma_start(
                        out=gathered[:, r, j, :], out_offset=None, in_=g.src_table[:, :],
                        in_offset=bass.IndirectOffsetOnAxis(ap=index[:, r, j:j + 1], axis=0),
                    ).then_inc(gather_done[r], 16)

            def four(i):
                for r in range(4):
                    gather(i * 4 + r, r)

            rounds(pool, N // 4, four)
            for r in range(N % 4):
                gather(N // 4 * 4 + r, r)

        @block.tensor
        def _(pe):
            def x(n, r, turn):
                pe.wait_ge(landed[r], turn * 32 + 32)
                since(pe, hot_done, n)
                nc.tensor.matmul(spread_ps[:, 0, :], g.select[:, :], split[:, r, :], start=True, stop=True).then_inc(spread_done, 1)
                since(pe, relu_done, n)
                nc.tensor.matmul(hidden_ps[0:D, 0, :], g.w_e1_parts[:, :], split[:, r, :], start=True, stop=True).then_inc(x_done, 1)

            def y(n, r):
                h = r % 2
                blk = numbers(nc, mybir.EngineType.PE, g.dst_tab[0:1, bass.ds(n * H, H)], B)
                pe.wait_ge(hot_done, n + 1)
                pe.wait_ge(relu_done, n + 1)
                since(pe, edge_done, n - 1)
                for j in range(H):
                    cols = slice(j * P, (j + 1) * P)
                    att_cols = slice(j * P, j * P + D)
                    nc.tensor.matmul(edge_ps[:, h, cols], hidden[:, r, cols], g.w_edge[:, :], start=True, stop=False, skip_group_check=True)
                    for k in range(3):
                        mm = nc.tensor.matmul(edge_ps[:, h, att_cols], node_hot[:, h, cols],
                                              g.dst_parts[:, bass.ds(blk[j], 1), k, :].rearrange("p o d -> p (o d)"),
                                              start=False, stop=(k == 2), skip_group_check=True)
                mm.then_inc(y_done, 1)

            def z(n, h):
                pe.wait_ge(parted, n * 3 + 3)
                since(pe, added, (n - 1) * H)
                for j in range(H):
                    hot = g.dst_hot[:, bass.ds(n * H + j, 1), :].rearrange("p o c -> p (o c)")
                    for k in range(3):
                        mm = nc.tensor.matmul(sum_ps[:, h, j * D:(j + 1) * D], hot, parts[:, h, k, j, :],
                                              start=(k == 0), stop=(k == 2))
                mm.then_inc(z_done, 1)

            def round_of(n, r, turn):
                if not isinstance(n, int) or n + 1 < N:
                    x(n + 1, (r + 1) % 4, turn + (r + 1) // 4)
                y(n, r)
                if not isinstance(n, int) or n >= 2:
                    z(n - 2, r % 2)

            x(0, 0, 0)
            for n in range(4):
                round_of(n, n, 0)
            with pe.Fori(1, TURNS) as i:
                for r in range(4):
                    round_of(i * 4 + r, r, i)
            for n in range(TURNS * 4, N):
                round_of(n, n % 4, n // 4)
            z(N - 2, (N - 2) % 2)
            z(N - 1, (N - 1) % 2)

        @block.scalar
        def _(act):
            def relu(n, r):
                act.wait_ge(x_done, n + 1)
                since(act, y_done, n - 3)
                nc.scalar.activation(hidden[0:D, r, :], hidden_ps[0:D, 0, :], ACT.Relu).then_inc(relu_done, 1)

            def message(n, h):
                act.wait_ge(scored_done, n + 1)
                since(act, msg_done, n - 1)
                nc.scalar.activation(att[:, h, :], logit[:, h, :], ACT.Sigmoid, bias=g.ba2[:, 0:1]).then_inc(att_done, 1)
                act.wait_ge(att_done, n + 1)
                since(act, parted, (n - 1) * 3)
                for j in range(H):
                    ins = nc.scalar.activation(msg[:, h, j, :], edge[:, h, j, D:2 * D], ACT.Copy, scale=att[:, h, j:j + 1])
                ins.then_inc(msg_done, 1)
                act.wait_ge(msg_done, n + 1)
                since(act, z_done, n - 1)
                nc.scalar.copy(parts[:, h, 0, :, :], msg[:, h, :, :]).then_inc(hi_done, 1)

            def round_of(n, r):
                if not isinstance(n, int) or n + 1 < N:
                    relu(n + 1, (r + 1) % 4)
                message(n, r % 2)

            relu(0, 0)
            for n in range(4):
                round_of(n, n)
            with act.Fori(1, TURNS) as i:
                for r in range(4):
                    round_of(i * 4 + r, r)
            for n in range(TURNS * 4, N):
                round_of(n, n % 4)

        @block.vector
        def _(dve):
            def hots(n, h):
                dve.wait_ge(spread_done, n + 1)
                since(dve, y_done, n - 1)
                nc.vector.tensor_scalar(node_hot[:, h, :], spread_ps[:, 0, :], g.iota_part[:, 0:1], None,
                                        ALU.is_equal).then_inc(hot_done, 1)

            def steps_of(n, r, turn, blk):
                h = r % 2
                o = 1 - h
                first = lambda m: isinstance(n, int) and n < m

                def edge_sum():
                    dve.wait_ge(y_done, n + 1)
                    dve.wait_ge(gather_done[r], turn * (16 * H) + 16 * H)
                    since(dve, msg_done, n - 1)
                    nc.vector.tensor_tensor(edge[:, h, :, :].rearrange("p j c -> p (j c)"), gathered[:, r, :, :].rearrange("p j c -> p (j c)"),
                                            edge_ps[:, h, :], ALU.add).then_inc(edge_done, 1)

                def weigh():
                    dve.wait_ge(edge_done, n + 1)
                    nc.vector.scalar_tensor_tensor(out=scored[:, h, :, :], in0=edge[:, h, :, 0:D], scalar=0.0,
                                                   in1=g.wa2[:, :].unsqueeze(1).broadcast_to([P, H, D]), op0=ALU.max, op1=ALU.mult).then_inc(weighed, 1)

                def score():
                    dve.wait_ge(weighed, n + 1)
                    nc.vector.tensor_reduce(logit[:, h, :], scored[:, h, :, :], AX.X, ALU.add).then_inc(scored_done, 1)

                def part(k):
                    since(dve, parted, (n - 1) * 3 + k)
                    if k == 0:
                        dve.wait_ge(hi_done, n)
                        nc.vector.tensor_tensor(left[:, :, :], msg[:, o, :, :], parts[:, o, 0, :, :], ALU.subtract).then_inc(parted, 1)
                    elif k == 1:
                        nc.vector.tensor_copy(parts[:, o, 1, :, :], left[:, :, :]).then_inc(parted, 1)
                    else:
                        nc.vector.tensor_tensor(parts[:, o, 2, :, :], left[:, :, :], parts[:, o, 1, :, :], ALU.subtract).then_inc(parted, 1)

                def add(j):
                    dve.wait_ge(z_done, n - 1)
                    since(dve, added, (n - 2) * H + j)
                    to = node(g.sums, blk[j])
                    nc.vector.tensor_tensor(to, to, sum_ps[:, h, j * D:(j + 1) * D], ALU.add).then_inc(added, 1)

                scores = [edge_sum, weigh, score] if not isinstance(n, int) or n < N else []
                in_parts = [] if first(1) or (isinstance(n, int) and n > N) else [lambda k=k: part(k) for k in range(3)]
                sums = [] if first(2) else [lambda j=j: add(j) for j in range(H)]
                chains = [scores, in_parts, sums]
                for k in range(H):
                    for chain in chains:
                        if k < len(chain):
                            chain[k]()

            def round_of(n, r, turn):
                if not isinstance(n, int) or n + 1 < N:
                    hots(n + 1, (r + 1) % 2)
                blk = None
                if not isinstance(n, int) or n >= 2:
                    blk = numbers(nc, mybir.EngineType.DVE, g.dst_tab[0:1, bass.ds(n * H - 2 * H, H)], B)
                steps_of(n, r, turn, blk)

            hots(0, 0)
            for n in range(4):
                round_of(n, n, 0)
            with dve.Fori(1, TURNS) as i:
                for r in range(4):
                    round_of(i * 4 + r, r, i)
            for n in range(TURNS * 4, N + 2):
                round_of(n, n % 4, n // 4)


def attention_layers(nc, g, S):
    B = S.blocks
    every = lambda row: row[:, :].unsqueeze(1).broadcast_to([P, B, D])
    with ExitStack() as ctx:
        sb = lambda name, shape, dt=F32: ctx.enter_context(nc.sbuf_tensor(name, shape, dt))
        g.dst_hot = sb("dst_hots", [P, S.dst_tiles, P], BF16)
        g.src_node = sb("src_node", [P, S.dst_tiles], U32)
        split_slots(nc, g, S)
        g.gather_done = [[nc.alloc_semaphore(name=f"l{l}_gathered_{r}") for r in range(4)] for l in range(S.layers)]
        g.h = sb("h", [P, B, D])
        g.dst_parts = sb("dst_parts", [P, B + 1, 3, D], BF16)
        g.sums = sb("sums", [P, B + 1, D])
        normed = sb("normed", [P, B, D])
        g.w_node = sb("w_node", [D, D])
        g.w_edge = sb("w_edge", [D + 4, 2 * D])
        g.w_e1 = sb("w_e1", [S.split_used, D])
        g.w_e1_parts = sb("w_e1_parts", [S.split_used, D], BF16)
        g.wa2, g.bias, g.ln_g, g.ln_b = (sb(n, [P, D]) for n in ("wa2", "bias", "ln_g", "ln_b"))
        g.ba2 = sb("ba2", [P, 1])
        g.select = sb("select", [S.split_used, P], BF16)
        with nc.Block() as block:
            @block.vector
            def _(dve):
                nc.vector.tensor_copy(g.h[:, :, :], g.x[:, :, :])
                nc.vector.tensor_copy(g.select[:, :], g.ident[0:S.split_used, 0:1].broadcast_to([S.split_used, P]))
        for l in range(S.layers):
            node_tables(nc, g, S, l)
            edge_layer(nc, g, S, l)

            def add_bias(step):
                step(nc.vector.tensor_tensor(g.sums[:, 0:B, :], g.sums[:, 0:B, :], every(g.bias), ALU.add))

            def affine(step):
                step(nc.vector.tensor_tensor(normed[:, :, :], normed[:, :, :], every(g.ln_g), ALU.mult))
                step(nc.vector.tensor_tensor(normed[:, :, :], normed[:, :, :], every(g.ln_b), ALU.add))
                if l < S.layers - 1:
                    step(nc.vector.scalar_tensor_tensor(out=g.h[:, :, :], in0=normed[:, :, :], scalar=0.0, in1=g.h[:, :, :],
                                                        op0=ALU.max, op1=ALU.add))
                else:
                    step(nc.vector.tensor_tensor(g.h[:, :, :], g.h[:, :, :], normed[:, :, :], ALU.add))

            layer_norm(nc, g, S, f"l{l}_norm", g.sums[:, 0:B, :], normed, add_bias, affine)

        def add_x(step):
            step(nc.vector.tensor_tensor(g.h[:, :, :], g.h[:, :, :], g.x[:, :, :], ALU.add))

        layer_norm(nc, g, S, "norm2", g.h, g.x, add_x)


def last_layer(nc, g, S):
    B = S.blocks
    K = 3
    with ExitStack() as ctx:
        sb = lambda name, shape, dt=F32: ctx.enter_context(nc.sbuf_tensor(name, shape, dt))
        w_inv2 = sb("w_inv_squared", [P, B])
        scaled = [sb("scaled_even", [P, B, D]), sb("scaled_odd", [P, B, D])]
        pairs = [sb("hops_0_1", [P, B, 2 * D]), sb("hops_2_3", [P, B, 2 * D])]
        hop = [pairs[k // 2][:, :, k % 2 * D:(k % 2 + 1) * D] for k in range(4)]
        with nc.Block() as block:
            @block.vector
            def _(dve):
                nc.vector.tensor_copy(hop[0], g.x[:, :, :])
                nc.vector.tensor_tensor(w_inv2[:, :], g.w_inv[:, :], g.w_inv[:, :], ALU.mult)
                nc.vector.tensor_tensor(scaled[0][:, :, :], g.x[:, :, :], spread(g.w_inv[:, :], D), ALU.mult)

        def finish(p, m, product):
            nc.vector.tensor_scalar(node(hop[p + 1], m), product, node_scale(g.w_inv, m), None, ALU.mult)
            return nc.vector.tensor_scalar(node(scaled[1 - p % 2], m), product, node_scale(w_inv2, m), None, ALU.mult)

        sweeps(nc, g, S, "normed", g.weights, 1, [(scaled[p % 2], scaled[1 - p % 2]) for p in range(K)], finish)
        with ExitStack() as ctx2:
            sem = lambda name: ctx2.enter_context(semaphore(nc, name))
            theta = ctx2.enter_context(nc.sbuf_tensor("theta", [P, 2, 2, D], F32))
            hop_t = ctx2.enter_context(nc.sbuf_tensor("hop_turned", [P, 4, 2 * P], F32))
            z = scaled[0]
            t_ps = ctx2.enter_context(nc.psum_tensor("hop_turn_ps", [P, 4, 512], F32))
            o_ps = ctx2.enter_context(nc.psum_tensor("theta_ps", [P, 4, 512], F32))
            zeroed, landed, summed, turned, copied, done, read = (sem(n) for n in (
                "thetas_zeroed", "thetas_landed", "thetas_of_hop_summed", "hops_turned", "hops_copied", "products_summed",
                "products_read"))
            block = ctx2.enter_context(nc.Block())

            @block.sync
            def _(sp):
                sp.wait_ge(zeroed, 1)
                for hop_of, which, src in ((0, 0, g.theta_f[0]), (1, 0, g.theta_b[0]), (1, 1, g.theta_b[1]), (2, 0, g.theta_f[1]),
                                           (2, 1, g.theta_b[2]), (3, 0, g.theta_f[2])):
                    rows = slice(hop_of % 2 * D, (hop_of % 2 + 1) * D)
                    sp.dma_start(theta[rows, which, hop_of // 2, :], src).then_inc(landed, 16)

            @block.tensor
            def _(pe):
                def turn(m):
                    since(pe, copied, m - 3)
                    for k in range(2):
                        mm = nc.tensor.transpose(t_ps[:, m % 4, k * P:(k + 1) * P], pairs[k][:, m, :], g.ident[:, :])
                    mm.then_inc(turned, 1)

                turn(0)
                turn(1)
                pe.wait_ge(summed, 1)
                for m in range(B):
                    if m + 2 < B:
                        turn(m + 2)
                    pe.wait_ge(copied, m + 1)
                    since(pe, read, m - 3)
                    for k in range(2):
                        mm = nc.tensor.matmul(o_ps[:, m % 4, 0:D], hop_t[:, m % 4, k * P:(k + 1) * P], theta[:, 0, k, :],
                                              start=(k == 0), stop=(k == 1))
                    mm.then_inc(done, 1)

            @block.scalar
            def _(act):
                for m in range(B):
                    act.wait_ge(turned, m + 1)
                    since(act, done, m - 3)
                    nc.scalar.copy(hop_t[:, m % 4, :], t_ps[:, m % 4, 0:2 * P]).then_inc(copied, 1)

            @block.vector
            def _(dve):
                nc.vector.memset(theta[:, :, :, :], 0.0).then_inc(zeroed, 1)
                dve.wait_ge(landed, 6 * 16)
                nc.vector.tensor_tensor(theta[:, 0, :, :], theta[:, 0, :, :], theta[:, 1, :, :], ALU.add).then_inc(summed, 1)
                for m in range(B):
                    dve.wait_ge(done, m + 1)
                    nc.vector.tensor_tensor(z[:, m, :], o_ps[:, m % 4, 0:D], g.x[:, m, :], ALU.add).then_inc(read, 1)

        layer_norm(nc, g, S, "norm3", scaled[0], g.x)


def store_features(nc, g, S):
    full = (S.blocks - 1) * P
    with semaphore(nc, "out_stored") as stored, nc.Block() as block:
        @block.sync
        def _(sp):
            sp.dma_start(g.out[0:full, :].rearrange("(b p) d -> p b d", p=P), g.x[:, 0:S.blocks - 1, :]).then_inc(stored, 16)
            sp.dma_start(g.out[full:S.n, :], g.x[0:S.last_rows, S.blocks - 1, :]).then_inc(stored, 16)
            sp.wait_ge(stored, 32)


class Arrays:
    pass


def graph_network(nc, x, src, dst, edge_attr_3, edge_weight, L1_gnn_eps, L2_gnn_W_node, L2_gnn_W_e1, L2_gnn_b_e1,
                  L2_gnn_W_e2, L2_gnn_b_e2, L2_gnn_Wa1, L2_gnn_ba1, L2_gnn_Wa2, L2_gnn_ba2, L2_gnn_bias, L2_gnn_ln_g,
                  L2_gnn_ln_b, L3_gnn_theta_forward, L3_gnn_theta_backward, out):
    g = Arrays()
    g.x_in, g.eps1_in, g.out = x, L1_gnn_eps, out
    g.src, g.dst, g.w = src, dst, edge_weight
    g.ea = edge_attr_3.rearrange("e k -> (e k)")
    g.W_node, g.W_e1, g.b_e1, g.W_e2, g.b_e2 = L2_gnn_W_node, L2_gnn_W_e1, L2_gnn_b_e1, L2_gnn_W_e2, L2_gnn_b_e2
    g.Wa1, g.ba1, g.Wa2, g.ba2_in = L2_gnn_Wa1, L2_gnn_ba1, L2_gnn_Wa2, L2_gnn_ba2
    g.bias_in, g.ln_g_in, g.ln_b_in = L2_gnn_bias, L2_gnn_ln_g, L2_gnn_ln_b
    g.theta_f, g.theta_b = L3_gnn_theta_forward, L3_gnn_theta_backward
    S = Shapes(x.shape[0], src.shape[0])
    B, T, NT = S.blocks, S.in_tiles, S.tiles
    dram = lambda name, shape, dt=F32: nc.dram_tensor(name, shape, dt).ap()
    g.key_rows = dram("key_rows", [T, P])
    g.blk_rows = dram("blk_rows", [T, P])
    g.slots = dram("slots", [P * NT, S.rec])
    g.first_tiles = dram("first_tiles", [B * B + 1])
    blocks = dram("blocks", [B * B + 1 + S.body, P, 2, P])
    g.blocks = blocks.rearrange("q p k c -> (q p) (k c)")
    g.counts = blocks[0:B * B, :, 0, :].rearrange("(b a) p c -> b p a c", a=B)
    g.weights = blocks[0:B * B, :, 1, :].rearrange("(b a) p c -> a p b c", a=B)
    g.dst_slots = dram("dst_slots", [P * S.dst_tiles, S.rec])
    g.dst_firsts = dram("dst_firsts", [B + 1])
    g.attr_rows = dram("attr_rows", [S.rec, S.dst_tiles * P])
    g.split_rows = dram("split_rows", [S.split, S.dst_tiles * P], BF16)
    g.src_table = dram("src_table", [B * P, 2 * D])
    g.bucket_of = dram("bucket_of", [-(-(NT + 2) // P) * P])
    with ExitStack() as ctx:
        sb = lambda name, shape, dt=F32: ctx.enter_context(nc.sbuf_tensor(name, shape, dt))
        g.ident = sb("ident", [P, P])
        g.iota_free = sb("iota_free", [P, P])
        g.iota_part = sb("iota_part", [P, 1])
        g.earlier = sb("earlier", [P, P])
        g.before = sb("before", [P, P])
        g.off_diagonal = sb("off_diagonal", [P, P])
        g.dst_tab = sb("dst_tab", [1, S.dst_tiles], I32)
        g.deg = sb("degrees", [P, B, 3])
        constants(nc, g, S)
        with ExitStack() as ctx1:
            sb1 = lambda name, shape, dt=F32: ctx1.enter_context(nc.sbuf_tensor(name, shape, dt))
            g.rec = sb1("rec", [P, T, S.rec])
            g.src_blk = sb1("src_blk", [P, T])
            g.dst_blk = sb1("dst_blk", [P, T])
            g.key_col = sb1("key_col", [P, T])
            g.dst_index = sb1("dst_index", [P, T], U32)
            edges_in(nc, g, S)
            with ExitStack() as ctx2:
                g.src_hot = ctx2.enter_context(nc.sbuf_tensor("src_hot", [P, T, B], BF16))
                g.start = ctx2.enter_context(nc.sbuf_tensor("start", [B, T + 1, B], F32))
                g.shift = ctx2.enter_context(nc.sbuf_tensor("shift", [B, B], F32))
                count_buckets(nc, g, S)
                slot_edges(nc, g, S)
            g.same = sb1("same_bucket", [P, NT + 1])
            g.tab = sb1("tab", [1, NT], I32)
            g.tile_blk = sb1("tile_blk", [P, 2, -(-(NT + 2) // P)])
            g.sums = sb1("tile_sums", [P, 3, NT])
            tile_tables(nc, g, S)
            g.recs = sb1("recs", [P, NT, S.rec])
            load_slots(nc, g, S)
            build_matrices(nc, g, S)
            degrees(nc, g, S)
        g.x = sb("x", [P, B, D])
        g.w_inv = sb("w_inv", [P, B])
        load_features(nc, g, S)
        first_layers(nc, g, S)
        attention_layers(nc, g, S)
        last_layer(nc, g, S)
        store_features(nc, g, S)


_INS = ["x", "src", "dst", "edge_attr_3", "edge_weight", "L1_gnn_eps", "L2_gnn_W_node", "L2_gnn_W_e1", "L2_gnn_b_e1",
        "L2_gnn_W_e2", "L2_gnn_b_e2", "L2_gnn_Wa1", "L2_gnn_ba1", "L2_gnn_Wa2", "L2_gnn_ba2", "L2_gnn_bias", "L2_gnn_ln_g",
        "L2_gnn_ln_b", "L3_gnn_theta_forward", "L3_gnn_theta_backward"]


def kernel(**inputs):
    import numpy as _np
    import concourse.bacc as _bacc
    from concourse.bass_utils import run_bass_kernel_spmd as _run

    nc = _bacc.Bacc("TRN2", target_bir_lowering=False, num_devices=1)
    arrays, args = {}, []
    for name in _INS:
        a = _np.ascontiguousarray(inputs[name])
        arrays[f"in_{name}_dram"] = a
        args.append(nc.dram_tensor(f"in_{name}_dram", a.shape, mybir.dt.from_np(a.dtype), kind="ExternalInput").ap())
    shape = inputs["x"].shape
    args.append(nc.dram_tensor("out_0_dram", shape, F32, kind="ExternalOutput").ap())
    graph_network(nc, *args)
    r = _run(nc, [arrays], core_ids=[0])
    return r.results[0]["out_0_dram"]
```
